# Optimizing a Trainium2 kernel written in Bass

```python
import numpy as np
import jax
import jax.numpy as jnp

def _softmax(x, axis=-1):
    return jax.nn.softmax(x, axis=axis)

def _gelu(x):
    return jax.nn.gelu(x, approximate=True)

def _silu(x):
    return jax.nn.silu(x)

def _sigmoid(x):
    return jax.nn.sigmoid(x)

def _layernorm(x, axis=-1, eps=1e-05):
    m = jnp.mean(x, axis=axis, keepdims=True)
    v = jnp.var(x, axis=axis, keepdims=True)
    return (x - m) / jnp.sqrt(v + eps)

def _scatter_add(tgt, idx, src, axis=0):
    return tgt.at[idx].add(src)

def _segment_sum(src, seg, n):
    return jax.ops.segment_sum(src, seg, n)
kernel_name = 'mk_adaln_d2_jaxref_r8_e4075d'

def setup_inputs(seed: int=0):
    np.random.seed(seed)
    _w = jnp.asarray

    def _L0_attn_setup():
        import jax, jax.numpy as jnp
        import numpy as np
        EMB_DIM = 512
        N_HEADS = 32
        QKV_DIM = EMB_DIM // N_HEADS
        B, S = (4, 512)
        key = jax.random.key(seed)
        ks = jax.random.split(key, 7)
        std = 1.0 / np.sqrt(EMB_DIM)
        x = jax.random.normal(ks[0], (B, S, EMB_DIM), dtype=jnp.float32)
        Wq = jax.random.normal(ks[1], (EMB_DIM, QKV_DIM, N_HEADS), dtype=jnp.float32) * std
        bq = jnp.zeros((QKV_DIM, N_HEADS), dtype=jnp.float32)
        Wk = jax.random.normal(ks[2], (EMB_DIM, QKV_DIM, 1), dtype=jnp.float32) * std
        bk = jnp.zeros((QKV_DIM, 1), dtype=jnp.float32)
        Wv = jax.random.normal(ks[3], (EMB_DIM, QKV_DIM, 1), dtype=jnp.float32) * std
        bv = jnp.zeros((QKV_DIM, 1), dtype=jnp.float32)
        return {'x': x, 'Wq': Wq, 'bq': bq, 'Wk': Wk, 'bk': bk, 'Wv': Wv, 'bv': bv}
    _L0_attn_in = _L0_attn_setup()

    def _L0_ffn_setup():
        import jax, jax.numpy as jnp
        import numpy as np
        IN_F = 512
        OUT_F = 512
        N_CLUSTERS = 64
        THRESHOLD = 0.01
        TEMPERATURE = 0.1
        BATCH, SEQ = (4, 256)
        key = jax.random.key(seed)
        k1, k2, k3, k4, k5 = jax.random.split(key, 5)
        s = 1.0 / np.sqrt(IN_F)
        return {'input': jax.random.normal(k1, (BATCH, SEQ, IN_F), dtype=jnp.float32), 'weight': jax.random.normal(k2, (OUT_F, IN_F), dtype=jnp.float32) * s, 'bias': jax.random.uniform(k3, (OUT_F,), dtype=jnp.float32, minval=-s, maxval=s), 'centroids': jax.random.normal(k4, (N_CLUSTERS, IN_F), dtype=jnp.float32) * s, 'assignments': jax.random.randint(k5, (OUT_F,), 0, N_CLUSTERS, dtype=jnp.int32)}
    _L0_ffn_in = _L0_ffn_setup()
    _L0_c = _w((lambda *s: np.random.randn(*s).astype(np.float32) * 0.05)(4, 512))
    _L0_wmod = _w((lambda *s: np.random.randn(*s).astype(np.float32) * 0.05)(512, 6 * 512) * 512 ** (-0.5))

    def _L1_attn_setup():
        import jax, jax.numpy as jnp
        import numpy as np
        NUM_HEADS = 32
        NUM_KV_HEADS = 8
        HEAD_DIM = 128
        key = jax.random.key(seed)
        ks = jax.random.split(key, 5)
        B, S, H = (2, 256, 512)
        Dq = NUM_HEADS * HEAD_DIM
        Dkv = NUM_KV_HEADS * HEAD_DIM
        return {'hidden_states': jax.random.normal(ks[0], (B, S, H), jnp.float32), 'w_q': jax.random.normal(ks[1], (H, Dq), jnp.float32) * 0.02, 'w_k': jax.random.normal(ks[2], (H, Dkv), jnp.float32) * 0.02, 'w_v': jax.random.normal(ks[3], (H, Dkv), jnp.float32) * 0.02, 'w_o': jax.random.normal(ks[4], (Dq, H), jnp.float32) * 0.02}
    _L1_attn_in = _L1_attn_setup()

    def _L1_ffn_setup():
        import jax, jax.numpy as jnp
        import numpy as np

        def _dequant_linear(x, wq, scale):
            w = wq.astype(jnp.float32) * scale[:, None]
            return jnp.einsum('bsh,oh->bso', x, w)
        key = jax.random.key(seed)
        ks = jax.random.split(key, 7)
        B, S, H, I = (2, 256, 512, 1792)
        x = jax.random.normal(ks[0], (B, S, H), dtype=jnp.float32)
        gate_wq = jax.random.randint(ks[1], (I, H), -128, 128, dtype=jnp.int32)
        up_wq = jax.random.randint(ks[2], (I, H), -128, 128, dtype=jnp.int32)
        down_wq = jax.random.randint(ks[3], (H, I), -128, 128, dtype=jnp.int32)
        gate_scale = jax.random.uniform(ks[4], (I,), dtype=jnp.float32, minval=0.5, maxval=1.5) / (127.0 * np.sqrt(H))
        up_scale = jax.random.uniform(ks[5], (I,), dtype=jnp.float32, minval=0.5, maxval=1.5) / (127.0 * np.sqrt(H))
        down_scale = jax.random.uniform(ks[6], (H,), dtype=jnp.float32, minval=0.5, maxval=1.5) / (127.0 * np.sqrt(I))
        return {'x': x, 'gate_wq': gate_wq, 'gate_scale': gate_scale, 'up_wq': up_wq, 'up_scale': up_scale, 'down_wq': down_wq, 'down_scale': down_scale}
    _L1_ffn_in = _L1_ffn_setup()
    _L1_c = _w((lambda *s: np.random.randn(*s).astype(np.float32) * 0.05)(4, 512))
    _L1_wmod = _w((lambda *s: np.random.randn(*s).astype(np.float32) * 0.05)(512, 6 * 512) * 512 ** (-0.5))
    _d = {'L0_attn_x': _L0_attn_in['x'], 'L0_attn_Wq': _L0_attn_in['Wq'], 'L0_attn_bq': _L0_attn_in['bq'], 'L0_attn_Wk': _L0_attn_in['Wk'], 'L0_attn_bk': _L0_attn_in['bk'], 'L0_attn_Wv': _L0_attn_in['Wv'], 'L0_attn_bv': _L0_attn_in['bv'], 'L0_ffn_weight': _L0_ffn_in['weight'], 'L0_ffn_bias': _L0_ffn_in['bias'], 'L0_ffn_centroids': _L0_ffn_in['centroids'], 'L0_ffn_assignments': _L0_ffn_in['assignments'], 'L0_c': _L0_c, 'L0_wmod': _L0_wmod, 'L1_attn_w_q': _L1_attn_in['w_q'], 'L1_attn_w_k': _L1_attn_in['w_k'], 'L1_attn_w_v': _L1_attn_in['w_v'], 'L1_attn_w_o': _L1_attn_in['w_o'], 'L1_ffn_gate_wq': _L1_ffn_in['gate_wq'], 'L1_ffn_gate_scale': _L1_ffn_in['gate_scale'], 'L1_ffn_up_wq': _L1_ffn_in['up_wq'], 'L1_ffn_up_scale': _L1_ffn_in['up_scale'], 'L1_ffn_down_wq': _L1_ffn_in['down_wq'], 'L1_ffn_down_scale': _L1_ffn_in['down_scale'], 'L1_c': _L1_c, 'L1_wmod': _L1_wmod}
    _x0 = _d['L0_attn_x']
    _d['L0_attn_x'] = jax.random.normal(jax.random.fold_in(jax.random.key(seed), 1), (4, 512, 512), dtype=_x0.dtype)
    del _x0
    return _d

def reference(L0_attn_x, L0_attn_Wq, L0_attn_bq, L0_attn_Wk, L0_attn_bk, L0_attn_Wv, L0_attn_bv, L0_ffn_weight, L0_ffn_bias, L0_ffn_centroids, L0_ffn_assignments, L0_c, L0_wmod, L1_attn_w_q, L1_attn_w_k, L1_attn_w_v, L1_attn_w_o, L1_ffn_gate_wq, L1_ffn_gate_scale, L1_ffn_up_wq, L1_ffn_up_scale, L1_ffn_down_wq, L1_ffn_down_scale, L1_c, L1_wmod):

    def _L0_attn_ref(x, Wq, bq, Wk, bk, Wv, bv):
        import jax, jax.numpy as jnp
        import numpy as np
        EMB_DIM = 512
        N_HEADS = 32
        QKV_DIM = EMB_DIM // N_HEADS
        B, S = (4, 512)
        q = jnp.einsum('bsD,Ddh->bsdh', x, Wq) + bq
        k = (jnp.einsum('bsD,Ddh->bsdh', x, Wk) + bk)[..., 0]
        v = (jnp.einsum('bsD,Ddh->bsdh', x, Wv) + bv)[..., 0]
        qkv_dim = q.shape[-2]
        n_heads = q.shape[-1]
        scale = 1.0 / jnp.sqrt(jnp.asarray(qkv_dim, dtype=q.dtype))
        scores = jnp.einsum('bsdh,bse->bsde', q, k) * scale
        p = jax.nn.softmax(scores, axis=-1)
        o = jnp.einsum('bsde,bse->bsd', p, v)
        out = jnp.broadcast_to(o[..., None], o.shape + (n_heads,))
        return out.reshape(x.shape[:-1] + (qkv_dim * n_heads,))

    def _L0_ffn_ref(input, weight, bias, centroids, assignments):
        import jax, jax.numpy as jnp
        import numpy as np
        IN_F = 512
        OUT_F = 512
        N_CLUSTERS = 64
        THRESHOLD = 0.01
        TEMPERATURE = 0.1
        BATCH, SEQ = (4, 256)
        shape = input.shape
        x = input.reshape(-1, shape[-1])
        dots = jax.nn.softmax(x @ centroids.T / TEMPERATURE, axis=-1)
        hits = dots > THRESHOLD
        query_sel = jnp.any(hits, axis=1)
        cluster_sel = jnp.any(hits, axis=0)
        row_sel = cluster_sel[assignments]
        dense = x @ weight.T + bias
        out = jnp.where(query_sel[:, None] & row_sel[None, :], dense, jnp.zeros((), dense.dtype))
        return out.reshape(*shape[:-1], -1)

    def _L1_attn_ref(hidden_states, w_q, w_k, w_v, w_o):
        import jax, jax.numpy as jnp
        import numpy as np
        NUM_HEADS = 32
        NUM_KV_HEADS = 8
        HEAD_DIM = 128
        B, S, _ = hidden_states.shape
        Hq, Hkv, D = (NUM_HEADS, NUM_KV_HEADS, HEAD_DIM)
        g = Hq // Hkv
        scale = D ** (-0.5)
        q = (hidden_states @ w_q).reshape(B, S, Hkv, g, D)
        k = (hidden_states @ w_k).reshape(B, S, Hkv, D)
        v = (hidden_states @ w_v).reshape(B, S, Hkv, D)
        scores = jnp.einsum('bqhgd,bkhd->bhgqk', q, k) * scale
        causal = jnp.tril(jnp.ones((S, S), dtype=bool))
        scores = jnp.where(causal, scores, -jnp.inf)
        probs = jax.nn.softmax(scores.astype(jnp.float32), axis=-1).astype(q.dtype)
        attn = jnp.einsum('bhgqk,bkhd->bqhgd', probs, v)
        attn = attn.reshape(B, S, Hq * D)
        return attn @ w_o

    def _L1_ffn_ref(x, gate_wq, gate_scale, up_wq, up_scale, down_wq, down_scale):
        import jax, jax.numpy as jnp
        import numpy as np

        def _dequant_linear(x, wq, scale):
            w = wq.astype(jnp.float32) * scale[:, None]
            return jnp.einsum('bsh,oh->bso', x, w)
        gate = _dequant_linear(x, gate_wq, gate_scale)
        up = _dequant_linear(x, up_wq, up_scale)
        h = jax.nn.silu(gate) * up
        return _dequant_linear(h, down_wq, down_scale)
    x = L0_attn_x
    mod = (_silu(L0_c) @ L0_wmod).reshape(L0_c.shape[0], 6, 1, -1)
    sa, ca, ga, sb, cb, gb = (mod[:, 0], mod[:, 1], mod[:, 2], mod[:, 3], mod[:, 4], mod[:, 5])
    ga = (2 * (ga >= 0) - 1) * jnp.maximum(jnp.abs(ga), 0.25)
    gb = (2 * (gb >= 0) - 1) * jnp.maximum(jnp.abs(gb), 0.25)
    h = _layernorm(x, axis=-1) * (1 + ca) + sa
    x = x + ga * _L0_attn_ref(h, L0_attn_Wq, L0_attn_bq, L0_attn_Wk, L0_attn_bk, L0_attn_Wv, L0_attn_bv)
    h = _layernorm(x, axis=-1) * (1 + cb) + sb
    x = x + gb * _L0_ffn_ref(h, L0_ffn_weight, L0_ffn_bias, L0_ffn_centroids, L0_ffn_assignments)
    mod = (_silu(L1_c) @ L1_wmod).reshape(L1_c.shape[0], 6, 1, -1)
    sa, ca, ga, sb, cb, gb = (mod[:, 0], mod[:, 1], mod[:, 2], mod[:, 3], mod[:, 4], mod[:, 5])
    ga = (2 * (ga >= 0) - 1) * jnp.maximum(jnp.abs(ga), 0.25)
    gb = (2 * (gb >= 0) - 1) * jnp.maximum(jnp.abs(gb), 0.25)
    h = _layernorm(x, axis=-1) * (1 + ca) + sa
    x = x + ga * _L1_attn_ref(h, L1_attn_w_q, L1_attn_w_k, L1_attn_w_v, L1_attn_w_o)
    h = _layernorm(x, axis=-1) * (1 + cb) + sb
    x = x + gb * _L1_ffn_ref(h, L1_ffn_gate_wq, L1_ffn_gate_scale, L1_ffn_up_wq, L1_ffn_up_scale, L1_ffn_down_wq, L1_ffn_down_scale)
    return x

_drawn_inputs = setup_inputs


def setup_inputs(seed=0):
    import zlib

    import numpy as np

    out = dict(_drawn_inputs(seed))
    spreads = {'L0_attn_bq': (0.0, 0.8), 'L0_attn_bk': (0.0, 0.579), 'L0_attn_bv': (0.0, 0.44)}
    factors = {'L0_ffn_bias': 8.0,
     'L1_attn_w_q': 8.0,
     'L1_attn_w_k': 8.0,
     'L1_attn_w_v': 3.525,
     'L1_attn_w_o': 3.553,
     'L1_ffn_gate_scale': 6.003,
     'L1_ffn_up_scale': 6.767,
     'L1_ffn_down_scale': 6.841}
    for name, (base, spread) in spreads.items():
        noise = np.random.default_rng([zlib.crc32(name.encode()), seed]).standard_normal(out[name].shape)
        drawn = base * np.exp(spread * noise) if base else spread * noise
        out[name] = jnp.asarray(drawn.astype(out[name].dtype))
    for name, factor in factors.items():
        out[name] = (out[name] * factor).astype(out[name].dtype)
    return out
```

```python
from contextlib import ExitStack

import concourse.bass as bass
from concourse import mybir

ALU = mybir.AluOpType
ACT = mybir.ActivationFunctionType
AX = mybir.AxisListType
F32 = mybir.dt.float32
F32R = mybir.dt.float32r
BF16 = mybir.dt.bfloat16
I32 = mybir.dt.int32

P = 128
EPS = 1e-5
NEG = -1e30
GATE_MIN = 0.25
THRESHOLD = 0.01
TEMPERATURE = 0.1
MOD_SA, MOD_CA, MOD_GA, MOD_SB, MOD_CB, MOD_GB = range(6)


def adaln_two_blocks(nc, x, Wq, bq, Wk, bk, Wv, bv, ffn_w, ffn_b, cent, assign, c0, wmod0,
                     w_q, w_k, w_v, w_o, gate_wq, gate_s, up_wq, up_s, down_wq, down_s, c1, wmod1, out):
    B, S, D = x.shape
    DC = D // P
    TB = S // P
    NT = B * TB
    NM = 6 * D // P
    E0, H0 = Wq.shape[1], Wq.shape[2]
    NCL = cent.shape[0]
    HD = P
    NQ = w_q.shape[1] // HD
    NKV = w_k.shape[1] // HD
    GQ = NQ // NKV
    F = gate_wq.shape[0]
    FC = F // P
    QSCALE = float(HD) ** -0.5
    PAIR = 2
    assert D == 512 and S == 512 and E0 * H0 == D and GQ * HD == D and F % P == 0

    x_t = x.rearrange("b (t p) d -> b p t d", p=P)
    out_t = out.rearrange("b (t p) d -> b p t d", p=P)
    mid = nc.dram_tensor("x_mid", [B, S, D], F32, kind="Internal").ap()
    mid_t = mid.rearrange("b (t p) d -> b p t d", p=P)

    ctx = ExitStack()
    with ctx:
        names = [0]

        def sb(stack, name, shape, dt):
            names[0] += 1
            return stack.enter_context(nc.sbuf_tensor(f"{name}_{names[0]}", shape, dt))

        held = {}

        def sem(stack, name):
            names[0] += 1
            s_ = stack.enter_context(nc.semaphore(f"{name}_{names[0]}"))
            held.setdefault(id(stack), []).append(s_)
            return s_

        def clear(stack):
            sems = held.pop(id(stack))
            with nc.Block() as block:
                @block.sync
                def _(sp):
                    for s_ in sems:
                        sp.sem_clear(s_)

        ps = ctx.enter_context(nc.psum_tensor("ps", [P, 8, 512], F32))
        ident = sb(ctx, "ident", [P, P], F32)
        ident_b = sb(ctx, "ident_b", [P, P], BF16)
        mask = sb(ctx, "mask", [P, TB * P], F32)
        mod = [sb(ctx, f"mod{layer}", [P, NM, B], F32) for layer in range(2)]

        def gate_rows(pe, bank, layer, which, b):
            for c in range(DC):
                col = mod[layer][:, DC * which + c, b:b + 1].to_broadcast([P, P])
                last = nc.tensor.transpose(ps[:, bank, c * P:(c + 1) * P], col, ident[:])
            return last

        def mods_products(pe, bank, layer, wm, cT):
            for n in range(NM):
                for k in range(DC):
                    last = nc.tensor.matmul(ps[:, bank, n * B:(n + 1) * B], wm[:, k, n * P:(n + 1) * P],
                                            cT[:, layer, k, :], start=(k == 0), stop=(k == DC - 1))
            return last

        def mods_finish(link, layer, bank, tmp):
            m = mod[layer]
            link(nc.vector.tensor_copy(m[:], ps[:, bank, 0:NM * B].rearrange("p (n b) -> p n b", b=B)))
            for which in (MOD_CA, MOD_CB):
                v = m[:, DC * which:DC * which + DC, :]
                link(nc.vector.tensor_scalar(v, v, 1.0, None, ALU.add))
            for which in (MOD_GA, MOD_GB):
                v = m[:, DC * which:DC * which + DC, :]
                link(nc.vector.tensor_scalar(tmp[:, 0], v, 0.0, 2.0, ALU.is_ge, ALU.mult))
                link(nc.vector.tensor_scalar(tmp[:, 0], tmp[:, 0], 1.0, None, ALU.subtract))
                link(nc.vector.scalar_tensor_tensor(tmp[:, 1], v, -1.0, v, ALU.mult, ALU.max))
                link(nc.vector.scalar_tensor_tensor(v, tmp[:, 1], GATE_MIN, tmp[:, 0], ALU.max, ALU.mult))

        def tile_stats(link, xt, stats, mv):
            for t in range(TB):
                last = nc.vector.bn_stats(stats[:, t, :], xt[:, t, :])
            link(last)
            for t in range(TB):
                last = nc.vector.bn_aggr(mv[:, t, :], stats[:, t, :])
            link(last)
            return nc.vector.tensor_scalar(mv[:, :, 1], mv[:, :, 1], EPS, None, ALU.add)

        def normalise(link, xt, mv, std, xh):
            link(nc.vector.reciprocal(std[:], std[:]))
            for t in range(TB):
                last = nc.vector.tensor_scalar(xh[:, t, :], xt[:, t, :], mv[:, t, 0:1], std[:, t:t + 1],
                                               ALU.subtract, ALU.mult)
            return last

        def turn_chunk(bank, xh, c):
            for t in range(TB):
                last = nc.tensor.transpose(ps[:, bank, t * P:(t + 1) * P], xh[:, t, c * P:(c + 1) * P], ident[:])
            return last

        def modulate(dst, bank, layer, scale, shift, c, b):
            return nc.scalar.activation(dst, ps[:, bank, :], ACT.Identity,
                                        bias=mod[layer][:, DC * shift + c, b:b + 1],
                                        scale=mod[layer][:, DC * scale + c, b:b + 1])

        l0 = ExitStack()
        with l0:
            X = sb(l0, "X", [P, NT, D], F32)
            ld_ffn = sem(l0, "ld_ffn")

            a = ExitStack()
            with a:
                wm0 = sb(a, "wm0", [P, DC, 6 * D], F32)
                wm1 = sb(a, "wm1", [P, DC, 6 * D], F32)
                cT = sb(a, "cT", [P, 2, DC, B], F32)
                tmp_g = sb(a, "tmp_g", [P, 2, DC, B], F32)
                ld_wm1 = sem(a, "ld_wm1")
                c_in = sb(a, "c_in", [B, 2, D], F32)
                c_act = sb(a, "c_act", [B, 2, D], F32)
                wq_in = sb(a, "wq_in", [P, DC, D], F32)
                wcat = sb(a, "wcat", [P, DC, 3 * E0], F32)
                bq_in = sb(a, "bq_in", [P, D], F32)
                bcat = sb(a, "bcat", [P, 3 * E0], F32)
                stats = sb(a, "stats", [P, TB, 6], F32)
                mv = sb(a, "mv", [P, TB, 2], F32)
                std = sb(a, "std", [P, TB], F32)
                xh = sb(a, "xh", [P, TB, D], F32)
                hT = sb(a, "hT", [P, DC, S], F32)
                qkv = sb(a, "qkv", [P, TB, 3 * E0], F32)
                sc = sb(a, "sc", [P, TB, E0 * E0], F32)
                ex = sb(a, "ex", [P, TB, E0 * E0], F32)
                red = sb(a, "red", [P, 4, TB * E0], F32)
                upd = sb(a, "upd", [P, TB, D], F32)
                ld_c, ld_w, ld_wm, ld_b = (sem(a, n) for n in ("ld_c", "ld_w", "ld_wm", "ld_b"))
                ld_x = [sem(a, f"ld_x{b}") for b in range(B)]
                consts, silu_done, ct_turned, ct_copied = (sem(a, n) for n in ("consts", "silu", "ct_turned", "ct_copied"))
                mods_ps, mods_done, chain = (sem(a, n) for n in ("mods_ps", "mods_done", "chain"))
                var_done, std_done, xh_done, turned, hT_done = (sem(a, n) for n in ("var", "std", "xh", "turned", "hT"))
                projected, logits, ex_done, upd_done, wcat_done = (sem(a, n) for n in ("projected", "logits", "ex", "upd", "wcat"))
                gates_ps, x1_done = sem(a, "gates_ps"), sem(a, "x1")
                BANK_C, BANK_MOD, BANK_T, BANK_P, BANK_G = 0, 1, 2, 6, 7

                with nc.Block() as block:
                    @block.sync
                    def _(sp):
                        for layer, c in enumerate((c0, c1)):
                            sp.dma_start(c_in[:, layer, :], c).then_inc(ld_c, 16)
                        sp.dma_start(X[:, 0:TB, :], x_t[0]).then_inc(ld_x[0], 16)
                        wm_v = wmod0.rearrange("(c p) n -> c p n", p=P)
                        for c in range(DC):
                            sp.dma_start(wm0[:, c, :], wm_v[c]).then_inc(ld_wm, 16)
                        sp.dma_start(wq_in[:], Wq.rearrange("(c p) e h -> p c (e h)", p=P)).then_inc(ld_w, 16)
                        sp.dma_start(wcat[:, :, E0:2 * E0], Wk.rearrange("(c p) e o -> p c (e o)", p=P)).then_inc(ld_w, 16)
                        sp.dma_start(wcat[:, :, 2 * E0:3 * E0], Wv.rearrange("(c p) e o -> p c (e o)", p=P)).then_inc(ld_w, 16)
                        sp.dma_start(bq_in[:], bq.rearrange("(o e) h -> o (e h)", o=1).to_broadcast([P, D])).then_inc(ld_b, 16)
                        sp.dma_start(bcat[:, E0:2 * E0], bk.rearrange("e o -> o e").to_broadcast([P, E0])).then_inc(ld_b, 16)
                        sp.dma_start(bcat[:, 2 * E0:3 * E0], bv.rearrange("e o -> o e").to_broadcast([P, E0])).then_inc(ld_b, 16)
                        for b in range(1, B):
                            sp.dma_start(X[:, b * TB:(b + 1) * TB, :], x_t[b]).then_inc(ld_x[b], 16)
                        sp.dma_start(wm1[:], wmod1.rearrange("(c p) n -> p c n", p=P)).then_inc(ld_wm1, 16)

                    @block.gpsimd
                    def _(pool):
                        nc.gpsimd.memset(ident[:], 0.0).then_inc(consts, 1)
                        nc.gpsimd.memset(mask[:], 0.0).then_inc(consts, 1)
                        pool.wait_ge(consts, 2)
                        nc.gpsimd.affine_select(out=ident[:], in_=ident[:], compare_op=ALU.not_equal, fill=1.0,
                                                base=0, pattern=[[-1, P]], channel_multiplier=1).then_inc(consts, 1)
                        nc.gpsimd.affine_select(out=mask[:, (TB - 1) * P:], in_=mask[:, (TB - 1) * P:], compare_op=ALU.is_ge, fill=NEG,
                                                base=0, pattern=[[-1, P]], channel_multiplier=1).then_inc(consts, 1)
                        pool.wait_ge(consts, 4)
                        nc.gpsimd.tensor_copy(ident_b[:], ident[:]).then_inc(consts, 1)
                        for b in range(B):
                            Xb = X[:, b * TB:(b + 1) * TB, :]
                            pool.wait_ge(upd_done, b + 1)
                            nc.gpsimd.tensor_tensor(Xb, Xb, upd[:], ALU.add).then_inc(x1_done, 1)

                    @block.scalar
                    def _(act):
                        act.wait_ge(ld_c, 32)
                        nc.scalar.activation(c_act[:], c_in[:], ACT.Silu).then_inc(silu_done, 1)

                        def root(b):
                            act.wait_ge(var_done, b + 1)
                            nc.scalar.activation(std[:], mv[:, :, 1], ACT.Sqrt).then_inc(std_done, 1)

                        def transposed(b):
                            if b == 0:
                                act.wait_ge(mods_done, 1)
                            else:
                                act.wait_ge(projected, b)
                            for c in range(DC):
                                act.wait_ge(turned, DC * b + c + 1)
                                modulate(hT[:, c, :], BANK_T + c, 0, MOD_CA, MOD_SA, c, b).then_inc(hT_done, 1)

                        root(0)
                        transposed(0)
                        for b in range(B):
                            if b + 1 < B:
                                root(b + 1)
                                transposed(b + 1)
                            act.wait_ge(logits, b + 1)
                            nc.scalar.activation(ex[:], sc[:], ACT.Exp, scale=float(E0) ** -0.5).then_inc(ex_done, 1)

                    @block.vector
                    def _(dve):
                        n_chain = [0]

                        def link(ins):
                            n_chain[0] += 1
                            ins.then_inc(chain, 1)
                            dve.wait_ge(chain, n_chain[0])

                        def statistics(b):
                            dve.wait_ge(ld_x[b], 16)
                            if b >= 1:
                                dve.wait_ge(xh_done, b)
                            tile_stats(link, X[:, b * TB:(b + 1) * TB, :], stats, mv).then_inc(var_done, 1)

                        def normal(b):
                            dve.wait_ge(std_done, b + 1)
                            if b >= 1:
                                dve.wait_ge(turned, DC * b)
                            normalise(link, X[:, b * TB:(b + 1) * TB, :], mv, std, xh).then_inc(xh_done, 1)

                        statistics(0)
                        normal(0)
                        dve.wait_ge(ct_turned, 1)
                        nc.vector.tensor_copy(cT[:], ps[:, BANK_C, 0:2 * DC * B].rearrange(
                            "p (l c b) -> p l c b", l=2, b=B)).then_inc(ct_copied, 1)
                        dve.wait_ge(ld_w, 48)
                        for c in range(DC):
                            last = nc.vector.tensor_reduce(wcat[:, c, 0:E0], wq_in[:, c, :].rearrange(
                                "p (e h) -> p e h", h=H0), AX.X, ALU.add)
                        last.then_inc(wcat_done, 1)
                        dve.wait_ge(ld_b, 48)
                        link(nc.vector.tensor_reduce(bcat[:, 0:E0], bq_in[:].rearrange("p (e h) -> p e h", h=H0),
                                                     AX.X, ALU.add))
                        dve.wait_ge(mods_ps, 1)
                        mods_finish(link, 0, BANK_MOD, tmp_g)
                        dve.sem_inc(mods_done, 1)

                        flat = lambda t: t.rearrange("p t k -> p (t k)")
                        for b in range(B):
                            if b + 1 < B:
                                statistics(b + 1)
                                normal(b + 1)
                            dve.wait_ge(projected, b + 1)
                            pv = ps[:, BANK_P, 0:TB * 3 * E0].rearrange("p (t k) -> p t k", t=TB)
                            link(nc.vector.tensor_tensor(qkv[:], pv, bcat[:].rearrange("p (o k) -> p o k", o=1)
                                                         .to_broadcast([P, TB, 3 * E0]), ALU.add))
                            s4 = sc[:].rearrange("p t (d e) -> p t d e", e=E0)
                            row = lambda k: qkv[:, :, k * E0:(k + 1) * E0].rearrange("p t (o e) -> p t o e", o=1) \
                                .to_broadcast([P, TB, E0, E0])
                            col = qkv[:, :, 0:E0].rearrange("p t (d o) -> p t d o", o=1).to_broadcast([P, TB, E0, E0])
                            link(nc.vector.tensor_tensor(s4, col, row(1), ALU.mult))
                            s3 = sc[:].rearrange("p t (d e) -> p (t d) e", e=E0)
                            e3 = ex[:].rearrange("p t (d e) -> p (t d) e", e=E0)
                            wide = lambda v: v.rearrange("p (k o) -> p k o", o=1).to_broadcast([P, TB * E0, E0])
                            link(nc.vector.tensor_reduce(red[:, 0], s3, AX.X, ALU.max))
                            nc.vector.tensor_tensor(s3, s3, wide(red[:, 0]), ALU.subtract).then_inc(logits, 1)
                            dve.wait_ge(ex_done, b + 1)
                            link(nc.vector.tensor_reduce(red[:, 1], e3, AX.X, ALU.add))
                            link(nc.vector.tensor_tensor(s4, ex[:].rearrange("p t (d e) -> p t d e", e=E0), row(2), ALU.mult))
                            link(nc.vector.tensor_reduce(red[:, 2], s3, AX.X, ALU.add))
                            link(nc.vector.reciprocal(red[:, 1], red[:, 1]))
                            link(nc.vector.tensor_tensor(red[:, 3], red[:, 2], red[:, 1], ALU.mult))
                            dve.wait_ge(gates_ps, b + 1)
                            if b >= 1:
                                dve.wait_ge(x1_done, b)
                            for t in range(TB):
                                o = red[:, 3, t * E0:(t + 1) * E0].rearrange("p (d o) -> p d o", o=1).to_broadcast([P, E0, H0])
                                last = nc.vector.tensor_tensor(upd[:, t, :].rearrange("p (d h) -> p d h", h=H0),
                                                               ps[:, BANK_G, :].rearrange("p (d h) -> p d h", h=H0), o, ALU.mult)
                            last.then_inc(upd_done, 1)
                        dve.wait_ge(mods_ps, 2)
                        mods_finish(link, 1, BANK_MOD, tmp_g)

                    @block.tensor
                    def _(pe):
                        pe.wait_ge(consts, 3)
                        pe.wait_ge(silu_done, 1)
                        for layer in range(2):
                            for c in range(DC):
                                k = (layer * DC + c) * B
                                last = nc.tensor.transpose(ps[:, BANK_C, k:k + B], c_act[:, layer, c * P:(c + 1) * P],
                                                           ident[0:B, 0:B])
                        last.then_inc(ct_turned, 1)

                        def turn(b):
                            pe.wait_ge(xh_done, b + 1)
                            for c in range(DC):
                                if b >= 1:
                                    pe.wait_ge(hT_done, DC * (b - 1) + c + 1)
                                turn_chunk(BANK_T + c, xh, c).then_inc(turned, 1)

                        turn(0)
                        pe.wait_ge(ct_copied, 1)
                        pe.wait_ge(ld_wm, 16 * DC)
                        mods_products(pe, BANK_MOD, 0, wm0, cT).then_inc(mods_ps, 1)
                        pe.wait_ge(mods_done, 1)
                        pe.wait_ge(wcat_done, 1)
                        for b in range(B):
                            pe.wait_ge(hT_done, DC * (b + 1))
                            if b >= 1:
                                pe.wait_ge(logits, b)
                            for t in range(TB):
                                for c in range(DC):
                                    last = nc.tensor.matmul(ps[:, BANK_P, t * 3 * E0:(t + 1) * 3 * E0],
                                                            hT[:, c, t * P:(t + 1) * P], wcat[:, c, :],
                                                            start=(c == 0), stop=(c == DC - 1))
                            last.then_inc(projected, 1)
                            if b >= 1:
                                pe.wait_ge(upd_done, b)
                            gate_rows(pe, BANK_G, 0, MOD_GA, b).then_inc(gates_ps, 1)
                            if b + 1 < B:
                                turn(b + 1)
                        pe.wait_ge(ld_wm1, 16)
                        mods_products(pe, BANK_MOD, 1, wm1, cT).then_inc(mods_ps, 1)

                clear(a)

            f = ExitStack()
            with f:
                w_in = sb(f, "w_in", [P, DC, D], F32)
                wT_hi = sb(f, "wT_hi", [P, DC, D], F32R)
                wT_lo = sb(f, "wT_lo", [P, DC, D], F32R)
                cen_in = sb(f, "cen_in", [NCL, D], F32)
                cenT = sb(f, "cenT", [P, DC, NCL], F32)
                bias_r = sb(f, "bias_r", [P, D], F32)
                asg = sb(f, "asg", [NCL, D], I32)
                stats = sb(f, "stats", [P, TB, 6], F32)
                mv = sb(f, "mv", [P, TB, 2], F32)
                std = sb(f, "std", [P, TB], F32)
                xh = sb(f, "xh", [P, TB, D], F32)
                hT = sb(f, "hT", [P, DC, S], F32)
                hT_hi = sb(f, "hT_hi", [P, B, DC, S], F32R)
                hT_lo = sb(f, "hT_lo", [P, B, DC, S], F32R)
                lg = sb(f, "lg", [P, TB, NCL], F32)
                pr = sb(f, "pr", [P, TB, NCL], F32)
                top = sb(f, "top", [P, TB, NCL], F32)
                red = sb(f, "red", [P, 3, TB], F32)
                qsel = sb(f, "qsel", [P, NT], F32)
                topc = sb(f, "topc", [P, NCL], F32)
                topv = sb(f, "topv", [NCL, 2], F32)
                ones = sb(f, "ones", [NCL, P], F32)
                selb = sb(f, "selb", [NCL, P], F32)
                clid = sb(f, "clid", [NCL, 1], I32)
                clidf = sb(f, "clidf", [NCL, 1], F32)
                onehot = sb(f, "onehot", [NCL, D], F32)
                rsel = sb(f, "rsel", [P, D], F32)
                gsel = sb(f, "gsel", [P, B, D], F32)
                ud = sb(f, "ud", [P, 2, 2, D], F32)
                names_ = ("chain", "var", "std", "xh", "turned", "hT", "hi", "lo", "cen_ps", "cenT", "w_ps", "w_hi",
                          "w_lo", "lgps", "lg", "ex", "iota", "top_done", "top_ps", "selb", "rsel_ps", "rsel",
                          "gate_ps", "gsel", "dense", "dense_read", "u_done", "x2", "stored")
                s = {n: sem(f, "f_" + n) for n in names_}
                BANK_L, BANK_X = 0, 1
                BANK_T, BANK_D = 2, 6

                with nc.Block() as block:
                    @block.sync
                    def _(sp):
                        sp.dma_start(cen_in[:], cent).then_inc(ld_ffn, 16)
                        sp.dma_start(w_in[:], ffn_w.rearrange("(c p) i -> p c i", p=P)).then_inc(ld_ffn, 16)
                        sp.dma_start(bias_r[:], ffn_b.rearrange("(o d) -> o d", o=1).to_broadcast([P, D])).then_inc(ld_ffn, 16)
                        sp.dma_start(asg[:], assign.rearrange("(o d) -> o d", o=1).to_broadcast([NCL, D])).then_inc(ld_ffn, 16)
                        for t in range(NT):
                            sp.wait_ge(s["x2"], t + 1)
                            sp.dma_start(mid_t[t // TB][:, t % TB, :], X[:, t, :]).then_inc(s["stored"], 16)
                        sp.wait_ge(s["stored"], 16 * NT)

                    @block.gpsimd
                    def _(pool):
                        nc.gpsimd.iota(clid[:], pattern=[[0, 1]], base=0, channel_multiplier=1).then_inc(s["iota"], 1)
                        for t in range(NT):
                            pool.wait_ge(s["u_done"], t + 1)
                            nc.gpsimd.tensor_tensor(X[:, t, :], X[:, t, :], ud[:, t % 2, 1], ALU.add).then_inc(s["x2"], 1)

                    @block.scalar
                    def _(act):
                        def root(b):
                            act.wait_ge(s["var"], b + 1)
                            nc.scalar.activation(std[:], mv[:, :, 1], ACT.Sqrt).then_inc(s["std"], 1)

                        def transposed(b):
                            if b >= 1:
                                act.wait_ge(s["lgps"], b)
                                act.wait_ge(s["lo"], DC * b)
                            for c in range(DC):
                                act.wait_ge(s["turned"], DC * b + c + 1)
                                modulate(hT[:, c, :], BANK_T + c, 0, MOD_CB, MOD_SB, c, b).then_inc(s["hT"], 1)
                                modulate(hT_hi[:, b, c, :], BANK_T + c, 0, MOD_CB, MOD_SB, c, b).then_inc(s["hi"], 1)

                        root(0)
                        act.wait_ge(s["cen_ps"], 1)
                        nc.scalar.activation(cenT[:], ps[:, BANK_X, 0:DC * NCL].rearrange("p (c k) -> p c k", c=DC),
                                             ACT.Copy).then_inc(s["cenT"], 1)
                        for b in range(B):
                            transposed(b)
                            if b + 1 < B:
                                root(b + 1)
                            act.wait_ge(s["lg"], b + 1)
                            nc.scalar.activation(lg[:], lg[:], ACT.Exp, scale=1.0 / TEMPERATURE).then_inc(s["ex"], 1)
                        for c in range(DC):
                            act.wait_ge(s["w_ps"], c + 1)
                            nc.scalar.activation(wT_hi[:, c, :], ps[:, BANK_T + c, :], ACT.Copy).then_inc(s["w_hi"], 1)

                    @block.vector
                    def _(dve):
                        n_chain = [0]

                        def link(ins):
                            n_chain[0] += 1
                            ins.then_inc(s["chain"], 1)
                            dve.wait_ge(s["chain"], n_chain[0])

                        def statistics(b):
                            tile_stats(link, X[:, b * TB:(b + 1) * TB, :], stats, mv).then_inc(s["var"], 1)

                        def normal(b):
                            dve.wait_ge(s["std"], b + 1)
                            if b >= 1:
                                dve.wait_ge(s["turned"], DC * b)
                            normalise(link, X[:, b * TB:(b + 1) * TB, :], mv, std, xh).then_inc(s["xh"], 1)

                        link(nc.vector.memset(top[:], 0.0))
                        link(nc.vector.memset(ones[:], 1.0))
                        statistics(0)
                        normal(0)
                        dve.wait_ge(s["iota"], 1)
                        link(nc.vector.tensor_copy(clidf[:], clid[:]))
                        dve.wait_ge(ld_ffn, 64)
                        link(nc.vector.tensor_scalar(onehot[:], asg[:], clidf[:, 0:1], None, ALU.is_equal))
                        wide = lambda v: v.rearrange("p (k o) -> p k o", o=1).to_broadcast([P, TB, NCL])
                        for b in range(B):
                            for c in range(DC):
                                dve.wait_ge(s["hi"], DC * b + c + 1)
                                nc.vector.tensor_tensor(hT_lo[:, b, c, :], hT[:, c, :], hT_hi[:, b, c, :].bitcast(F32),
                                                        ALU.subtract).then_inc(s["lo"], 1)
                            if b + 1 < B:
                                dve.wait_ge(s["xh"], b + 1)
                                statistics(b + 1)
                                normal(b + 1)
                            dve.wait_ge(s["lgps"], b + 1)
                            lp = ps[:, BANK_L, 0:TB * NCL].rearrange("p (t k) -> p t k", t=TB)
                            link(nc.vector.tensor_reduce(red[:, 0], lp, AX.X, ALU.max))
                            nc.vector.tensor_tensor(lg[:], lp, wide(red[:, 0]), ALU.subtract).then_inc(s["lg"], 1)
                            dve.wait_ge(s["ex"], b + 1)
                            link(nc.vector.tensor_reduce(red[:, 1], lg[:], AX.X, ALU.add))
                            link(nc.vector.reciprocal(red[:, 1], red[:, 1]))
                            link(nc.vector.tensor_tensor(pr[:], lg[:], wide(red[:, 1]), ALU.mult))
                            link(nc.vector.tensor_reduce(red[:, 2], pr[:], AX.X, ALU.max))
                            link(nc.vector.tensor_scalar(qsel[:, b * TB:(b + 1) * TB], red[:, 2], THRESHOLD, None, ALU.is_gt))
                            link(nc.vector.tensor_tensor(top[:], top[:], pr[:], ALU.max))
                        nc.vector.tensor_reduce(topc[:], top[:].rearrange("p t k -> p k t"), AX.X, ALU.max).then_inc(s["top_done"], 1)
                        for c in range(DC):
                            dve.wait_ge(s["w_hi"], c + 1)
                            nc.vector.tensor_tensor(wT_lo[:, c, :], ps[:, BANK_T + c, :], wT_hi[:, c, :].bitcast(F32),
                                                    ALU.subtract).then_inc(s["w_lo"], 1)
                        dve.wait_ge(s["top_ps"], 1)
                        link(nc.vector.tensor_reduce(topv[:, 0:1], ps[0:NCL, BANK_X, 0:P], AX.X, ALU.max))
                        link(nc.vector.tensor_scalar(topv[:, 1:2], topv[:, 0:1], THRESHOLD, None, ALU.is_gt))
                        nc.vector.tensor_scalar(selb[:], ones[:], topv[:, 1:2], None, ALU.mult).then_inc(s["selb"], 1)
                        dve.wait_ge(s["rsel_ps"], 1)
                        link(nc.vector.tensor_copy(rsel[:], ps[:, BANK_L, :]))
                        for b in range(B):
                            dve.wait_ge(s["gate_ps"], b + 1)
                            nc.vector.tensor_tensor(gsel[:, b, :], ps[:, BANK_X, :], rsel[:], ALU.mult).then_inc(s["gsel"], 1)
                        dve.wait_ge(s["gsel"], B)
                        for t in range(NT):
                            dve.wait_ge(s["dense"], t + 1)
                            nc.vector.tensor_tensor(ud[:, t % 2, 0], ps[:, BANK_D + t % 2, :], bias_r[:], ALU.add) \
                                .then_inc(s["dense_read"], 1)
                            dve.wait_ge(s["dense_read"], t + 1)
                            if t >= 2:
                                dve.wait_ge(s["x2"], t - 1)
                            nc.vector.scalar_tensor_tensor(ud[:, t % 2, 1], ud[:, t % 2, 0], qsel[:, t:t + 1],
                                                           gsel[:, t // TB, :], ALU.mult, ALU.mult).then_inc(s["u_done"], 1)

                    @block.tensor
                    def _(pe):
                        pe.wait_ge(ld_ffn, 64)
                        for c in range(DC):
                            last = nc.tensor.transpose(ps[:, BANK_X, c * NCL:(c + 1) * NCL], cen_in[:, c * P:(c + 1) * P],
                                                       ident[0:NCL, 0:NCL])
                        last.then_inc(s["cen_ps"], 1)
                        for b in range(B):
                            pe.wait_ge(s["xh"], b + 1)
                            for c in range(DC):
                                if b >= 1:
                                    pe.wait_ge(s["hi"], DC * (b - 1) + c + 1)
                                turn_chunk(BANK_T + c, xh, c).then_inc(s["turned"], 1)
                            if b == 0:
                                pe.wait_ge(s["cenT"], 1)
                            else:
                                pe.wait_ge(s["lg"], b)
                            pe.wait_ge(s["hT"], DC * (b + 1))
                            for t in range(TB):
                                for c in range(DC):
                                    last = nc.tensor.matmul(ps[:, BANK_L, t * NCL:(t + 1) * NCL],
                                                            hT[:, c, t * P:(t + 1) * P], cenT[:, c, :],
                                                            start=(c == 0), stop=(c == DC - 1))
                            last.then_inc(s["lgps"], 1)
                        pe.wait_ge(s["hi"], DC * B)
                        for c in range(DC):
                            for o in range(DC):
                                last = nc.tensor.transpose(ps[:, BANK_T + c, o * P:(o + 1) * P],
                                                           w_in[:, o, c * P:(c + 1) * P], ident[:])
                            last.then_inc(s["w_ps"], 1)
                        pe.wait_ge(s["top_done"], 1)
                        nc.tensor.transpose(ps[0:NCL, BANK_X, 0:P], topc[:], ident[:]).then_inc(s["top_ps"], 1)
                        pe.wait_ge(s["selb"], 1)
                        nc.tensor.matmul(ps[:, BANK_L, :], selb[:], onehot[:], start=True, stop=True).then_inc(s["rsel_ps"], 1)
                        for b in range(B):
                            if b >= 1:
                                pe.wait_ge(s["gsel"], b)
                            gate_rows(pe, BANK_X, 0, MOD_GB, b).then_inc(s["gate_ps"], 1)
                        pe.wait_ge(s["w_lo"], DC)
                        pe.wait_ge(s["lo"], DC * B)
                        for t in range(NT):
                            if t >= 2:
                                pe.wait_ge(s["dense_read"], t - 1)
                            b, r = t // TB, t % TB
                            parts = [(hT_hi, wT_hi), (hT_lo, wT_hi), (hT_hi, wT_lo)]
                            for c in range(DC):
                                for n, (h, w) in enumerate(parts):
                                    last = nc.tensor.matmul(ps[:, BANK_D + t % 2, :], h[:, b, c, r * P:(r + 1) * P], w[:, c, :],
                                                            start=(c == 0 and n == 0), stop=(c == DC - 1 and n == 2))
                            last.then_inc(s["dense"], 1)

                clear(f)

        a = ExitStack()
        with a:
            NP = PAIR * TB
            UNITS = PAIR * GQ
            KEYS = [(i + 1) * P for i in range(TB)]
            SC = [(3, 0, 0, 512), (2, 1, 0, 384), (1, 2, 0, 256), (0, 2, 256, 256)]
            PO = {3: 0, 2: 512, 1: 896, 0: 1152}
            PW = 1280
            T0, T2, TZ, T3, T1 = 0, 512, 768, 896, 1024
            TW = 1408
            PVS = [(T0, 512, 0, 0), (T1, 384, P, 1), (T2, 256, 2 * P, 2), (TZ, 256, 2 * P, 3)]
            BANK_S, BANK_T, BANK_V, BANK_J = 0, 3, 5, 6
            JOBS = ["V0", "K0", "Q0", "K1", "Q1", "V1"] + [f"Q{u}" for u in range(2, UNITS)] + \
                   [f"W{t}" for t in range(NP)]
            NJ = len(JOBS)
            TJOBS = ["V0"] + [f"0.{k}" for k in range(3)] + ["V1"] + [f"{u}.{k}" for u in range(1, UNITS) for k in range(3)]
            NTJ = len(TJOBS)
            TJOB = {n: i for i, n in enumerate(TJOBS)}
            assert NJ % 2 == 0 and NTJ % 2 == 0
            JOB = {n: i for i, n in enumerate(JOBS)}

            wq_in = sb(a, "wq_in", [P, DC, D], F32)
            wk_in = sb(a, "wk_in", [P, DC, HD], F32)
            wv_in = sb(a, "wv_in", [P, DC, HD], F32)
            wo_in = sb(a, "wo_in", [P, GQ, D], F32)
            wq = [sb(a, f"wq{i}", [P, DC, D], F32R) for i in range(2)]
            wk = [sb(a, f"wk{i}", [P, DC, HD], F32R) for i in range(2)]
            wv = [sb(a, f"wv{i}", [P, DC, HD], F32R) for i in range(2)]
            wo = [sb(a, f"wo{i}", [P, GQ, D], F32R) for i in range(2)]
            hT = [sb(a, f"hT{i}", [P, DC, PAIR * S], F32R) for i in range(2)]
            acc = sb(a, "acc", [P, NP, D], F32)

            wq_v = w_q.rearrange("(c p) n -> p c n", p=P)
            wk_v = w_k.rearrange("(c p) n -> p c n", p=P)
            wv_v = w_v.rearrange("(c p) n -> p c n", p=P)
            wo_v = w_o.rearrange("(g h p) n -> g p h n", p=P, h=GQ)
            qkv_in, wo_ld = sem(a, "qkv_in"), sem(a, "wo_ld")
            qkv_split, wo_split = sem(a, "qkv_split"), sem(a, "wo_split")
            NSPL = 2 + GQ

            def load_qkv(sp, g):
                sp.dma_start(wk_in[:], wk_v[:, :, bass.ts(g, HD)]).then_inc(qkv_in, 16)
                sp.dma_start(wv_in[:], wv_v[:, :, bass.ts(g, HD)]).then_inc(qkv_in, 16)
                sp.dma_start(wq_in[:], wq_v[:, :, bass.ts(g, D)]).then_inc(qkv_in, 16)

            waits_seen = sem(a, "waits_seen")

            def round_part(dst, src):
                nc.gpsimd.sem_inc(waits_seen, 1)
                return nc.gpsimd.tensor_copy(dst, src)

            def split_qkv(pool, hi_done, hi_base, before):
                n = 0
                for dst, src, w in ((wk, wk_in, HD), (wv, wv_in, HD), (wq, wq_in, D)):
                    for q in range(w // HD):
                        cols = slice(q * HD, (q + 1) * HD)
                        before(n)
                        round_part(dst[0][:, :, cols], src[:, :, cols]).then_inc(hi_done, 1)
                        n += 1
                        pool.wait_ge(hi_done, hi_base + n)
                        nc.gpsimd.tensor_tensor(dst[1][:, :, cols], src[:, :, cols], dst[0][:, :, cols].bitcast(F32),
                                                ALU.subtract).then_inc(qkv_split, 1)

            for pair in range(B // PAIR):
                ln = ExitStack()
                with ln:
                    xt = sb(ln, "xt", [P, 2, TB, D], F32)
                    stats = sb(ln, "stats", [P, TB, 6], F32)
                    mv = sb(ln, "mv", [P, TB, 2], F32)
                    std = sb(ln, "std", [P, TB], F32)
                    hf = sb(ln, "hf", [P, DC, S], F32)
                    xh = sb(ln, "xh", [P, TB, D], F32)
                    s = {n: sem(ln, "n_" + n) for n in ("ld", "chain", "var", "std", "xh", "turned", "hf", "hi", "lo",
                                                        "split")}
                    with nc.Block() as block:
                        @block.sync
                        def _(sp):
                            for i in range(PAIR):
                                sp.dma_start(xt[:, i], mid_t[PAIR * pair + i]).then_inc(s["ld"], 16)
                            if pair == 0:
                                load_qkv(sp, 0)

                        @block.gpsimd
                        def _(pool):
                            if pair == 0:
                                pool.wait_ge(qkv_in, 48)
                                split_qkv(pool, s["split"], 0, lambda n: None)
                                pool.sem_inc(wo_split, GQ)

                        @block.scalar
                        def _(act):
                            for i in range(PAIR):
                                b = PAIR * pair + i
                                act.wait_ge(s["var"], i + 1)
                                nc.scalar.activation(std[:], mv[:, :, 1], ACT.Sqrt).then_inc(s["std"], 1)
                                if i >= 1:
                                    act.wait_ge(s["lo"], DC * i)
                                for c in range(DC):
                                    act.wait_ge(s["turned"], DC * i + c + 1)
                                    modulate(hf[:, c, :], BANK_T - 1 + c, 1, MOD_CA, MOD_SA, c, b).then_inc(s["hf"], 1)
                                    modulate(hT[0][:, c, i * S:(i + 1) * S], BANK_T - 1 + c, 1, MOD_CA, MOD_SA, c, b) \
                                        .then_inc(s["hi"], 1)

                        @block.vector
                        def _(dve):
                            n_chain = [0]

                            def link(ins):
                                n_chain[0] += 1
                                ins.then_inc(s["chain"], 1)
                                dve.wait_ge(s["chain"], n_chain[0])

                            link(nc.vector.memset(acc[:], 0.0))
                            for i in range(PAIR):
                                dve.wait_ge(s["ld"], 16 * PAIR)
                                if i >= 1:
                                    dve.wait_ge(s["xh"], i)
                                tile_stats(link, xt[:, i], stats, mv).then_inc(s["var"], 1)
                                dve.wait_ge(s["std"], i + 1)
                                if i >= 1:
                                    dve.wait_ge(s["turned"], DC * i)
                                normalise(link, xt[:, i], mv, std, xh).then_inc(s["xh"], 1)
                                for c in range(DC):
                                    dve.wait_ge(s["hi"], DC * i + c + 1)
                                    nc.vector.tensor_tensor(hT[1][:, c, i * S:(i + 1) * S], hf[:, c, :],
                                                            hT[0][:, c, i * S:(i + 1) * S].bitcast(F32),
                                                            ALU.subtract).then_inc(s["lo"], 1)

                        @block.tensor
                        def _(pe):
                            for i in range(PAIR):
                                pe.wait_ge(s["xh"], i + 1)
                                for c in range(DC):
                                    if i >= 1:
                                        pe.wait_ge(s["hi"], DC * (i - 1) + c + 1)
                                    turn_chunk(BANK_T - 1 + c, xh, c).then_inc(s["turned"], 1)

                    clear(ln)

                at = ExitStack()
                with at:
                    vT = sb(at, "vT", [P, S], F32)
                    kT = [sb(at, f"kT{i}", [P, PAIR, S], F32R) for i in range(2)]
                    V = [sb(at, f"V{i}", [P, PAIR, TB, HD], F32R) for i in range(2)]
                    qT = [sb(at, f"qT{i}", [P, 2, S], F32R) for i in range(2)]
                    pe_ = sb(at, "probs", [P, 2, PW], F32)
                    pt = [sb(at, f"pt{i}", [P, TW], F32R) for i in range(2)]
                    oT = [sb(at, f"oT{i}", [P, PAIR, GQ, S], F32R) for i in range(2)]
                    nmax = sb(at, "nmax", [P, 2, TB], F32)
                    rsum = sb(at, "rsum", [P, 2, TB], F32)
                    rinv = sb(at, "rinv", [P, 2, TB], F32)

                    job_full = sem(at, "job_full")
                    job_hi, kq_ready, v_copied = (sem(at, n) for n in ("job_hi", "kq_ready", "v_copied"))
                    s_full, max_done, exp_done, rinv_done, p_ready = (sem(at, n) for n in (
                        "s_full", "max_done", "exp_done", "rinv_done", "p_ready"))
                    t_full, t_hi, t_ready = (sem(at, n) for n in ("t_full", "t_hi", "t_ready"))
                    o_full, o_hi, o_ready = (sem(at, n) for n in ("o_full", "o_hi", "o_ready"))
                    zeroed, w_hi, acc_done = (sem(at, n) for n in ("zeroed", "w_hi", "acc_done"))

                    KQ_JOBS = [j for j in JOBS if j[0] in "KQ"]
                    NKQ = len(KQ_JOBS)
                    STEP_Q = {u: u + 2 for u in range(UNITS - 2)}
                    STEP_W = {UNITS - 2: (0, 1), UNITS - 1: (2, 3)}

                    def full(g, name):
                        return NJ * g + (JOB[name] + 2)

                    def turned(g, name):
                        return NTJ * g + (TJOB[name] + 1)

                    def parted(g, name):
                        return NTJ * g + (TJOB[name] + 3)

                    def left(g, j):
                        name = JOBS[j]
                        if j < 0:
                            return acc_done, NP * g + (NP + j + 1)
                        if name[0] == "W":
                            return acc_done, NP * g + (NP + int(name[1:]) + 1)
                        if name[0] == "V":
                            return v_copied, PAIR * g + (int(name[1:]) + 1)
                        return kq_ready, NKQ * g + (KQ_JOBS.index(name) + 1)

                    with nc.Block() as block:
                        @block.sync
                        def _(sp):
                            with sp.Fori(0, NKV) as g:
                                sp.wait_ge(wo_split, GQ * g + GQ * (1 + pair * NKV))
                                sp.dma_start(wo_in[:], wo_v[bass.ds(g, 1)].rearrange("g p h n -> p (g h) n")).then_inc(wo_ld, 16)
                                sp.wait_ge(qkv_split, NSPL * g + NSPL * (1 + pair * NKV))
                                load_qkv(sp, (g + 1) % NKV)

                        @block.gpsimd
                        def _(pool):
                            HIS = GQ + NSPL
                            with pool.Fori(0, NKV) as g:
                                pool.wait_ge(wo_ld, 16 * g + 16 * (1 + pair * NKV))
                                pool.wait_ge(job_full, NJ * g + 1)
                                for h in range(GQ):
                                    round_part(wo[0][:, h, :], wo_in[:, h, :]).then_inc(w_hi, 1)
                                    pool.wait_ge(w_hi, HIS * g + (h + 1))
                                    nc.gpsimd.tensor_tensor(wo[1][:, h, :], wo_in[:, h, :], wo[0][:, h, :].bitcast(F32),
                                                            ALU.subtract).then_inc(wo_split, 1)
                                pool.wait_ge(qkv_in, 48 * g + 48 * (2 + pair * NKV))
                                last_use = ["K1", "V1"] + [f"Q{u}" for u in range(UNITS - GQ, UNITS)]
                                split_qkv(pool, w_hi, HIS * g + GQ, lambda n: pool.wait_ge(job_full, full(g, last_use[n])))

                        @block.tensor
                        def _(pe):
                            pe.sem_inc(job_full, 1)
                            pe.wait_ge(zeroed, 2)
                            with pe.Fori(0, NKV) as g:
                                def job_bank(name):
                                    j = JOB[name]
                                    pe.wait_ge(*left(g, j - 2))
                                    return BANK_J + j % 2

                                def project(name, w, cols, b):
                                    bank = job_bank(name)
                                    for c in range(DC):
                                        for n, (i, k) in enumerate(((0, 0), (0, 1), (1, 0))):
                                            last = nc.tensor.matmul(ps[:, bank, :], w[i][:, c, cols],
                                                                    hT[k][:, c, b * S:(b + 1) * S],
                                                                    start=(c == 0 and n == 0), stop=(c == DC - 1 and n == 2))
                                    last.then_inc(job_full, 1)
                                    return last

                                def q_project(u):
                                    h = u % GQ
                                    project(f"Q{u}", wq, slice(h * HD, (h + 1) * HD), u // GQ)

                                def turn_bank(name):
                                    j = TJOB[name]
                                    pe.wait_ge(t_ready, NTJ * g + (j + 1))
                                    return BANK_T + j % 2

                                def turn_v(b):
                                    bank = turn_bank(f"V{b}")
                                    pe.wait_ge(v_copied, PAIR * g + (b + 1))
                                    for t in range(TB):
                                        last = nc.tensor.transpose(ps[:, bank, t * P:(t + 1) * P], vT[:, t * P:(t + 1) * P], ident[:])
                                    last.then_inc(t_full, 1)

                                def scores(u):
                                    b = u // GQ
                                    pe.wait_ge(kq_ready, NKQ * g + (KQ_JOBS.index(f"Q{u}") + 1))
                                    for n, (i, bank, col, N) in enumerate(SC):
                                        if n < 3:
                                            pe.wait_ge(exp_done, UNITS * TB * g + (TB * u + (1, 2, 4)[n]))
                                        q = slice(i * P, (i + 1) * P)
                                        for k, (x_, y_) in enumerate(((0, 0), (0, 1), (1, 0))):
                                            last = nc.tensor.matmul(ps[:, BANK_S + bank, col:col + N], qT[x_][:, u % 2, q],
                                                                    kT[y_][:, b, 0:N], start=(k == 0), stop=(k == 2))
                                        last.then_inc(s_full, 1)

                                def turn(u, k):
                                    if k == 0:
                                        pe.wait_ge(p_ready, UNITS * TB * g + TB * (u + 1))
                                    bank = turn_bank(f"{u}.{k}")
                                    blocks = ([(i, 0) for i in range(4)], [(3, 3), (1, 1), (2, 1), (3, 1)], [(2, 2), (3, 2)])[k]
                                    for n, (i, kt) in enumerate(blocks):
                                        last = nc.tensor.transpose(ps[:, bank, n * P:(n + 1) * P],
                                                                   pe_[:, u % 2, PO[i] + kt * P:PO[i] + (kt + 1) * P], ident[:])
                                    last.then_inc(t_full, 1)

                                def outputs(u):
                                    b = u // GQ
                                    if u % GQ == 0:
                                        pe.wait_ge(t_ready, parted(g, f"V{b}"))
                                    pe.wait_ge(o_ready, UNITS * g + (u + 1))
                                    for n, (col, N, q0, kt) in enumerate(PVS):
                                        if n < 3:
                                            pe.wait_ge(t_ready, parted(g, f"{u}.{n}"))
                                        for k, (x_, y_) in enumerate(((0, 0), (1, 0), (0, 1))):
                                            last = nc.tensor.matmul(ps[:, BANK_V, q0:q0 + N], V[x_][:, b, kt, :],
                                                                    pt[y_][:, col:col + N], start=(n == 0 and k == 0),
                                                                    stop=(n == 3 and k == 2))
                                    last.then_inc(o_full, 1)

                                def out_project(t):
                                    bank = job_bank(f"W{t}")
                                    b, r = t // TB, t % TB
                                    if t == 0:
                                        pe.wait_ge(wo_split, GQ * g + GQ * (2 + pair * NKV))
                                    for h in range(GQ):
                                        if r == 0:
                                            pe.wait_ge(o_ready, UNITS * g + (GQ * b + h + 2))
                                        for n, (x_, y_) in enumerate(((0, 0), (1, 0), (0, 1))):
                                            last = nc.tensor.matmul(ps[:, bank, :], oT[x_][:, b, h, r * P:(r + 1) * P], wo[y_][:, h, :],
                                                                    start=(h == 0 and n == 0), stop=(h == GQ - 1 and n == 2))
                                    last.then_inc(job_full, 1)

                                def split_done(n):
                                    pe.wait_ge(qkv_split, NSPL * g + (NSPL * pair * NKV + n))

                                split_done(2)
                                project("V0", wv, slice(0, HD), 0)
                                project("K0", wk, slice(0, HD), 0)
                                split_done(3)
                                q_project(0)
                                turn_v(0)
                                project("K1", wk, slice(0, HD), 1)
                                scores(0)
                                split_done(4)
                                q_project(1)
                                project("V1", wv, slice(0, HD), 1)
                                for u in range(UNITS):
                                    if u + 1 < UNITS:
                                        scores(u + 1)
                                    turn(u, 0)
                                    turn(u, 1)
                                    if u in STEP_Q:
                                        if STEP_Q[u] < GQ:
                                            split_done(3 + STEP_Q[u])
                                        q_project(STEP_Q[u])
                                    for t in STEP_W.get(u, ())[0:1]:
                                        out_project(t)
                                    turn(u, 2)
                                    for t in STEP_W.get(u, ())[1:2]:
                                        out_project(t)
                                    outputs(u)
                                    if u == 0:
                                        turn_v(1)
                                for t in range(TB, NP):
                                    out_project(t)

                        @block.scalar
                        def _(act):
                            act.sem_inc(exp_done, TB)
                            with act.Fori(0, NKV) as g:
                                def hi(name, dst, scale=1.0):
                                    j = JOB[name]
                                    act.wait_ge(job_full, full(g, JOBS[j]))
                                    nc.scalar.activation(dst, ps[:, BANK_J + j % 2, :], ACT.Copy, scale=scale).then_inc(job_hi, 1)

                                def v_copy(b):
                                    j = JOB[f"V{b}"]
                                    act.wait_ge(job_full, full(g, JOBS[j]))
                                    nc.scalar.activation(vT[:], ps[:, BANK_J + j % 2, :], ACT.Copy).then_inc(v_copied, 1)

                                def exps(u):
                                    for n, (i, bank, col, _) in enumerate(SC):
                                        if n < 3:
                                            act.wait_ge(max_done, UNITS * TB * g + (TB * u + (1, 2, 4)[n]))
                                        nc.scalar.activation(pe_[:, u % 2, PO[i]:PO[i] + KEYS[i]], ps[:, BANK_S + bank, col:col + KEYS[i]],
                                                             ACT.Exp, bias=nmax[:, u % 2, i:i + 1], scale=-1.0,
                                                             accum_out=rsum[:, u % 2, i:i + 1]).then_inc(exp_done, 1)

                                def turned_hi(name, dst, N):
                                    act.wait_ge(t_full, turned(g, name))
                                    nc.scalar.activation(dst, ps[:, BANK_T + TJOB[name] % 2, 0:N], ACT.Copy).then_inc(t_hi, 1)

                                def t_part(u, k):
                                    col, N = ((T0, 512), (T3, 512), (T2, 256))[k]
                                    turned_hi(f"{u}.{k}", pt[0][:, col:col + N], N)

                                def v_part(b):
                                    turned_hi(f"V{b}", V[0][:, b].rearrange("p t d -> p (t d)"), 512)

                                hi_q = lambda u: hi(f"Q{u}", qT[0][:, u % 2, :], QSCALE)
                                v_copy(0)
                                hi("K0", kT[0][:, 0, :])
                                hi_q(0)
                                v_part(0)
                                hi("K1", kT[0][:, 1, :])
                                exps(0)
                                hi_q(1)
                                v_copy(1)
                                for u in range(UNITS):
                                    if u + 1 < UNITS:
                                        exps(u + 1)
                                    t_part(u, 0)
                                    t_part(u, 1)
                                    if u in STEP_Q:
                                        hi_q(STEP_Q[u])
                                    t_part(u, 2)
                                    act.wait_ge(o_full, UNITS * g + (u + 1))
                                    nc.scalar.activation(oT[0][:, u // GQ, u % GQ, :], ps[:, BANK_V, :], ACT.Copy).then_inc(o_hi, 1)
                                    if u == 0:
                                        v_part(1)

                        @block.vector
                        def _(dve):
                            for i in range(2):
                                nc.vector.memset(pt[i][:, TZ:TZ + P].bitcast(F32), 0.0).then_inc(zeroed, 1)
                            dve.sem_inc(t_ready, 2)
                            dve.sem_inc(o_ready, 1)
                            dve.sem_inc(acc_done, NP)
                            with dve.Fori(0, NKV) as g:
                                def lo(name, dst, hi_part, done, scale=1.0):
                                    j = JOB[name]
                                    dve.wait_ge(job_hi, NKQ * g + (KQ_JOBS.index(name) + 1))
                                    nc.vector.scalar_tensor_tensor(dst, ps[:, BANK_J + j % 2, :], scale, hi_part.bitcast(F32),
                                                                   ALU.mult, ALU.subtract).then_inc(done, 1)

                                def lo_kq(name, dst, hi_part, scale=1.0):
                                    lo(name, dst, hi_part, kq_ready, scale)

                                def lo_q(u):
                                    lo_kq(f"Q{u}", qT[1][:, u % 2, :], qT[0][:, u % 2, :], QSCALE)

                                def maxima(u):
                                    for n, (i, bank, col, _) in enumerate(SC):
                                        if n < 3:
                                            dve.wait_ge(s_full, UNITS * TB * g + (TB * u + (1, 2, 4)[n]))
                                            dve.sem_inc(waits_seen, 1)
                                        v = ps[:, BANK_S + bank, col:col + KEYS[i]]
                                        nc.vector.tensor_tensor_reduce(out=v, in0=v, in1=mask[:, TB * P - KEYS[i]:], scale=-1.0,
                                                                       scalar=3e38, op0=ALU.add, op1=ALU.min,
                                                                       accum_out=nmax[:, u % 2, i:i + 1]).then_inc(max_done, 1)

                                def scale_rows(u):
                                    dve.wait_ge(exp_done, UNITS * TB * g + (TB * (u + 1) + TB))
                                    nc.vector.reciprocal(rinv[:, u % 2, :], rsum[:, u % 2, :]).then_inc(rinv_done, 1)
                                    dve.wait_ge(rinv_done, UNITS * g + (u + 1))
                                    for i in range(TB):
                                        v = pe_[:, u % 2, PO[i]:PO[i] + KEYS[i]]
                                        nc.vector.tensor_scalar(v, v, rinv[:, u % 2, i:i + 1], None, ALU.mult).then_inc(p_ready, 1)

                                def turned_lo(name, dst, hi_part, N):
                                    dve.wait_ge(t_hi, turned(g, name))
                                    nc.vector.tensor_tensor(dst, ps[:, BANK_T + TJOB[name] % 2, 0:N], hi_part.bitcast(F32),
                                                            ALU.subtract).then_inc(t_ready, 1)

                                def t_part(u, k):
                                    col, N = ((T0, 512), (T3, 512), (T2, 256))[k]
                                    turned_lo(f"{u}.{k}", pt[1][:, col:col + N], pt[0][:, col:col + N], N)

                                def v_part(b):
                                    flat = lambda t: t[:, b].rearrange("p t d -> p (t d)")
                                    turned_lo(f"V{b}", flat(V[1]), flat(V[0]), 512)

                                def add_out(t):
                                    j = JOB[f"W{t}"]
                                    dve.wait_ge(job_full, full(g, JOBS[j]))
                                    nc.vector.tensor_tensor(acc[:, t, :], acc[:, t, :], ps[:, BANK_J + j % 2, :], ALU.add) \
                                        .then_inc(acc_done, 1)

                                lo_kq("K0", kT[1][:, 0, :], kT[0][:, 0, :])
                                lo_q(0)
                                v_part(0)
                                lo_kq("K1", kT[1][:, 1, :], kT[0][:, 1, :])
                                maxima(0)
                                scale_rows(0)
                                lo_q(1)
                                for u in range(UNITS):
                                    if u + 1 < UNITS:
                                        maxima(u + 1)
                                    t_part(u, 0)
                                    t_part(u, 1)
                                    if u in STEP_Q:
                                        lo_q(STEP_Q[u])
                                    for t in STEP_W.get(u, ())[0:1]:
                                        add_out(t)
                                    t_part(u, 2)
                                    if u + 1 < UNITS:
                                        scale_rows(u + 1)
                                    for t in STEP_W.get(u, ())[1:2]:
                                        add_out(t)
                                    dve.wait_ge(o_hi, UNITS * g + (u + 1))
                                    nc.vector.tensor_tensor(oT[1][:, u // GQ, u % GQ, :], ps[:, BANK_V, :],
                                                            oT[0][:, u // GQ, u % GQ, :].bitcast(F32), ALU.subtract) \
                                        .then_inc(o_ready, 1)
                                    if u == 0:
                                        v_part(1)
                                for t in range(TB, NP):
                                    add_out(t)

                    clear(at)

                cl = ExitStack()
                with cl:
                    xt = sb(cl, "xt", [P, PAIR, TB, D], F32)
                    s = {n: sem(cl, "c_" + n) for n in ("ld", "gate", "prod", "x3", "store")}
                    with nc.Block() as block:
                        @block.sync
                        def _(sp):
                            for i in range(PAIR):
                                sp.dma_start(xt[:, i], mid_t[PAIR * pair + i]).then_inc(s["ld"], 16)
                            for i in range(PAIR):
                                sp.wait_ge(s["x3"], i + 1)
                                sp.dma_start(mid_t[PAIR * pair + i], xt[:, i]).then_inc(s["store"], 16)
                            sp.wait_ge(s["store"], 16 * PAIR)

                        @block.vector
                        def _(dve):
                            for i in range(PAIR):
                                dve.wait_ge(s["gate"], i + 1)
                                for t in range(TB):
                                    last = nc.vector.tensor_tensor(acc[:, i * TB + t, :], acc[:, i * TB + t, :],
                                                                   ps[:, i, :], ALU.mult)
                                last.then_inc(s["prod"], 1)
                                dve.wait_ge(s["prod"], i + 1)
                                dve.wait_ge(s["ld"], 16 * PAIR)
                                nc.vector.tensor_tensor(xt[:, i], xt[:, i], acc[:, i * TB:(i + 1) * TB, :],
                                                        ALU.add).then_inc(s["x3"], 1)

                        @block.tensor
                        def _(pe):
                            for i in range(PAIR):
                                gate_rows(pe, i, 1, MOD_GA, PAIR * pair + i).then_inc(s["gate"], 1)

                    clear(cl)
            clear(a)

        f = ExitStack()
        with f:
            gw = sb(f, "gw", [P, DC, F], F32R)
            uw = sb(f, "uw", [P, DC, F], F32R)
            dw = sb(f, "dw", [P, FC, D], F32R)
            gsc = sb(f, "gsc", [P, FC], F32)
            usc = sb(f, "usc", [P, FC], F32)
            dgb = sb(f, "dgb", [P, B, D], F32)
            ld_s = sem(f, "ld_s")

            pr = ExitStack()
            with pr:
                UN = 2
                SL = 3 * UN
                raw = sb(pr, "raw", [P, SL, D], I32)
                wb = sb(pr, "wb", [P, SL, D], BF16)
                dsc = sb(pr, "dsc", [P, D], F32)
                s = {n: sem(pr, "p_" + n) for n in ("cast", "turned", "done", "gate", "dgb", "dsc")}
                ld = [sem(pr, f"ld{k}") for k in range(SL)]
                assert FC % UN == 0 and SL <= 8
                g_v = gate_wq.rearrange("(j p) i -> j p i", p=P)
                u_v = up_wq.rearrange("(j p) i -> j p i", p=P)
                d_v = down_wq.rearrange("(o p) (j i) -> j p o i", p=P, i=P)

                with nc.Block() as block:
                    @block.sync
                    def _(sp):
                        with sp.Fori(0, FC // UN) as i:
                            for k in range(SL):
                                j = i * UN + k // 3
                                sp.wait_ge(s["cast"], SL * i + (k + 1))
                                v = (g_v, u_v, d_v)[k % 3][bass.ds(j, 1)]
                                if k % 3 < 2:
                                    sp.dma_start(raw[:, k, :], v.rearrange("j p i -> p (j i)")).then_inc(ld[k], 16)
                                else:
                                    sp.dma_start(raw[:, k, :].rearrange("p (o i) -> p o i", i=P),
                                                 v.rearrange("j p o i -> p (j o) i")).then_inc(ld[k], 16)
                        with nc.allow_non_contiguous_dma("scales with the hidden width on partitions"):
                            sp.dma_start(gsc[:], gate_s.rearrange("(j p) -> p j", p=P)).then_inc(ld_s, 16)
                            sp.dma_start(usc[:], up_s.rearrange("(j p) -> p j", p=P)).then_inc(ld_s, 16)
                        sp.dma_start(dsc[:], down_s.rearrange("(o d) -> o d", o=1).to_broadcast([P, D])).then_inc(s["dsc"], 16)
                        sp.wait_ge(ld_s, 32)

                    @block.scalar
                    def _(act):
                        act.sem_inc(s["cast"], SL)
                        act.sem_inc(s["turned"], SL)
                        with act.Fori(0, FC // UN) as i:
                            for k in range(SL):
                                act.wait_ge(ld[k], 16 * i + 16)
                                act.wait_ge(s["turned"], SL * i + (k + 1))
                                nc.scalar.activation(wb[:, k, :], raw[:, k, :], ACT.Copy).then_inc(s["cast"], 1)

                    @block.tensor
                    def _(pe):
                        pe.wait_ge(s["cast"], SL)
                        with pe.Fori(0, FC // UN) as i:
                            for k in range(SL):
                                pe.wait_ge(s["cast"], SL * i + (SL + k + 1))
                                pe.wait_ge(s["done"], SL * i + (k + 1))
                                bank = ps[:, k, 0:D // 2].bitcast(BF16)
                                for c in range(DC):
                                    last = nc.tensor.transpose(bank[:, c * P:(c + 1) * P], wb[:, k, c * P:(c + 1) * P], ident_b[:])
                                last.then_inc(s["turned"], 1)
                        for b in range(B):
                            if b >= 2:
                                pe.wait_ge(s["dgb"], b - 1)
                            gate_rows(pe, 6 + b % 2, 1, MOD_GB, b).then_inc(s["gate"], 1)

                    @block.vector
                    def _(dve):
                        dve.sem_inc(s["done"], SL)
                        with dve.Fori(0, FC // UN) as i:
                            for k in range(SL):
                                j = i * UN + k // 3
                                dve.wait_ge(s["turned"], SL * i + (SL + k + 1))
                                bank = ps[:, k, 0:D // 2].bitcast(BF16)
                                if k % 3 < 2:
                                    dst = (gw, uw)[k % 3][:, :, bass.ds(j * P, P)]
                                    src = bank.rearrange("p (c o) -> p c o", c=DC)
                                else:
                                    dst = dw[:, bass.ds(j, 1), :].rearrange("p j o -> p (j o)")
                                    src = bank
                                nc.vector.tensor_copy(dst, src).then_inc(s["done"], 1)
                        dve.wait_ge(s["dsc"], 16)
                        for b in range(B):
                            dve.wait_ge(s["gate"], b + 1)
                            nc.vector.tensor_tensor(dgb[:, b, :], dsc[:], ps[:, 6 + b % 2, :], ALU.mult).then_inc(s["dgb"], 1)

                clear(pr)

            m = ExitStack()
            with m:
                xt = sb(m, "xt", [P, 2, TB, D], F32)
                stats = sb(m, "stats", [P, TB, 6], F32)
                mv = sb(m, "mv", [P, TB, 2], F32)
                std = sb(m, "std", [P, TB], F32)
                xh = sb(m, "xh", [P, TB, D], F32)
                hf = sb(m, "hf", [P, 2, S], F32)
                hT = [sb(m, f"hT{i}", [P, DC, S], F32R) for i in range(2)]
                sg = sb(m, "sg", [P, 2, S], F32)
                hid = sb(m, "hid", [P, 2, S], F32)
                hd = [sb(m, f"hd{i}", [P, FC, S], F32R) for i in range(2)]
                yt = sb(m, "yt", [P, 2, D], F32)
                s = {n: sem(m, "m_" + n) for n in ("stat", "stat_seen", "agg", "var", "std", "rstd", "xh", "turned", "hf", "hi", "lo",
                                                   "gate", "up", "sg", "hid", "hhi", "hlo", "down", "yt", "y")}
                ld = [sem(m, f"ld{k}") for k in range(2)]
                st = [sem(m, f"st{k}") for k in range(2)]
                BANK_T = 4
                LN_ROUNDS = B + 1

                with nc.Block() as block:
                    @block.sync
                    def _(sp):
                        sp.dma_start(xt[:, 0], mid_t[0]).then_inc(ld[0], 16)
                        sp.sem_inc(st[1], 16)
                        with sp.Fori(0, B // 2) as i:
                            for k in range(2):
                                sp.wait_ge(st[1 - k], (16 * TB * i + 16) if k == 0 else 16 * TB * (i + 1))
                                nb = (i * 2 + k + 1) % B
                                sp.dma_start(xt[:, 1 - k], mid_t[bass.ds(nb, 1)].rearrange("b p t d -> p (b t) d")) \
                                    .then_inc(ld[1 - k], 16)
                                for r in range(TB):
                                    sp.wait_ge(s["y"], TB * 2 * i + (TB * (k + 1) + r + 1))
                                    sp.dma_start(out_t[bass.ds(i * 2 + k, 1), :, r, :].rearrange("b p d -> p (b d)"),
                                                 xt[:, k, r, :]).then_inc(st[k], 16)
                        for k in range(2):
                            sp.wait_ge(st[k], 16 * TB * (B // 2) + 16 * k)
                        sp.wait_ge(ld[0], 16 * (B // 2 + 1))

                    @block.scalar
                    def _(act):
                        def norm(r, slot_rounds, b):
                            act.wait_ge(s["var"], slot_rounds + 1)
                            nc.scalar.activation(std[:], mv[:, :, 1], ACT.Sqrt).then_inc(s["std"], 1)

                        def modulated(r, b):
                            for c in range(DC):
                                act.wait_ge(s["turned"], DC * r + (c + 1))
                                act.wait_ge(s["lo"], DC * r + (c + 1))
                                bias = mod[1][:, DC * MOD_SB + c, bass.ds(b, 1)]
                                scale = mod[1][:, DC * MOD_CB + c, bass.ds(b, 1)]
                                for dst, done in ((hf[:, c % 2, :], "hf"), (hT[0][:, c, :], "hi")):
                                    nc.scalar.activation(dst, ps[:, BANK_T + c, :], ACT.Identity, bias=bias, scale=scale) \
                                        .then_inc(s[done], 1)

                        act.sem_inc(s["hi"], DC)
                        norm(0, 0, 0)
                        modulated(0, 0)
                        with act.Fori(0, B // 2) as i:
                            for k in range(2):
                                n = i * 2 + k
                                for j in range(FC):
                                    act.wait_ge(s["gate"], FC * 2 * i + (FC * k + j + 1))
                                    act.wait_ge(s["hid"], FC * 2 * i + (FC * k + j + 1))
                                    nc.scalar.activation(sg[:, j % 2, :], ps[:, 2 * (j % 2), :], ACT.Silu,
                                                         scale=gsc[:, j:j + 1]).then_inc(s["sg"], 1)
                                    act.wait_ge(s["hid"], FC * 2 * i + (FC * k + j + 3))
                                    nc.scalar.activation(hd[0][:, j, :], hid[:, j % 2, :], ACT.Copy).then_inc(s["hhi"], 1)
                                norm(0, i * 2 + (k + 1), 0)
                                modulated(i * 2 + (k + 1), (i * 2 + k + 1) % B)

                    @block.vector
                    def _(dve):
                        def statistics(r, slot, loads):
                            dve.wait_ge(ld[slot], loads)
                            for t in range(TB):
                                last = nc.vector.bn_stats(stats[:, t, :], xt[:, slot, t, :])
                            last.then_inc(s["stat"], 1)
                            dve.wait_ge(s["stat"], r + 1)
                            dve.sem_inc(s["stat_seen"], 1)
                            for t in range(TB):
                                last = nc.vector.bn_aggr(mv[:, t, :], stats[:, t, :])
                            last.then_inc(s["agg"], 1)
                            dve.wait_ge(s["agg"], r + 1)
                            nc.vector.tensor_scalar(mv[:, :, 1], mv[:, :, 1], EPS, None, ALU.add).then_inc(s["var"], 1)
                            dve.wait_ge(s["std"], r + 1)
                            nc.vector.reciprocal(std[:], std[:]).then_inc(s["rstd"], 1)
                            dve.wait_ge(s["rstd"], r + 1)
                            for t in range(TB):
                                last = nc.vector.tensor_scalar(xh[:, t, :], xt[:, slot, t, :], mv[:, t, 0:1], std[:, t:t + 1],
                                                               ALU.subtract, ALU.mult)
                            last.then_inc(s["xh"], 1)

                        def lows(r):
                            for c in range(DC):
                                dve.wait_ge(s["hi"], DC * r + (DC + c + 1))
                                nc.vector.tensor_tensor(hT[1][:, c, :], hf[:, c % 2, :], hT[0][:, c, :].bitcast(F32),
                                                        ALU.subtract).then_inc(s["lo"], 1)

                        dve.wait_ge(ld_s, 32)
                        dve.sem_inc(s["hid"], 2)
                        dve.sem_inc(s["lo"], 2)
                        dve.sem_inc(s["hlo"], 1)
                        dve.sem_inc(s["y"], TB)
                        statistics(0, 0, 16)
                        lows(0)
                        with dve.Fori(0, B // 2) as i:
                            for k in range(2):
                                r = i * 2 + (k + 1)
                                for j in range(FC):
                                    n = FC * 2 * i + (FC * k + j)
                                    dve.wait_ge(s["up"], n + 1)
                                    dve.wait_ge(s["sg"], n + 1)
                                    dve.wait_ge(s["hlo"], n + 1)
                                    nc.vector.scalar_tensor_tensor(hid[:, j % 2, :], ps[:, 2 * (j % 2) + 1, :], usc[:, j:j + 1],
                                                                   sg[:, j % 2, :], ALU.mult, ALU.mult).then_inc(s["hid"], 1)
                                    dve.wait_ge(s["hhi"], n + 1)
                                    nc.vector.tensor_tensor(hd[1][:, j, :], hid[:, j % 2, :], hd[0][:, j, :].bitcast(F32),
                                                            ALU.subtract).then_inc(s["hlo"], 1)
                                statistics(r, 1 - k, 16 * (i + 1) if k == 0 else 16 * (i + 2))
                                lows(r)
                                for t in range(TB):
                                    q = TB * 2 * i + (TB * k + t)
                                    dve.wait_ge(s["down"], q + 1)
                                    gate = dgb[:, bass.ds(i * 2 + k, 1), :].rearrange("p b d -> p (b d)")
                                    nc.vector.tensor_tensor(yt[:, t % 2, :], gate, ps[:, t, :], ALU.mult).then_inc(s["yt"], 1)
                                    dve.wait_ge(s["yt"], q + 1)
                                    nc.vector.tensor_tensor(xt[:, k, t, :], xt[:, k, t, :], yt[:, t % 2, :], ALU.add) \
                                        .then_inc(s["y"], 1)

                    @block.tensor
                    def _(pe):
                        def turn(r):
                            pe.wait_ge(s["xh"], r + 1)
                            for c in range(DC):
                                pe.wait_ge(s["hi"], DC * r + (c + 1))
                                turn_chunk(BANK_T + c, xh, c).then_inc(s["turned"], 1)

                        turn(0)
                        with pe.Fori(0, B // 2) as i:
                            for k in range(2):
                                for j in range(FC):
                                    n = FC * 2 * i + (FC * k + j)
                                    if j == 0:
                                        pe.wait_ge(s["lo"], DC * 2 * i + (DC * (k + 1) + 2))
                                        pe.wait_ge(s["y"], TB * 2 * i + TB * (k + 1))
                                    pe.wait_ge(s["hid"], n + 1)
                                    for w, bank, done in ((gw, 2 * (j % 2), "gate"), (uw, 2 * (j % 2) + 1, "up")):
                                        for c in range(DC):
                                            for h in range(2):
                                                last = nc.tensor.matmul(ps[:, bank, :], w[:, c, j * P:(j + 1) * P], hT[h][:, c, :],
                                                                        start=(c == 0 and h == 0), stop=(c == DC - 1 and h == 1))
                                        last.then_inc(s[done], 1)
                                turn(i * 2 + (k + 1))
                                pe.wait_ge(s["hlo"], FC * 2 * i + (FC * (k + 1) + 1))
                                for t in range(TB):
                                    for j in range(FC):
                                        for h in range(2):
                                            last = nc.tensor.matmul(ps[:, t, :], hd[h][:, j, t * P:(t + 1) * P], dw[:, j, :],
                                                                    start=(j == 0 and h == 0), stop=(j == FC - 1 and h == 1))
                                    last.then_inc(s["down"], 1)


_INS = ['L0_attn_x', 'L0_attn_Wq', 'L0_attn_bq', 'L0_attn_Wk', 'L0_attn_bk', 'L0_attn_Wv', 'L0_attn_bv', 'L0_ffn_weight',
        'L0_ffn_bias', 'L0_ffn_centroids', 'L0_ffn_assignments', 'L0_c', 'L0_wmod', 'L1_attn_w_q', 'L1_attn_w_k',
        'L1_attn_w_v', 'L1_attn_w_o', 'L1_ffn_gate_wq', 'L1_ffn_gate_scale', 'L1_ffn_up_wq', 'L1_ffn_up_scale',
        'L1_ffn_down_wq', 'L1_ffn_down_scale', 'L1_c', 'L1_wmod']


def kernel(**inputs):
    import numpy as _np
    import concourse.bacc as _bacc
    from concourse import mybir as _mybir
    from concourse.bass_utils import run_bass_kernel_spmd as _run

    nc = _bacc.Bacc("TRN2", target_bir_lowering=False, num_devices=1)
    arrays, args = {}, []
    for name in _INS:
        a = _np.ascontiguousarray(inputs[name])
        arrays[f"in_{name}_dram"] = a
        args.append(nc.dram_tensor(f"in_{name}_dram", a.shape, _mybir.dt.from_np(a.dtype), kind="ExternalInput").ap())
    x = arrays["in_L0_attn_x_dram"]
    args.append(nc.dram_tensor("out_0_dram", x.shape, _mybir.dt.from_np(x.dtype), kind="ExternalOutput").ap())
    adaln_two_blocks(nc, *args)
    r = _run(nc, [arrays], core_ids=[0])
    return r.results[0]["out_0_dram"]
```

```python
from contextlib import ExitStack

import concourse.bass as bass
from concourse import mybir

ALU = mybir.AluOpType
ACT = mybir.ActivationFunctionType
AX = mybir.AxisListType
F32 = mybir.dt.float32
F32R = mybir.dt.float32r
BF16 = mybir.dt.bfloat16
I32 = mybir.dt.int32

P = 128
EPS = 1e-5
NEG = -1e30
GATE_MIN = 0.25
THRESHOLD = 0.01
TEMPERATURE = 0.1
MOD_SA, MOD_CA, MOD_GA, MOD_SB, MOD_CB, MOD_GB = range(6)


def adaln_two_blocks(nc, x, Wq, bq, Wk, bk, Wv, bv, ffn_w, ffn_b, cent, assign, c0, wmod0,
                     w_q, w_k, w_v, w_o, gate_wq, gate_s, up_wq, up_s, down_wq, down_s, c1, wmod1, out):
    B, S, D = x.shape
    DC = D // P
    TB = S // P
    NT = B * TB
    NM = 6 * D // P
    E0, H0 = Wq.shape[1], Wq.shape[2]
    NCL = cent.shape[0]
    HD = P
    NQ = w_q.shape[1] // HD
    NKV = w_k.shape[1] // HD
    GQ = NQ // NKV
    F = gate_wq.shape[0]
    FC = F // P
    QSCALE = float(HD) ** -0.5
    PAIR = 2
    assert D == 512 and S == 512 and E0 * H0 == D and GQ * HD == D and F % P == 0

    x_t = x.rearrange("b (t p) d -> b p t d", p=P)
    out_t = out.rearrange("b (t p) d -> b p t d", p=P)
    mid = nc.dram_tensor("x_mid", [B, S, D], F32, kind="Internal").ap()
    mid_t = mid.rearrange("b (t p) d -> b p t d", p=P)
    att = nc.dram_tensor("attended", [B, S, D], F32, kind="Internal").ap()
    att_t = att.rearrange("b (t p) d -> b p t d", p=P)

    ctx = ExitStack()
    with ctx:
        names = [0]

        def sb(stack, name, shape, dt):
            names[0] += 1
            return stack.enter_context(nc.sbuf_tensor(f"{name}_{names[0]}", shape, dt))

        def sem(name):
            names[0] += 1
            return ctx.enter_context(nc.semaphore(f"{name}_{names[0]}"))

        ps = ctx.enter_context(nc.psum_tensor("ps", [P, 8, 512], F32))
        ident = sb(ctx, "ident", [P, P], F32)
        ident_b = sb(ctx, "ident_b", [P, P], BF16)
        mod = [sb(ctx, f"mod{layer}", [P, NM, B], F32) for layer in range(2)]

        mv_2 = sb(ctx, "mv_2", [P, NT, 2], F32)
        rstd_2 = sb(ctx, "rstd_2", [P, NT], F32)

        def gate_rows(pe, bank, layer, which, b):
            for c in range(DC):
                col = mod[layer][:, DC * which + c, b:b + 1].to_broadcast([P, P])
                last = nc.tensor.transpose(ps[:, bank, c * P:(c + 1) * P], col, ident[:])
            return last

        def mods_products(pe, bank, layer, wm, cT):
            for n in range(NM):
                for k in range(DC):
                    last = nc.tensor.matmul(ps[:, bank, n * B:(n + 1) * B], wm[:, k, n * P:(n + 1) * P],
                                            cT[:, layer, k, :], start=(k == 0), stop=(k == DC - 1))
            return last

        def mods_finish(link, layer, bank, tmp):
            m = mod[layer]
            link(nc.vector.tensor_copy(m[:], ps[:, bank, 0:NM * B].rearrange("p (n b) -> p n b", b=B)))
            for which in (MOD_CA, MOD_CB):
                v = m[:, DC * which:DC * which + DC, :]
                link(nc.vector.tensor_scalar(v, v, 1.0, None, ALU.add))
            for which in (MOD_GA, MOD_GB):
                v = m[:, DC * which:DC * which + DC, :]
                link(nc.vector.tensor_scalar(tmp[:, 0], v, 0.0, 2.0, ALU.is_ge, ALU.mult))
                link(nc.vector.tensor_scalar(tmp[:, 0], tmp[:, 0], 1.0, None, ALU.subtract))
                link(nc.vector.scalar_tensor_tensor(tmp[:, 1], v, -1.0, v, ALU.mult, ALU.max))
                link(nc.vector.scalar_tensor_tensor(v, tmp[:, 1], GATE_MIN, tmp[:, 0], ALU.max, ALU.mult))

        def tile_stats(link, xt, stats, mv):
            for t in range(TB):
                last = nc.vector.bn_stats(stats[:, t, :], xt[:, t, :])
            link(last)
            for t in range(TB):
                last = nc.vector.bn_aggr(mv[:, t, :], stats[:, t, :])
            link(last)
            return nc.vector.tensor_scalar(mv[:, :, 1], mv[:, :, 1], EPS, None, ALU.add)

        def normalise(link, xt, mv, std, xh):
            link(nc.vector.reciprocal(std[:], std[:]))
            for t in range(TB):
                last = nc.vector.tensor_scalar(xh[:, t, :], xt[:, t, :], mv[:, t, 0:1], std[:, t:t + 1],
                                               ALU.subtract, ALU.mult)
            return last

        def turn_chunk(bank, xh, c):
            for t in range(TB):
                last = nc.tensor.transpose(ps[:, bank, t * P:(t + 1) * P], xh[:, t, c * P:(c + 1) * P], ident[:])
            return last

        def modulate(dst, bank, layer, scale, shift, c, b):
            return nc.scalar.activation(dst, ps[:, bank, :], ACT.Identity,
                                        bias=mod[layer][:, DC * shift + c, b:b + 1],
                                        scale=mod[layer][:, DC * scale + c, b:b + 1])

        l0 = ExitStack()
        with l0:
            X = sb(l0, "X", [P, NT, D], F32)
            ld_ffn = sem("ld_ffn")

            a = ExitStack()
            with a:
                wm0 = sb(a, "wm0", [P, DC, 6 * D], F32)
                wm1 = sb(a, "wm1", [P, DC, 6 * D], F32)
                cT = sb(a, "cT", [P, 2, DC, B], F32)
                tmp_g = sb(a, "tmp_g", [P, 2, DC, B], F32)
                ld_wm1 = sem("ld_wm1")
                c_in = sb(a, "c_in", [B, 2, D], F32)
                c_act = sb(a, "c_act", [B, 2, D], F32)
                wq_in = sb(a, "wq_in", [P, DC, D], F32)
                wcat = sb(a, "wcat", [P, DC, 3 * E0], F32)
                bq_in = sb(a, "bq_in", [P, D], F32)
                bcat = sb(a, "bcat", [P, 3 * E0], F32)
                stats = sb(a, "stats", [P, TB, 6], F32)
                mv = sb(a, "mv", [P, TB, 2], F32)
                std = sb(a, "std", [P, TB], F32)
                xh = sb(a, "xh", [P, TB, D], F32)
                hT = sb(a, "hT", [P, DC, S], F32)
                qkv = sb(a, "qkv", [P, TB, 3 * E0], F32)
                sc = sb(a, "sc", [P, TB, E0 * E0], F32)
                ex = sb(a, "ex", [P, TB, E0 * E0], F32)
                red = sb(a, "red", [P, 4, TB * E0], F32)
                upd = sb(a, "upd", [P, TB, D], F32)
                ld_c, ld_w, ld_wm, ld_b = (sem(n) for n in ("ld_c", "ld_w", "ld_wm", "ld_b"))
                ld_x = [sem(f"ld_x{b}") for b in range(B)]
                consts, silu_done, ct_turned, ct_copied = (sem(n) for n in ("consts", "silu", "ct_turned", "ct_copied"))
                mods_ps, mods_done, chain = (sem(n) for n in ("mods_ps", "mods_done", "chain"))
                var_done, std_done, xh_done, turned, hT_done = (sem(n) for n in ("var", "std", "xh", "turned", "hT"))
                projected, logits, ex_done, upd_done, wcat_done = (sem(n) for n in ("projected", "logits", "ex", "upd", "wcat"))
                gates_ps, x1_done = sem("gates_ps"), sem("x1")
                BANK_C, BANK_MOD, BANK_T, BANK_P, BANK_G = 0, 1, 2, 6, 7

                with nc.Block() as block:
                    @block.sync
                    def _(sp):
                        for layer, c in enumerate((c0, c1)):
                            sp.dma_start(c_in[:, layer, :], c).then_inc(ld_c, 16)
                        sp.dma_start(X[:, 0:TB, :], x_t[0]).then_inc(ld_x[0], 16)
                        wm_v = wmod0.rearrange("(c p) n -> c p n", p=P)
                        for c in range(DC):
                            sp.dma_start(wm0[:, c, :], wm_v[c]).then_inc(ld_wm, 16)
                        sp.dma_start(wq_in[:], Wq.rearrange("(c p) e h -> p c (e h)", p=P)).then_inc(ld_w, 16)
                        sp.dma_start(wcat[:, :, E0:2 * E0], Wk.rearrange("(c p) e o -> p c (e o)", p=P)).then_inc(ld_w, 16)
                        sp.dma_start(wcat[:, :, 2 * E0:3 * E0], Wv.rearrange("(c p) e o -> p c (e o)", p=P)).then_inc(ld_w, 16)
                        sp.dma_start(bq_in[:], bq.rearrange("(o e) h -> o (e h)", o=1).to_broadcast([P, D])).then_inc(ld_b, 16)
                        sp.dma_start(bcat[:, E0:2 * E0], bk.rearrange("e o -> o e").to_broadcast([P, E0])).then_inc(ld_b, 16)
                        sp.dma_start(bcat[:, 2 * E0:3 * E0], bv.rearrange("e o -> o e").to_broadcast([P, E0])).then_inc(ld_b, 16)
                        for b in range(1, B):
                            sp.dma_start(X[:, b * TB:(b + 1) * TB, :], x_t[b]).then_inc(ld_x[b], 16)
                        sp.dma_start(wm1[:], wmod1.rearrange("(c p) n -> p c n", p=P)).then_inc(ld_wm1, 16)

                    @block.gpsimd
                    def _(pool):
                        nc.gpsimd.memset(ident[:], 0.0).then_inc(consts, 1)
                        pool.wait_ge(consts, 1)
                        nc.gpsimd.affine_select(out=ident[:], in_=ident[:], compare_op=ALU.not_equal, fill=1.0,
                                                base=0, pattern=[[-1, P]], channel_multiplier=1).then_inc(consts, 1)
                        pool.wait_ge(consts, 2)
                        nc.gpsimd.tensor_copy(ident_b[:], ident[:]).then_inc(consts, 1)
                        for b in range(B):
                            Xb = X[:, b * TB:(b + 1) * TB, :]
                            pool.wait_ge(upd_done, b + 1)
                            nc.gpsimd.tensor_tensor(Xb, Xb, upd[:], ALU.add).then_inc(x1_done, 1)

                    @block.scalar
                    def _(act):
                        act.wait_ge(ld_c, 32)
                        nc.scalar.activation(c_act[:], c_in[:], ACT.Silu).then_inc(silu_done, 1)

                        def root(b):
                            act.wait_ge(var_done, b + 1)
                            nc.scalar.activation(std[:], mv[:, :, 1], ACT.Sqrt).then_inc(std_done, 1)

                        def transposed(b):
                            if b == 0:
                                act.wait_ge(mods_done, 1)
                            else:
                                act.wait_ge(projected, b)
                            for c in range(DC):
                                act.wait_ge(turned, DC * b + c + 1)
                                modulate(hT[:, c, :], BANK_T + c, 0, MOD_CA, MOD_SA, c, b).then_inc(hT_done, 1)

                        root(0)
                        transposed(0)
                        for b in range(B):
                            if b + 1 < B:
                                root(b + 1)
                                transposed(b + 1)
                            act.wait_ge(logits, b + 1)
                            nc.scalar.activation(ex[:], sc[:], ACT.Exp, scale=float(E0) ** -0.5).then_inc(ex_done, 1)

                    @block.vector
                    def _(dve):
                        n_chain = [0]

                        def link(ins):
                            n_chain[0] += 1
                            ins.then_inc(chain, 1)
                            dve.wait_ge(chain, n_chain[0])

                        def statistics(b):
                            dve.wait_ge(ld_x[b], 16)
                            if b >= 1:
                                dve.wait_ge(xh_done, b)
                            tile_stats(link, X[:, b * TB:(b + 1) * TB, :], stats, mv).then_inc(var_done, 1)

                        def normal(b):
                            dve.wait_ge(std_done, b + 1)
                            if b >= 1:
                                dve.wait_ge(turned, DC * b)
                            normalise(link, X[:, b * TB:(b + 1) * TB, :], mv, std, xh).then_inc(xh_done, 1)

                        statistics(0)
                        normal(0)
                        dve.wait_ge(ct_turned, 1)
                        nc.vector.tensor_copy(cT[:], ps[:, BANK_C, 0:2 * DC * B].rearrange(
                            "p (l c b) -> p l c b", l=2, b=B)).then_inc(ct_copied, 1)
                        dve.wait_ge(ld_w, 48)
                        for c in range(DC):
                            last = nc.vector.tensor_reduce(wcat[:, c, 0:E0], wq_in[:, c, :].rearrange(
                                "p (e h) -> p e h", h=H0), AX.X, ALU.add)
                        last.then_inc(wcat_done, 1)
                        dve.wait_ge(ld_b, 48)
                        link(nc.vector.tensor_reduce(bcat[:, 0:E0], bq_in[:].rearrange("p (e h) -> p e h", h=H0),
                                                     AX.X, ALU.add))
                        dve.wait_ge(mods_ps, 1)
                        mods_finish(link, 0, BANK_MOD, tmp_g)
                        dve.sem_inc(mods_done, 1)

                        flat = lambda t: t.rearrange("p t k -> p (t k)")
                        for b in range(B):
                            if b + 1 < B:
                                statistics(b + 1)
                                normal(b + 1)
                            dve.wait_ge(projected, b + 1)
                            pv = ps[:, BANK_P, 0:TB * 3 * E0].rearrange("p (t k) -> p t k", t=TB)
                            link(nc.vector.tensor_tensor(qkv[:], pv, bcat[:].rearrange("p (o k) -> p o k", o=1)
                                                         .to_broadcast([P, TB, 3 * E0]), ALU.add))
                            s4 = sc[:].rearrange("p t (d e) -> p t d e", e=E0)
                            row = lambda k: qkv[:, :, k * E0:(k + 1) * E0].rearrange("p t (o e) -> p t o e", o=1) \
                                .to_broadcast([P, TB, E0, E0])
                            col = qkv[:, :, 0:E0].rearrange("p t (d o) -> p t d o", o=1).to_broadcast([P, TB, E0, E0])
                            link(nc.vector.tensor_tensor(s4, col, row(1), ALU.mult))
                            s3 = sc[:].rearrange("p t (d e) -> p (t d) e", e=E0)
                            e3 = ex[:].rearrange("p t (d e) -> p (t d) e", e=E0)
                            wide = lambda v: v.rearrange("p (k o) -> p k o", o=1).to_broadcast([P, TB * E0, E0])
                            link(nc.vector.tensor_reduce(red[:, 0], s3, AX.X, ALU.max))
                            nc.vector.tensor_tensor(s3, s3, wide(red[:, 0]), ALU.subtract).then_inc(logits, 1)
                            dve.wait_ge(ex_done, b + 1)
                            link(nc.vector.tensor_reduce(red[:, 1], e3, AX.X, ALU.add))
                            link(nc.vector.tensor_tensor(s4, ex[:].rearrange("p t (d e) -> p t d e", e=E0), row(2), ALU.mult))
                            link(nc.vector.tensor_reduce(red[:, 2], s3, AX.X, ALU.add))
                            link(nc.vector.reciprocal(red[:, 1], red[:, 1]))
                            link(nc.vector.tensor_tensor(red[:, 3], red[:, 2], red[:, 1], ALU.mult))
                            dve.wait_ge(gates_ps, b + 1)
                            if b >= 1:
                                dve.wait_ge(x1_done, b)
                            for t in range(TB):
                                o = red[:, 3, t * E0:(t + 1) * E0].rearrange("p (d o) -> p d o", o=1).to_broadcast([P, E0, H0])
                                last = nc.vector.tensor_tensor(upd[:, t, :].rearrange("p (d h) -> p d h", h=H0),
                                                               ps[:, BANK_G, :].rearrange("p (d h) -> p d h", h=H0), o, ALU.mult)
                            last.then_inc(upd_done, 1)
                        dve.wait_ge(mods_ps, 2)
                        mods_finish(link, 1, BANK_MOD, tmp_g)

                    @block.tensor
                    def _(pe):
                        pe.wait_ge(consts, 2)
                        pe.wait_ge(silu_done, 1)
                        for layer in range(2):
                            for c in range(DC):
                                k = (layer * DC + c) * B
                                last = nc.tensor.transpose(ps[:, BANK_C, k:k + B], c_act[:, layer, c * P:(c + 1) * P],
                                                           ident[0:B, 0:B])
                        last.then_inc(ct_turned, 1)

                        def turn(b):
                            pe.wait_ge(xh_done, b + 1)
                            for c in range(DC):
                                if b >= 1:
                                    pe.wait_ge(hT_done, DC * (b - 1) + c + 1)
                                turn_chunk(BANK_T + c, xh, c).then_inc(turned, 1)

                        turn(0)
                        pe.wait_ge(ct_copied, 1)
                        pe.wait_ge(ld_wm, 16 * DC)
                        mods_products(pe, BANK_MOD, 0, wm0, cT).then_inc(mods_ps, 1)
                        pe.wait_ge(mods_done, 1)
                        pe.wait_ge(wcat_done, 1)
                        for b in range(B):
                            pe.wait_ge(hT_done, DC * (b + 1))
                            if b >= 1:
                                pe.wait_ge(logits, b)
                            for t in range(TB):
                                for c in range(DC):
                                    last = nc.tensor.matmul(ps[:, BANK_P, t * 3 * E0:(t + 1) * 3 * E0],
                                                            hT[:, c, t * P:(t + 1) * P], wcat[:, c, :],
                                                            start=(c == 0), stop=(c == DC - 1))
                            last.then_inc(projected, 1)
                            if b >= 1:
                                pe.wait_ge(upd_done, b)
                            gate_rows(pe, BANK_G, 0, MOD_GA, b).then_inc(gates_ps, 1)
                            if b + 1 < B:
                                turn(b + 1)
                        pe.wait_ge(ld_wm1, 16)
                        mods_products(pe, BANK_MOD, 1, wm1, cT).then_inc(mods_ps, 1)


            f = ExitStack()
            with f:
                w_in = sb(f, "w_in", [P, DC, D], F32)
                wT_hi = sb(f, "wT_hi", [P, DC, D], F32R)
                wT_lo = sb(f, "wT_lo", [P, DC, D], F32R)
                cen_in = sb(f, "cen_in", [NCL, D], F32)
                cenT = sb(f, "cenT", [P, DC, NCL], F32)
                bias_r = sb(f, "bias_r", [P, D], F32)
                asg = sb(f, "asg", [NCL, D], I32)
                stats = sb(f, "stats", [P, TB, 6], F32)
                mv = sb(f, "mv", [P, TB, 2], F32)
                std = sb(f, "std", [P, TB], F32)
                xh = sb(f, "xh", [P, TB, D], F32)
                hT = sb(f, "hT", [P, DC, S], F32)
                hT_hi = sb(f, "hT_hi", [P, B, DC, S], F32R)
                hT_lo = sb(f, "hT_lo", [P, B, DC, S], F32R)
                lg = sb(f, "lg", [P, TB, NCL], F32)
                pr = sb(f, "pr", [P, TB, NCL], F32)
                top = sb(f, "top", [P, TB, NCL], F32)
                red = sb(f, "red", [P, 3, TB], F32)
                qsel = sb(f, "qsel", [P, NT], F32)
                topc = sb(f, "topc", [P, NCL], F32)
                topv = sb(f, "topv", [NCL, 2], F32)
                ones = sb(f, "ones", [NCL, P], F32)
                selb = sb(f, "selb", [NCL, P], F32)
                clid = sb(f, "clid", [NCL, 1], I32)
                clidf = sb(f, "clidf", [NCL, 1], F32)
                onehot = sb(f, "onehot", [NCL, D], F32)
                rsel = sb(f, "rsel", [P, D], F32)
                gsel = sb(f, "gsel", [P, B, D], F32)
                ud = sb(f, "ud", [P, 2, 2, D], F32)
                stats_2 = sb(f, "stats_2", [P, NT, 6], F32)
                names_ = ("chain", "var", "std", "xh", "turned", "hT", "hi", "lo", "cen_ps", "cenT", "w_ps", "w_hi",
                          "w_lo", "lgps", "lg", "ex", "iota", "top_done", "top_ps", "selb", "rsel_ps", "rsel",
                          "gate_ps", "gsel", "dense", "dense_read", "u_done", "x2", "stored", "var_2", "std_2")
                s = {n: sem("f_" + n) for n in names_}
                BANK_L, BANK_X = 0, 1
                BANK_T, BANK_D = 2, 6

                with nc.Block() as block:
                    @block.sync
                    def _(sp):
                        sp.dma_start(cen_in[:], cent).then_inc(ld_ffn, 16)
                        sp.dma_start(w_in[:], ffn_w.rearrange("(c p) i -> p c i", p=P)).then_inc(ld_ffn, 16)
                        sp.dma_start(bias_r[:], ffn_b.rearrange("(o d) -> o d", o=1).to_broadcast([P, D])).then_inc(ld_ffn, 16)
                        sp.dma_start(asg[:], assign.rearrange("(o d) -> o d", o=1).to_broadcast([NCL, D])).then_inc(ld_ffn, 16)
                        for t in range(NT):
                            sp.wait_ge(s["x2"], t + 1)
                            sp.dma_start(mid_t[t // TB][:, t % TB, :], X[:, t, :]).then_inc(s["stored"], 16)
                        sp.wait_ge(s["stored"], 16 * NT)

                    @block.gpsimd
                    def _(pool):
                        nc.gpsimd.iota(clid[:], pattern=[[0, 1]], base=0, channel_multiplier=1).then_inc(s["iota"], 1)
                        for t in range(NT):
                            pool.wait_ge(s["u_done"], t + 1)
                            nc.gpsimd.tensor_tensor(X[:, t, :], X[:, t, :], ud[:, t % 2, 1], ALU.add).then_inc(s["x2"], 1)

                    @block.scalar
                    def _(act):
                        def root(b):
                            act.wait_ge(s["var"], b + 1)
                            nc.scalar.activation(std[:], mv[:, :, 1], ACT.Sqrt).then_inc(s["std"], 1)

                        def transposed(b):
                            if b >= 1:
                                act.wait_ge(s["lgps"], b)
                                act.wait_ge(s["lo"], DC * b)
                            for c in range(DC):
                                act.wait_ge(s["turned"], DC * b + c + 1)
                                modulate(hT[:, c, :], BANK_T + c, 0, MOD_CB, MOD_SB, c, b).then_inc(s["hT"], 1)
                                modulate(hT_hi[:, b, c, :], BANK_T + c, 0, MOD_CB, MOD_SB, c, b).then_inc(s["hi"], 1)

                        root(0)
                        act.wait_ge(s["cen_ps"], 1)
                        nc.scalar.activation(cenT[:], ps[:, BANK_X, 0:DC * NCL].rearrange("p (c k) -> p c k", c=DC),
                                             ACT.Copy).then_inc(s["cenT"], 1)
                        for b in range(B):
                            transposed(b)
                            if b + 1 < B:
                                root(b + 1)
                            act.wait_ge(s["lg"], b + 1)
                            nc.scalar.activation(lg[:], lg[:], ACT.Exp, scale=1.0 / TEMPERATURE).then_inc(s["ex"], 1)
                        for c in range(DC):
                            act.wait_ge(s["w_ps"], c + 1)
                            nc.scalar.activation(wT_hi[:, c, :], ps[:, BANK_T + c, :], ACT.Copy).then_inc(s["w_hi"], 1)
                        act.wait_ge(s["var_2"], 1)
                        nc.scalar.activation(rstd_2[:], mv_2[:, :, 1], ACT.Sqrt).then_inc(s["std_2"], 1)

                    @block.vector
                    def _(dve):
                        n_chain = [0]

                        def link(ins):
                            n_chain[0] += 1
                            ins.then_inc(s["chain"], 1)
                            dve.wait_ge(s["chain"], n_chain[0])

                        def statistics(b):
                            tile_stats(link, X[:, b * TB:(b + 1) * TB, :], stats, mv).then_inc(s["var"], 1)

                        def normal(b):
                            dve.wait_ge(s["std"], b + 1)
                            if b >= 1:
                                dve.wait_ge(s["turned"], DC * b)
                            normalise(link, X[:, b * TB:(b + 1) * TB, :], mv, std, xh).then_inc(s["xh"], 1)

                        link(nc.vector.memset(top[:], 0.0))
                        link(nc.vector.memset(ones[:], 1.0))
                        statistics(0)
                        normal(0)
                        dve.wait_ge(s["iota"], 1)
                        link(nc.vector.tensor_copy(clidf[:], clid[:]))
                        dve.wait_ge(ld_ffn, 64)
                        link(nc.vector.tensor_scalar(onehot[:], asg[:], clidf[:, 0:1], None, ALU.is_equal))
                        wide = lambda v: v.rearrange("p (k o) -> p k o", o=1).to_broadcast([P, TB, NCL])
                        for b in range(B):
                            for c in range(DC):
                                dve.wait_ge(s["hi"], DC * b + c + 1)
                                nc.vector.tensor_tensor(hT_lo[:, b, c, :], hT[:, c, :], hT_hi[:, b, c, :].bitcast(F32),
                                                        ALU.subtract).then_inc(s["lo"], 1)
                            if b + 1 < B:
                                dve.wait_ge(s["xh"], b + 1)
                                statistics(b + 1)
                                normal(b + 1)
                            dve.wait_ge(s["lgps"], b + 1)
                            lp = ps[:, BANK_L, 0:TB * NCL].rearrange("p (t k) -> p t k", t=TB)
                            link(nc.vector.tensor_reduce(red[:, 0], lp, AX.X, ALU.max))
                            nc.vector.tensor_tensor(lg[:], lp, wide(red[:, 0]), ALU.subtract).then_inc(s["lg"], 1)
                            dve.wait_ge(s["ex"], b + 1)
                            link(nc.vector.tensor_reduce(red[:, 1], lg[:], AX.X, ALU.add))
                            link(nc.vector.reciprocal(red[:, 1], red[:, 1]))
                            link(nc.vector.tensor_tensor(pr[:], lg[:], wide(red[:, 1]), ALU.mult))
                            link(nc.vector.tensor_reduce(red[:, 2], pr[:], AX.X, ALU.max))
                            link(nc.vector.tensor_scalar(qsel[:, b * TB:(b + 1) * TB], red[:, 2], THRESHOLD, None, ALU.is_gt))
                            link(nc.vector.tensor_tensor(top[:], top[:], pr[:], ALU.max))
                        nc.vector.tensor_reduce(topc[:], top[:].rearrange("p t k -> p k t"), AX.X, ALU.max).then_inc(s["top_done"], 1)
                        for c in range(DC):
                            dve.wait_ge(s["w_hi"], c + 1)
                            nc.vector.tensor_tensor(wT_lo[:, c, :], ps[:, BANK_T + c, :], wT_hi[:, c, :].bitcast(F32),
                                                    ALU.subtract).then_inc(s["w_lo"], 1)
                        dve.wait_ge(s["top_ps"], 1)
                        link(nc.vector.tensor_reduce(topv[:, 0:1], ps[0:NCL, BANK_X, 0:P], AX.X, ALU.max))
                        link(nc.vector.tensor_scalar(topv[:, 1:2], topv[:, 0:1], THRESHOLD, None, ALU.is_gt))
                        nc.vector.tensor_scalar(selb[:], ones[:], topv[:, 1:2], None, ALU.mult).then_inc(s["selb"], 1)
                        dve.wait_ge(s["rsel_ps"], 1)
                        link(nc.vector.tensor_copy(rsel[:], ps[:, BANK_L, :]))
                        for b in range(B):
                            dve.wait_ge(s["gate_ps"], b + 1)
                            nc.vector.tensor_tensor(gsel[:, b, :], ps[:, BANK_X, :], rsel[:], ALU.mult).then_inc(s["gsel"], 1)
                        dve.wait_ge(s["gsel"], B)
                        for t in range(NT):
                            dve.wait_ge(s["dense"], t + 1)
                            nc.vector.tensor_tensor(ud[:, t % 2, 0], ps[:, BANK_D + t % 2, :], bias_r[:], ALU.add) \
                                .then_inc(s["dense_read"], 1)
                            dve.wait_ge(s["dense_read"], t + 1)
                            if t >= 2:
                                dve.wait_ge(s["x2"], t - 1)
                            nc.vector.scalar_tensor_tensor(ud[:, t % 2, 1], ud[:, t % 2, 0], qsel[:, t:t + 1],
                                                           gsel[:, t // TB, :], ALU.mult, ALU.mult).then_inc(s["u_done"], 1)
                            if t >= 2:
                                nc.vector.bn_stats(stats_2[:, t - 2, :], X[:, t - 2, :])
                        for t in (NT - 2, NT - 1):
                            dve.wait_ge(s["x2"], t + 1)
                            last = nc.vector.bn_stats(stats_2[:, t, :], X[:, t, :])
                        link(last)
                        for t in range(NT):
                            last = nc.vector.bn_aggr(mv_2[:, t, :], stats_2[:, t, :])
                        link(last)
                        nc.vector.tensor_scalar(mv_2[:, :, 1], mv_2[:, :, 1], EPS, None, ALU.add).then_inc(s["var_2"], 1)
                        dve.wait_ge(s["std_2"], 1)
                        link(nc.vector.reciprocal(rstd_2[:], rstd_2[:]))

                    @block.tensor
                    def _(pe):
                        pe.wait_ge(ld_ffn, 64)
                        for c in range(DC):
                            last = nc.tensor.transpose(ps[:, BANK_X, c * NCL:(c + 1) * NCL], cen_in[:, c * P:(c + 1) * P],
                                                       ident[0:NCL, 0:NCL])
                        last.then_inc(s["cen_ps"], 1)
                        for b in range(B):
                            pe.wait_ge(s["xh"], b + 1)
                            for c in range(DC):
                                if b >= 1:
                                    pe.wait_ge(s["hi"], DC * (b - 1) + c + 1)
                                turn_chunk(BANK_T + c, xh, c).then_inc(s["turned"], 1)
                            if b == 0:
                                pe.wait_ge(s["cenT"], 1)
                            else:
                                pe.wait_ge(s["lg"], b)
                            pe.wait_ge(s["hT"], DC * (b + 1))
                            for t in range(TB):
                                for c in range(DC):
                                    last = nc.tensor.matmul(ps[:, BANK_L, t * NCL:(t + 1) * NCL],
                                                            hT[:, c, t * P:(t + 1) * P], cenT[:, c, :],
                                                            start=(c == 0), stop=(c == DC - 1))
                            last.then_inc(s["lgps"], 1)
                        pe.wait_ge(s["hi"], DC * B)
                        for c in range(DC):
                            for o in range(DC):
                                last = nc.tensor.transpose(ps[:, BANK_T + c, o * P:(o + 1) * P],
                                                           w_in[:, o, c * P:(c + 1) * P], ident[:])
                            last.then_inc(s["w_ps"], 1)
                        pe.wait_ge(s["top_done"], 1)
                        nc.tensor.transpose(ps[0:NCL, BANK_X, 0:P], topc[:], ident[:]).then_inc(s["top_ps"], 1)
                        pe.wait_ge(s["selb"], 1)
                        nc.tensor.matmul(ps[:, BANK_L, :], selb[:], onehot[:], start=True, stop=True).then_inc(s["rsel_ps"], 1)
                        for b in range(B):
                            if b >= 1:
                                pe.wait_ge(s["gsel"], b)
                            gate_rows(pe, BANK_X, 0, MOD_GB, b).then_inc(s["gate_ps"], 1)
                        pe.wait_ge(s["w_lo"], DC)
                        pe.wait_ge(s["lo"], DC * B)
                        for t in range(NT):
                            if t >= 2:
                                pe.wait_ge(s["dense_read"], t - 1)
                            b, r = t // TB, t % TB
                            parts = [(hT_hi, wT_hi), (hT_lo, wT_hi), (hT_hi, wT_lo)]
                            for c in range(DC):
                                for n, (h, w) in enumerate(parts):
                                    last = nc.tensor.matmul(ps[:, BANK_D + t % 2, :], h[:, b, c, r * P:(r + 1) * P], w[:, c, :],
                                                            start=(c == 0 and n == 0), stop=(c == DC - 1 and n == 2))
                            last.then_inc(s["dense"], 1)


        a = ExitStack()
        with a:
            NP = PAIR * TB
            UNITS = PAIR * GQ
            KEYS = [(i + 1) * P for i in range(TB)]
            SC = [(3, 0, 0), (2, 1, 0), (1, 2, 0), (0, 2, 256)]
            PO = {3: 0, 2: 512, 1: 896, 0: 1152}
            PW = 1280
            T0, T2, T1 = 0, 512, 768
            TW = 1152
            PVS = [(T0, 512, 0, 0), (T1, 384, P, 1), (T2, 256, 2 * P, 2)]
            BANK_S, BANK_T, BANK_V, BANK_J = 0, 3, 5, 6
            JOBS = ["V0", "K0", "Q0", "K1", "Q1", "V1"] + [f"Q{u}" for u in range(2, UNITS)] + \
                   [f"W{t}" for t in range(NP)]
            NJ = len(JOBS)
            TJOBS = ["V0"] + [f"0.{k}" for k in range(3)] + ["V1"] + [f"{u}.{k}" for u in range(1, UNITS) for k in range(3)]
            NTJ = len(TJOBS)
            TJOB = {n: i for i, n in enumerate(TJOBS)}
            assert NJ % 2 == 0 and NTJ % 2 == 0
            JOB = {n: i for i, n in enumerate(JOBS)}

            wq_in = sb(a, "wq_in", [P, DC, D], F32)
            wk_in = sb(a, "wk_in", [P, DC, HD], F32)
            wv_in = sb(a, "wv_in", [P, DC, HD], F32)
            wo_in = sb(a, "wo_in", [P, GQ, D], F32)
            wq = [sb(a, f"wq{i}", [P, DC, D], F32R) for i in range(2)]
            wk = [sb(a, f"wk{i}", [P, DC, HD], F32R) for i in range(2)]
            wv = [sb(a, f"wv{i}", [P, DC, HD], F32R) for i in range(2)]
            wo = [sb(a, f"wo{i}", [P, GQ, D], F32R) for i in range(2)]
            hT = [sb(a, f"hT{i}", [P, DC, PAIR * S], F32R) for i in range(2)]
            acc = sb(a, "acc", [P, NP, D], F32)

            wq_v = w_q.rearrange("(c p) n -> p c n", p=P)
            wk_v = w_k.rearrange("(c p) n -> p c n", p=P)
            wv_v = w_v.rearrange("(c p) n -> p c n", p=P)
            wo_v = w_o.rearrange("(g h p) n -> g p h n", p=P, h=GQ)
            qkv_in, wo_ld = sem("qkv_in"), sem("wo_ld")
            qkv_split, wo_split = sem("qkv_split"), sem("wo_split")
            NSPL = 2 + GQ

            def load_qkv(sp, g):
                sp.dma_start(wk_in[:], wk_v[:, :, bass.ts(g, HD)]).then_inc(qkv_in, 16)
                sp.dma_start(wv_in[:], wv_v[:, :, bass.ts(g, HD)]).then_inc(qkv_in, 16)
                sp.dma_start(wq_in[:], wq_v[:, :, bass.ts(g, D)]).then_inc(qkv_in, 16)

            waits_seen = sem("waits_seen")

            def round_part(dst, src):
                nc.gpsimd.sem_inc(waits_seen, 1)
                return nc.gpsimd.tensor_copy(dst, src)

            def split_qkv(pool, hi_done, hi_base, before):
                n = 0
                for dst, src, w in ((wk, wk_in, HD), (wv, wv_in, HD), (wq, wq_in, D)):
                    for q in range(w // HD):
                        cols = slice(q * HD, (q + 1) * HD)
                        before(n)
                        round_part(dst[0][:, :, cols], src[:, :, cols]).then_inc(hi_done, 1)
                        n += 1
                        pool.wait_ge(hi_done, hi_base + n)
                        nc.gpsimd.tensor_tensor(dst[1][:, :, cols], src[:, :, cols], dst[0][:, :, cols].bitcast(F32),
                                                ALU.subtract).then_inc(qkv_split, 1)

            at = ExitStack()
            with at:
                with ExitStack() as early:
                    rows_1 = sb(early, "rows_1", [P, TB, D], F32)
                    hf = sb(early, "hf", [P, PAIR, DC, S], F32)
                kT = [sb(at, f"kT{i}", [P, PAIR, S], F32R) for i in range(2)]
                oT = [sb(at, f"oT{i}", [P, PAIR, GQ, S], F32R) for i in range(2)]
                vT = sb(at, "vT", [P, S], F32)
                V = [sb(at, f"V{i}", [P, PAIR, TB - 1, HD], F32R) for i in range(2)]
                qT = [sb(at, f"qT{i}", [P, 2, S - P], F32R) for i in range(2)]
                pe_ = sb(at, "probs", [P, 2, PW], F32)
                pt = [sb(at, f"pt{i}", [P, TW], F32R) for i in range(2)]
                q_first = sb(at, "q_first", [P, 2, P], F32)
                k_first = sb(at, "k_first", [P, PAIR, P], F32)
                v_last = sb(at, "v_last", [P, PAIR, HD], F32)
                pt_last = sb(at, "pt_last", [P, P], F32)
                nmax = sb(at, "nmax", [P, 2, TB], F32)
                rsum = sb(at, "rsum", [P, 2, TB], F32)
                rinv = sb(at, "rinv", [P, 2, TB], F32)

                job_full = sem("job_full")
                job_hi, kq_ready, v_copied = (sem(n) for n in ("job_hi", "kq_ready", "v_copied"))
                s_full, max_done, exp_done, rinv_done, p_ready = (sem(n) for n in (
                    "s_full", "max_done", "exp_done", "rinv_done", "p_ready"))
                t_full, t_hi, t_ready = (sem(n) for n in ("t_full", "t_hi", "t_ready"))
                o_full, o_hi, o_ready = (sem(n) for n in ("o_full", "o_hi", "o_ready"))
                w_hi, acc_done, cleared = (sem(n) for n in ("w_hi", "acc_done", "cleared"))
                gate_r = sb(at, "gate_r", [P, B, D], F32)
                mask = sb(at, "mask", [P, TB * P], F32)
                masked = sem("masked")
                gates_full, gates_copied, gated = (sem(n) for n in ("gates_full", "gates_copied", "gated"))
                n_xh, n_turned, n_hf, n_hi, n_lo = (sem("n_" + n) for n in ("xh", "turned", "hf", "hi", "lo"))
                ld_x = [sem(f"ld_x{i}") for i in range(PAIR)]
                stored = [sem(f"stored{t}") for t in range(NP)]

                probs_flat = pe_[:].rearrange("p u k -> p (u k)")[:, 0:TB * D].rearrange("p (t d) -> p t d", d=D)
                BANK_H = [(2, 3, 4, 5), (6, 7, 0, 1)]
                
                def rows(i, t):
                    return probs_flat[:, t, :] if i == 0 else rows_1[:, t, :]

                KQ_JOBS = [j for j in JOBS if j[0] in "KQ"]
                NKQ = len(KQ_JOBS)
                STEP_Q = {u: u + 2 for u in range(UNITS - 2)}
                STEP_W = {UNITS - 2: (0, 1), UNITS - 1: (2, 3)}

                def full(g, name):
                    return NJ * g + (JOB[name] + 2)

                def turned(g, name):
                    return NTJ * g + (TJOB[name] + 1)

                def parted(g, name):
                    return NTJ * g + (TJOB[name] + 3)

                def left(g, j):
                    name = JOBS[j]
                    if j < 0:
                        return acc_done, NP * g + (NP + j + 1)
                    if name[0] == "W":
                        return acc_done, NP * g + (NP + int(name[1:]) + 1)
                    if name[0] == "V":
                        return v_copied, PAIR * g + (int(name[1:]) + 1)
                    return kq_ready, NKQ * g + (KQ_JOBS.index(name) + 1)

                with nc.Block() as block:
                    @block.sync
                    def _(sp):
                        for pair in range(B // PAIR):
                            if pair == 0:
                                load_qkv(sp, 0)
                            with sp.Fori(NKV * pair, NKV * (pair + 1)) as g:
                                sp.wait_ge(wo_split, GQ * g + GQ)
                                sp.dma_start(wo_in[:], wo_v[bass.ds(g % NKV, 1)].rearrange("g p h n -> p (g h) n")).then_inc(wo_ld, 16)
                                sp.wait_ge(qkv_split, NSPL * g + NSPL)
                                load_qkv(sp, (g + 1) % NKV)

                            for t in range(NP):
                                sp.wait_ge(gated, NP * pair + t + 1)
                                sp.dma_start(att_t[PAIR * pair + t // TB][:, t % TB, :], acc[:, t, :]).then_inc(stored[t], 16)
                        for t in range(NP):
                            sp.wait_ge(stored[t], 16 * (B // PAIR))
                    @block.gpsimd
                    def _(pool):
                        HIS = GQ + NSPL
                        nc.gpsimd.memset(mask[:], 0.0).then_inc(masked, 1)
                        pool.wait_ge(masked, 1)
                        nc.gpsimd.affine_select(out=mask[:, (TB - 1) * P:], in_=mask[:, (TB - 1) * P:], compare_op=ALU.is_ge, fill=NEG,
                                                base=0, pattern=[[-1, P]], channel_multiplier=1).then_inc(masked, 1)
                        for t in range(NP):
                            nc.gpsimd.memset(acc[:, t, :], 0.0).then_inc(cleared, 1)
                        pool.wait_ge(cleared, NP)
                        pool.wait_ge(qkv_in, 48)
                        split_qkv(pool, w_hi, 0, lambda n: None)
                        pool.sem_inc(wo_split, GQ)
                        for pair in range(B // PAIR):
                            with pool.Fori(NKV * pair, NKV * (pair + 1)) as g:
                                pool.wait_ge(wo_ld, 16 * g + 16)
                                pool.wait_ge(job_full, NJ * g + 1)
                                for h in range(GQ):
                                    round_part(wo[0][:, h, :], wo_in[:, h, :]).then_inc(w_hi, 1)
                                    pool.wait_ge(w_hi, HIS * g + (NSPL + h + 1))
                                    nc.gpsimd.tensor_tensor(wo[1][:, h, :], wo_in[:, h, :], wo[0][:, h, :].bitcast(F32),
                                                            ALU.subtract).then_inc(wo_split, 1)
                                pool.wait_ge(qkv_in, 48 * g + 48 * 2)
                                last_use = ["K1", "V1"] + [f"Q{u}" for u in range(UNITS - GQ, UNITS)]
                                split_qkv(pool, w_hi, HIS * g + HIS, lambda n: pool.wait_ge(job_full, full(g, last_use[n])))

                            for t in range(NP):
                                pool.wait_ge(acc_done, NP * NKV * (pair + 1) + t + 1)
                                pool.wait_ge(gates_copied, B)
                                nc.gpsimd.tensor_tensor(acc[:, t, :], acc[:, t, :], gate_r[:, PAIR * pair + t // TB, :],
                                                        ALU.mult).then_inc(gated, 1)
                            if pair + 1 < B // PAIR:
                                for t in range(NP):
                                    pool.wait_ge(stored[t], 16 * (pair + 1))
                                    nc.gpsimd.memset(acc[:, t, :], 0.0).then_inc(cleared, 1)

                    @block.tensor
                    def _(pe):
                        pe.sem_inc(job_full, 1)
                        for b in range(B):
                            gate_rows(pe, BANK_H[1][b], 1, MOD_GA, b).then_inc(gates_full, 1)
                        for pair in range(B // PAIR):
                            heads = NKV * pair
                            if pair >= 1:
                                pe.wait_ge(exp_done, UNITS * TB * heads + TB)
                                pe.wait_ge(t_ready, NTJ * heads + 2)
                                pe.wait_ge(o_ready, UNITS * heads + 1)
                            for i in range(PAIR):
                                pe.wait_ge(n_xh, PAIR * pair + i + 1)
                                if i == 1:
                                    if pair == 0:
                                        pe.wait_ge(gates_copied, B)
                                    else:
                                        pe.wait_ge(acc_done, NP * heads + NP)
                                for c in range(DC):
                                    for t in range(TB):
                                        last = nc.tensor.transpose(ps[:, BANK_H[i][c], t * P:(t + 1) * P],
                                                                   rows(i, t)[:, c * P:(c + 1) * P], ident[:])
                                    last.then_inc(n_turned, 1)
                            pe.wait_ge(n_lo, DC * (PAIR * pair + 1))
                            pe.wait_ge(n_hf, DC * (PAIR * pair + 1) + 2)
                            with pe.Fori(NKV * pair, NKV * (pair + 1)) as g:
                                def job_bank(name):
                                    j = JOB[name]
                                    pe.wait_ge(*left(g, j - 2))
                                    return BANK_J + j % 2

                                def project(name, w, cols, b):
                                    bank = job_bank(name)
                                    for c in range(DC):
                                        for n, (i, k) in enumerate(((0, 0), (0, 1), (1, 0))):
                                            last = nc.tensor.matmul(ps[:, bank, :], w[i][:, c, cols],
                                                                    hT[k][:, c, b * S:(b + 1) * S],
                                                                    start=(c == 0 and n == 0), stop=(c == DC - 1 and n == 2))
                                    last.then_inc(job_full, 1)
                                    return last

                                def q_project(u):
                                    h = u % GQ
                                    project(f"Q{u}", wq, slice(h * HD, (h + 1) * HD), u // GQ)

                                def turn_bank(name):
                                    j = TJOB[name]
                                    pe.wait_ge(t_ready, NTJ * g + (j + 1))
                                    return BANK_T + j % 2

                                def turn_v(b):
                                    bank = turn_bank(f"V{b}")
                                    pe.wait_ge(v_copied, PAIR * g + (b + 1))
                                    for t in range(TB):
                                        last = nc.tensor.transpose(ps[:, bank, t * P:(t + 1) * P], vT[:, t * P:(t + 1) * P], ident[:])
                                    last.then_inc(t_full, 1)

                                def scores(u):
                                    b = u // GQ
                                    pe.wait_ge(kq_ready, NKQ * g + (KQ_JOBS.index(f"Q{u}") + 1))
                                    for n, (i, bank, col) in enumerate(SC):
                                        if n < 3:
                                            pe.wait_ge(exp_done, UNITS * TB * g + (TB * u + (1, 2, 4)[n]))
                                        dst = ps[:, BANK_S + bank, col:col + KEYS[i]]
                                        if i == 0:
                                            last = nc.tensor.matmul(dst, q_first[:, u % 2, :], k_first[:, b, :],
                                                                    start=True, stop=True)
                                        else:
                                            for k, (x_, y_) in enumerate(((0, 0), (0, 1), (1, 0))):
                                                last = nc.tensor.matmul(dst, qT[x_][:, u % 2, (i - 1) * P:i * P],
                                                                        kT[y_][:, b, 0:KEYS[i]], start=(k == 0), stop=(k == 2))
                                        last.then_inc(s_full, 1)

                                def turn(u, k):
                                    if k == 0:
                                        pe.wait_ge(p_ready, UNITS * TB * g + TB * (u + 1))
                                    bank = turn_bank(f"{u}.{k}")
                                    blocks = ([(i, 0) for i in range(4)], [(3, 3), (1, 1), (2, 1), (3, 1)], [(2, 2), (3, 2)])[k]
                                    for n, (i, kt) in enumerate(blocks):
                                        last = nc.tensor.transpose(ps[:, bank, n * P:(n + 1) * P],
                                                                   pe_[:, u % 2, PO[i] + kt * P:PO[i] + (kt + 1) * P], ident[:])
                                    last.then_inc(t_full, 1)

                                def outputs(u):
                                    b = u // GQ
                                    if u % GQ == 0:
                                        pe.wait_ge(t_ready, parted(g, f"V{b}"))
                                    pe.wait_ge(o_ready, UNITS * g + (u + 1))
                                    for n, (col, N, q0, kt) in enumerate(PVS):
                                        pe.wait_ge(t_ready, parted(g, f"{u}.{n}"))
                                        for k, (x_, y_) in enumerate(((0, 0), (1, 0), (0, 1))):
                                            last = nc.tensor.matmul(ps[:, BANK_V, q0:q0 + N], V[x_][:, b, kt, :],
                                                                    pt[y_][:, col:col + N], start=(n == 0 and k == 0), stop=(n == 2 and k == 2))
                                        if n == 1:
                                            nc.tensor.matmul(ps[:, BANK_V, 3 * P:], v_last[:, b, :], pt_last[:],
                                                             start=False, stop=False)
                                    last.then_inc(o_full, 1)

                                def out_project(t):
                                    bank = job_bank(f"W{t}")
                                    b, r = t // TB, t % TB
                                    if t == 0:
                                        pe.wait_ge(wo_split, GQ * g + GQ * 2)
                                    for h in range(GQ):
                                        if r == 0:
                                            pe.wait_ge(o_ready, UNITS * g + (GQ * b + h + 2))
                                        for n, (x_, y_) in enumerate(((0, 0), (1, 0), (0, 1))):
                                            last = nc.tensor.matmul(ps[:, bank, :], oT[x_][:, b, h, r * P:(r + 1) * P], wo[y_][:, h, :],
                                                                    start=(h == 0 and n == 0), stop=(h == GQ - 1 and n == 2))
                                    last.then_inc(job_full, 1)

                                def split_done(n):
                                    pe.wait_ge(qkv_split, NSPL * g + n)

                                split_done(2)
                                project("V0", wv, slice(0, HD), 0)
                                project("K0", wk, slice(0, HD), 0)
                                split_done(3)
                                q_project(0)
                                turn_v(0)
                                pe.wait_ge(n_lo, DC * PAIR * (pair + 1))
                                project("K1", wk, slice(0, HD), 1)
                                scores(0)
                                split_done(4)
                                q_project(1)
                                project("V1", wv, slice(0, HD), 1)
                                for u in range(UNITS):
                                    if u + 1 < UNITS:
                                        scores(u + 1)
                                    turn(u, 0)
                                    turn(u, 1)
                                    if u in STEP_Q:
                                        if STEP_Q[u] < GQ:
                                            split_done(3 + STEP_Q[u])
                                        q_project(STEP_Q[u])
                                    for t in STEP_W.get(u, ())[0:1]:
                                        out_project(t)
                                    turn(u, 2)
                                    for t in STEP_W.get(u, ())[1:2]:
                                        out_project(t)
                                    outputs(u)
                                    if u == 0:
                                        turn_v(1)
                                for t in range(TB, NP):
                                    out_project(t)

                    @block.scalar
                    def _(act):
                        def load_rows(pair):
                            nc.scalar.dma_start(probs_flat, mid_t[PAIR * pair]).then_inc(ld_x[0], 16)
                            nc.scalar.dma_start(rows_1[:], mid_t[PAIR * pair + 1]).then_inc(ld_x[1], 16)

                        act.sem_inc(exp_done, TB)
                        load_rows(0)
                        for b in range(B):
                            act.wait_ge(gates_full, b + 1)
                            nc.scalar.activation(gate_r[:, b, :], ps[:, BANK_H[1][b], :], ACT.Copy).then_inc(gates_copied, 1)
                        for pair in range(B // PAIR):
                            if pair >= 1:
                                act.wait_ge(t_full, NTJ * NKV * pair)
                                load_rows(pair)
                            for i in range(PAIR):
                                for c in range(DC):
                                    act.wait_ge(n_turned, DC * (PAIR * pair + i) + c + 1)
                                    modulate(hf[:, i, c, :], BANK_H[i][c], 1, MOD_CA, MOD_SA, c, PAIR * pair + i).then_inc(n_hf, 1)
                            with act.Fori(NKV * pair, NKV * (pair + 1)) as g:
                                def hi(name, dst, first, scale=1.0):
                                    j = JOB[name]
                                    act.wait_ge(job_full, full(g, JOBS[j]))
                                    bank = ps[:, BANK_J + j % 2, :]
                                    nc.scalar.activation(first, bank[:, 0:P], ACT.Copy, scale=scale)
                                    nc.scalar.activation(dst, bank[:, S - dst.shape[-1]:], ACT.Copy, scale=scale).then_inc(job_hi, 1)

                                def v_copy(b):
                                    j = JOB[f"V{b}"]
                                    act.wait_ge(job_full, full(g, JOBS[j]))
                                    nc.scalar.activation(vT[:], ps[:, BANK_J + j % 2, :], ACT.Copy).then_inc(v_copied, 1)

                                def exps(u):
                                    for n, (i, bank, col) in enumerate(SC):
                                        if n < 3:
                                            act.wait_ge(max_done, UNITS * TB * g + (TB * u + (1, 2, 4)[n]))
                                        nc.scalar.activation(pe_[:, u % 2, PO[i]:PO[i] + KEYS[i]], ps[:, BANK_S + bank, col:col + KEYS[i]],
                                                             ACT.Exp, bias=nmax[:, u % 2, i:i + 1], scale=-1.0,
                                                             accum_out=rsum[:, u % 2, i:i + 1]).then_inc(exp_done, 1)

                                def turned_hi(name, dst, col, single=None, single_col=0):
                                    act.wait_ge(t_full, turned(g, name))
                                    bank = ps[:, BANK_T + TJOB[name] % 2, :]
                                    if single is not None:
                                        nc.scalar.activation(single, bank[:, single_col:single_col + P], ACT.Copy)
                                    nc.scalar.activation(dst, bank[:, col:col + dst.shape[-1]], ACT.Copy).then_inc(t_hi, 1)

                                def t_part(u, k):
                                    first, N, _, _ = PVS[k]
                                    dst = pt[0][:, first:first + N]
                                    if k == 1:
                                        turned_hi(f"{u}.{k}", dst, P, pt_last[:])
                                    else:
                                        turned_hi(f"{u}.{k}", dst, 0)

                                def v_part(b):
                                    turned_hi(f"V{b}", V[0][:, b].rearrange("p t d -> p (t d)"), 0, v_last[:, b, :], (TB - 1) * P)

                                hi_q = lambda u: hi(f"Q{u}", qT[0][:, u % 2, :], q_first[:, u % 2, :], QSCALE)
                                v_copy(0)
                                hi("K0", kT[0][:, 0, :], k_first[:, 0, :])
                                hi_q(0)
                                v_part(0)
                                hi("K1", kT[0][:, 1, :], k_first[:, 1, :])
                                exps(0)
                                hi_q(1)
                                v_copy(1)
                                for u in range(UNITS):
                                    if u + 1 < UNITS:
                                        exps(u + 1)
                                    t_part(u, 0)
                                    t_part(u, 1)
                                    if u in STEP_Q:
                                        hi_q(STEP_Q[u])
                                    t_part(u, 2)
                                    act.wait_ge(o_full, UNITS * g + (u + 1))
                                    nc.scalar.activation(oT[0][:, u // GQ, u % GQ, :], ps[:, BANK_V, :], ACT.Copy).then_inc(o_hi, 1)
                                    if u == 0:
                                        v_part(1)

                    @block.vector
                    def _(dve):
                        dve.wait_ge(masked, 2)
                        dve.sem_inc(t_ready, 2)
                        dve.sem_inc(o_ready, 1)
                        dve.sem_inc(acc_done, NP)
                        for pair in range(B // PAIR):
                            for i in range(PAIR):
                                dve.wait_ge(ld_x[i], 16 * (pair + 1))
                                for t in range(TB):
                                    n = (PAIR * pair + i) * TB + t
                                    last = nc.vector.tensor_scalar(rows(i, t), rows(i, t), mv_2[:, n, 0:1], rstd_2[:, n:n + 1],
                                                                   ALU.subtract, ALU.mult)
                                last.then_inc(n_xh, 1)
                            for i in range(PAIR):
                                for c in range(DC + 1):
                                    n = DC * (PAIR * pair + i) + c
                                    if c < DC:
                                        dve.wait_ge(n_hf, n + 1)
                                        nc.vector.tensor_copy(hT[0][:, c, i * S:(i + 1) * S], hf[:, i, c, :]).then_inc(n_hi, 1)
                                    if c >= 1:
                                        dve.wait_ge(n_hi, n)
                                        nc.vector.tensor_tensor(hT[1][:, c - 1, i * S:(i + 1) * S], hf[:, i, c - 1, :],
                                                                hT[0][:, c - 1, i * S:(i + 1) * S].bitcast(F32),
                                                                ALU.subtract).then_inc(n_lo, 1)
                            with dve.Fori(NKV * pair, NKV * (pair + 1)) as g:
                                def lo(name, dst, hi_part, done, scale=1.0):
                                    j = JOB[name]
                                    dve.wait_ge(job_hi, NKQ * g + (KQ_JOBS.index(name) + 1))
                                    nc.vector.scalar_tensor_tensor(dst, ps[:, BANK_J + j % 2, S - dst.shape[-1]:], scale, hi_part.bitcast(F32),
                                                                   ALU.mult, ALU.subtract).then_inc(done, 1)

                                def lo_kq(name, dst, hi_part, scale=1.0):
                                    lo(name, dst, hi_part, kq_ready, scale)

                                def lo_q(u):
                                    lo_kq(f"Q{u}", qT[1][:, u % 2, :], qT[0][:, u % 2, :], QSCALE)

                                def maxima(u):
                                    for n, (i, bank, col) in enumerate(SC):
                                        if n < 3:
                                            dve.wait_ge(s_full, UNITS * TB * g + (TB * u + (1, 2, 4)[n]))
                                            dve.sem_inc(waits_seen, 1)
                                        v = ps[:, BANK_S + bank, col:col + KEYS[i]]
                                        nc.vector.tensor_tensor_reduce(out=v, in0=v, in1=mask[:, TB * P - KEYS[i]:], scale=-1.0,
                                                                       scalar=3e38, op0=ALU.add, op1=ALU.min,
                                                                       accum_out=nmax[:, u % 2, i:i + 1]).then_inc(max_done, 1)

                                def scale_rows(u):
                                    dve.wait_ge(exp_done, UNITS * TB * g + (TB * (u + 1) + TB))
                                    nc.vector.reciprocal(rinv[:, u % 2, :], rsum[:, u % 2, :]).then_inc(rinv_done, 1)
                                    dve.wait_ge(rinv_done, UNITS * g + (u + 1))
                                    for i in range(TB):
                                        v = pe_[:, u % 2, PO[i]:PO[i] + KEYS[i]]
                                        nc.vector.tensor_scalar(v, v, rinv[:, u % 2, i:i + 1], None, ALU.mult).then_inc(p_ready, 1)

                                def turned_lo(name, dst, hi_part, col):
                                    dve.wait_ge(t_hi, turned(g, name))
                                    nc.vector.tensor_tensor(dst, ps[:, BANK_T + TJOB[name] % 2, col:col + dst.shape[-1]],
                                                            hi_part.bitcast(F32), ALU.subtract).then_inc(t_ready, 1)

                                def t_part(u, k):
                                    first, N, _, _ = PVS[k]
                                    turned_lo(f"{u}.{k}", pt[1][:, first:first + N], pt[0][:, first:first + N], P if k == 1 else 0)

                                def v_part(b):
                                    flat = lambda t: t[:, b].rearrange("p t d -> p (t d)")
                                    turned_lo(f"V{b}", flat(V[1]), flat(V[0]), 0)

                                def add_out(t):
                                    j = JOB[f"W{t}"]
                                    dve.wait_ge(job_full, full(g, JOBS[j]))
                                    nc.vector.tensor_tensor(acc[:, t, :], acc[:, t, :], ps[:, BANK_J + j % 2, :], ALU.add) \
                                        .then_inc(acc_done, 1)

                                lo_kq("K0", kT[1][:, 0, :], kT[0][:, 0, :])
                                lo_q(0)
                                v_part(0)
                                lo_kq("K1", kT[1][:, 1, :], kT[0][:, 1, :])
                                maxima(0)
                                scale_rows(0)
                                lo_q(1)
                                for u in range(UNITS):
                                    if u + 1 < UNITS:
                                        maxima(u + 1)
                                    t_part(u, 0)
                                    t_part(u, 1)
                                    if u in STEP_Q:
                                        lo_q(STEP_Q[u])
                                    for t in STEP_W.get(u, ())[0:1]:
                                        add_out(t)
                                    t_part(u, 2)
                                    if u + 1 < UNITS:
                                        scale_rows(u + 1)
                                    for t in STEP_W.get(u, ())[1:2]:
                                        add_out(t)
                                    dve.wait_ge(o_hi, UNITS * g + (u + 1))
                                    nc.vector.tensor_tensor(oT[1][:, u // GQ, u % GQ, :], ps[:, BANK_V, :],
                                                            oT[0][:, u // GQ, u % GQ, :].bitcast(F32), ALU.subtract) \
                                        .then_inc(o_ready, 1)
                                    if u == 0:
                                        v_part(1)
                                for t in range(TB, NP):
                                    add_out(t)



        f = ExitStack()
        with f:
            gw = sb(f, "gw", [P, DC, F], F32R)
            uw = sb(f, "uw", [P, DC, F], F32R)
            dw = sb(f, "dw", [P, FC, D], F32R)
            gsc = sb(f, "gsc", [P, FC], F32)
            usc = sb(f, "usc", [P, FC], F32)
            dgb = sb(f, "dgb", [P, B, D], F32)
            xt = sb(f, "xt", [P, 2, TB, D], F32)
            at = sb(f, "at", [P, 2, D], F32)
            stats = sb(f, "stats", [P, TB, 6], F32)
            mv = sb(f, "mv", [P, TB, 2], F32)
            std = sb(f, "std", [P, TB], F32)
            xh = sb(f, "xh", [P, TB, D], F32)
            hT = [sb(f, f"hT{i}", [P, DC, S], F32R) for i in range(2)]
            sg = sb(f, "sg", [P, 2, S], F32)
            hid = sb(f, "hid", [P, 2, S], F32)
            with ExitStack() as early:
                at_first = sb(early, "at_first", [P, TB, D], F32)
                dsc = sb(early, "dsc", [P, D], F32)
            hd = [sb(f, f"hd{i}", [P, FC, S], F32R) for i in (1, 0)][::-1]
            WB = 4
            wb = sb(f, "wb", [P, WB, D], BF16)
            hf, yt = sg, hid
            raw = xh[:].bitcast(I32)
            s = {n: sem("m_" + n) for n in ("x3", "stat", "stat_seen", "agg", "var", "std", "rstd", "xh", "turned", "hf", "hi",
                                            "lo", "gate", "up", "sg", "hid", "hhi", "hlo", "down", "yt", "y", "cast",
                                            "w_turned", "prepped", "gates", "dgb", "ld_dsc", "ld_x", "st")}
            ld_s = sem("ld_s")
            ld_raw = [sem(f"ld_raw{k}") for k in range(WB)]
            ld_at = [sem(f"ld_at{k}") for k in range(2)]
            ld_at_first = sem("ld_at_first")
            BANK_T, BANK_W = 4, 5
            J_STAT, J_ROOT = 6, 12
            NW = 3 * FC
            AHEAD = 2
            g_v = gate_wq.rearrange("(j p) i -> j p i", p=P)
            u_v = up_wq.rearrange("(j p) i -> j p i", p=P)
            d_v = down_wq.rearrange("(o p) (j i) -> j p o i", p=P, i=P)

            with nc.Block() as block:
                @block.sync
                def _(sp):
                    sp.dma_start(xt[:, 0], mid_t[0]).then_inc(s["ld_x"], 16)
                    sp.dma_start(at_first[:], att_t[0]).then_inc(ld_at_first, 16)

                    def load_weights(q):
                        if q >= WB:
                            sp.wait_ge(s["cast"], q - WB + 1)
                        j, slot = q // 3, q % WB
                        if q % 3 < 2:
                            sp.dma_start(raw[:, slot, :], (g_v, u_v)[q % 3][j]).then_inc(ld_raw[slot], 16)
                        else:
                            sp.dma_start(raw[:, slot, :].rearrange("p (o i) -> p o i", i=P), d_v[j]).then_inc(ld_raw[slot], 16)

                    for q in range(WB):
                        load_weights(q)
                    sp.dma_start(dsc[:], down_s.rearrange("(o d) -> o d", o=1).to_broadcast([P, D])).then_inc(s["ld_dsc"], 16)
                    with nc.allow_non_contiguous_dma("scales with the hidden width on partitions"):
                        sp.dma_start(gsc[:], gate_s.rearrange("(j p) -> p j", p=P)).then_inc(ld_s, 16)
                        sp.dma_start(usc[:], up_s.rearrange("(j p) -> p j", p=P)).then_inc(ld_s, 16)
                    for q in range(WB, NW // 3):
                        load_weights(q)
                    sp.wait_ge(s["turned"], DC)
                    sp.dma_start(xt[:, 1], mid_t[1]).then_inc(s["ld_x"], 16)
                    for t in range(TB):
                        sp.wait_ge(s["x3"], TB + t - 1)
                        sp.dma_start(at[:, t % 2, :], att_t[1][:, t, :]).then_inc(ld_at[t % 2], 16)
                    for q in range(NW // 3, NW):
                        load_weights(q)
                    for t in range(TB):
                        sp.wait_ge(s["y"], t + 1)
                        sp.dma_start(out_t[0][:, t, :], xt[:, 0, t, :]).then_inc(s["st"], 16)
                    with sp.Fori(1, B) as n:
                        nxt = (n + 1) % B
                        sp.wait_ge(s["st"], 16 * TB * n)
                        sp.dma_start(xt[:, bass.ds((n + 1) % 2, 1)].rearrange("p k t d -> p (k t) d"),
                                     mid_t[bass.ds(nxt, 1)].rearrange("b p t d -> p (b t) d")).then_inc(s["ld_x"], 16)
                        for t in range(TB):
                            sp.wait_ge(s["x3"], TB * n + (TB + t - 1))
                            sp.dma_start(at[:, t % 2, :], att_t[bass.ds(nxt, 1), :, t, :].rearrange("b p d -> p (b d)")) \
                                .then_inc(ld_at[t % 2], 16)
                        for t in range(TB):
                            sp.wait_ge(s["y"], TB * n + (t + 1))
                            sp.dma_start(out_t[bass.ds(n, 1), :, t, :].rearrange("b p d -> p (b d)"),
                                         xt[:, bass.ds(n % 2, 1), t, :].rearrange("p k d -> p (k d)")).then_inc(s["st"], 16)
                    sp.wait_ge(s["st"], 16 * TB * B)

                @block.gpsimd
                def _(pool):
                    def add_attention(n, slot):
                        for t in range(TB):
                            pool.wait_ge(s["ld_x"], 16 * n + 32)
                            pool.wait_ge(ld_at[t % 2], 32 * n + 16 * (t // 2 + 1))
                            pool.sem_inc(waits_seen, 1)
                            x_ = xt[:, slot, t, :].rearrange("p k d -> p (k d)")
                            nc.gpsimd.tensor_tensor(x_, x_, at[:, t % 2, :], ALU.add).then_inc(s["x3"], 1)

                    add_attention(0, slice(1, 2))
                    with pool.Fori(1, B) as n:
                        add_attention(n, bass.ds((n + 1) % 2, 1))

                @block.scalar
                def _(act):
                    def cast(q):
                        act.wait_ge(ld_raw[q % WB], 16 * (q // WB + 1))
                        if q >= WB:
                            act.wait_ge(s["w_turned"], q - WB + 1)
                        nc.scalar.activation(wb[:, q % WB, :], raw[:, q % WB, :], ACT.Copy).then_inc(s["cast"], 1)

                    def root(r):
                        act.wait_ge(s["var"], r + 1)
                        nc.scalar.activation(std[:], mv[:, :, 1], ACT.Sqrt).then_inc(s["std"], 1)

                    def modulated(r, b):
                        for c in range(DC):
                            act.wait_ge(s["turned"], DC * r + (c + 1))
                            act.wait_ge(s["lo"], DC * r + (c + 1))
                            bias = mod[1][:, DC * MOD_SB + c, bass.ds(b, 1)]
                            scale = mod[1][:, DC * MOD_CB + c, bass.ds(b, 1)]
                            for dst, done in ((hf[:, c % 2, :], "hf"), (hT[0][:, c, :], "hi")):
                                nc.scalar.activation(dst, ps[:, BANK_T + c, :], ACT.Identity, bias=bias, scale=scale) \
                                    .then_inc(s[done], 1)

                    def batch(n, first):
                        for j in range(FC):
                            act.wait_ge(s["gate"], FC * n + (j + 1))
                            act.wait_ge(s["hid"], FC * n + (j + 1))
                            nc.scalar.activation(sg[:, j % 2, :], ps[:, 2 * (j % 2), :], ACT.Silu,
                                                 scale=gsc[:, j:j + 1]).then_inc(s["sg"], 1)
                            if first and j + AHEAD < FC:
                                for q in range(3 * (j + AHEAD), 3 * (j + AHEAD) + 3):
                                    cast(q)
                            act.wait_ge(s["hid"], FC * n + (j + 3))
                            nc.scalar.activation(hd[0][:, j, :], hid[:, j % 2, :], ACT.Copy).then_inc(s["hhi"], 1)
                            if j == J_ROOT:
                                root(n + 1)
                        modulated(n + 1, (n + 1) % B)

                    act.sem_inc(s["hi"], DC)
                    for q in range(WB):
                        cast(q)
                    root(0)
                    for q in range(WB, 3 * AHEAD):
                        cast(q)
                    modulated(0, 0)
                    batch(0, True)
                    with act.Fori(1, B) as n:
                        batch(n, False)

                @block.vector
                def _(dve):
                    def statistics(r, tile, t):
                        dve.wait_ge(s["x3"], TB * r + (t + 1))
                        nc.vector.bn_stats(stats[:, t, :], tile).then_inc(s["stat"], 1)

                    def variances(r):
                        dve.wait_ge(s["stat"], TB * r + TB)
                        dve.sem_inc(s["stat_seen"], 1)
                        for t in range(TB):
                            last = nc.vector.bn_aggr(mv[:, t, :], stats[:, t, :])
                        last.then_inc(s["agg"], 1)
                        dve.wait_ge(s["agg"], r + 1)
                        nc.vector.tensor_scalar(mv[:, :, 1], mv[:, :, 1], EPS, None, ALU.add).then_inc(s["var"], 1)

                    def normal(r, tiles, dst):
                        dve.wait_ge(s["std"], r + 1)
                        nc.vector.reciprocal(std[:], std[:]).then_inc(s["rstd"], 1)
                        dve.wait_ge(s["rstd"], r + 1)
                        for t in range(TB):
                            nc.vector.tensor_scalar(dst[:, t, :], tiles(t), mv[:, t, 0:1], std[:, t:t + 1],
                                                    ALU.subtract, ALU.mult).then_inc(s["xh"], 1)

                    def lows(r):
                        for c in range(DC):
                            dve.wait_ge(s["hi"], DC * r + (DC + c + 1))
                            nc.vector.tensor_tensor(hT[1][:, c, :], hf[:, c % 2, :], hT[0][:, c, :].bitcast(F32),
                                                    ALU.subtract).then_inc(s["lo"], 1)

                    def prepare(q):
                        j = q // 3
                        dve.wait_ge(s["w_turned"], q + 1)
                        bank = ps[:, BANK_W + q % 3, 0:D // 2].bitcast(BF16)
                        if q % 3 < 2:
                            nc.vector.tensor_copy((gw, uw)[q % 3][:, :, j * P:(j + 1) * P],
                                                  bank.rearrange("p (c o) -> p c o", c=DC)).then_inc(s["prepped"], 1)
                        else:
                            nc.vector.tensor_copy(dw[:, j, :], bank).then_inc(s["prepped"], 1)

                    def batch(n, first, here, other):
                        for j in range(FC):
                            q = FC * n + j
                            dve.wait_ge(s["up"], q + 1)
                            dve.wait_ge(s["sg"], q + 1)
                            dve.wait_ge(s["hlo"], q + 1)
                            nc.vector.scalar_tensor_tensor(hid[:, j % 2, :], ps[:, 2 * (j % 2) + 1, :], usc[:, j:j + 1],
                                                           sg[:, j % 2, :], ALU.mult, ALU.mult).then_inc(s["hid"], 1)
                            if first and j + AHEAD < FC:
                                for w in range(3 * (j + AHEAD), 3 * (j + AHEAD) + 3):
                                    prepare(w)
                            dve.wait_ge(s["hhi"], q + 1)
                            nc.vector.tensor_tensor(hd[1][:, j, :], hid[:, j % 2, :], hd[0][:, j, :].bitcast(F32),
                                                    ALU.subtract).then_inc(s["hlo"], 1)
                            if J_STAT <= j < J_STAT + TB:
                                statistics(n + 1, other(j - J_STAT), j - J_STAT)
                            if j == J_STAT + TB:
                                variances(n + 1)
                        normal(n + 1, other, xh)
                        for t in range(TB):
                            q = TB * n + t
                            dve.wait_ge(s["down"], q + 1)
                            gate = dgb[:, bass.ds(n, 1), :].rearrange("p b d -> p (b d)")
                            nc.vector.tensor_tensor(yt[:, t % 2, :], gate, ps[:, t, :], ALU.mult).then_inc(s["yt"], 1)
                            dve.wait_ge(s["yt"], q + 1)
                            nc.vector.tensor_tensor(here(t), here(t), yt[:, t % 2, :], ALU.add).then_inc(s["y"], 1)
                            if t == 0:
                                lows(n + 1)

                    dve.sem_inc(s["hid"], 2)
                    dve.sem_inc(s["lo"], 2)
                    dve.sem_inc(s["hlo"], 1)
                    dve.wait_ge(s["ld_x"], 16)
                    dve.wait_ge(ld_at_first, 16)
                    for t in range(TB + 1):
                        if t < TB:
                            nc.vector.tensor_tensor(xt[:, 0, t, :], xt[:, 0, t, :], at_first[:, t, :], ALU.add).then_inc(s["x3"], 1)
                        if t >= 1:
                            statistics(0, xt[:, 0, t - 1, :], t - 1)
                    variances(0)
                    for q in range(3):
                        prepare(q)
                    normal(0, lambda t: xt[:, 0, t, :], xt[:, 1])
                    lows(0)
                    for q in range(3, 3 * AHEAD):
                        prepare(q)
                    dve.wait_ge(s["ld_dsc"], 16)
                    for b in range(B):
                        dve.wait_ge(s["gates"], b + 1)
                        nc.vector.tensor_tensor(dgb[:, b, :], dsc[:], ps[:, b, :], ALU.mult).then_inc(s["dgb"], 1)
                    dve.wait_ge(ld_s, 32)
                    batch(0, True, lambda t: xt[:, 0, t, :], lambda t: xt[:, 1, t, :])
                    with dve.Fori(1, B) as n:
                        def tile(k):
                            return lambda t: xt[:, bass.ds((n + k) % 2, 1), t, :].rearrange("p k d -> p (k d)")
                        batch(n, False, tile(0), tile(1))

                @block.tensor
                def _(pe):
                    def turn(r, src):
                        pe.wait_ge(s["xh"], TB * r + TB)
                        for c in range(DC):
                            pe.wait_ge(s["hi"], DC * r + (c + 1))
                            turn_chunk(BANK_T + c, src, c).then_inc(s["turned"], 1)

                    def turn_weights(q):
                        pe.wait_ge(s["cast"], q + 1)
                        if q >= 3:
                            pe.wait_ge(s["prepped"], q - 2)
                        bank = ps[:, BANK_W + q % 3, 0:D // 2].bitcast(BF16)
                        for c in range(DC):
                            last = nc.tensor.transpose(bank[:, c * P:(c + 1) * P], wb[:, q % WB, c * P:(c + 1) * P], ident_b[:])
                        last.then_inc(s["w_turned"], 1)

                    def down(n, t):
                        pe.wait_ge(s["hlo"], FC * n + FC)
                        for j in range(FC):
                            if j == FC - 1:
                                pe.wait_ge(s["hlo"], FC * n + (FC + 1))
                            for h in range(2):
                                last = nc.tensor.matmul(ps[:, t, :], hd[h][:, j, t * P:(t + 1) * P], dw[:, j, :],
                                                        start=(j == 0 and h == 0), stop=(j == FC - 1 and h == 1))
                        last.then_inc(s["down"], 1)

                    def batch(n, first):
                        for j in range(FC):
                            if j == 0:
                                pe.wait_ge(s["lo"], DC * n + (DC + 2))
                            if first:
                                pe.wait_ge(s["prepped"], 3 * j + 3)
                                if j < 2:
                                    pe.wait_ge(s["dgb"], 2 * j + 2)
                            elif j < 2:
                                pe.wait_ge(s["y"], TB * n + (2 * j + 2 - TB))
                            pe.wait_ge(s["hid"], FC * n + (j + 1))
                            for w, bank, done in ((gw, 2 * (j % 2), "gate"), (uw, 2 * (j % 2) + 1, "up")):
                                for c in range(DC):
                                    for h in range(2):
                                        last = nc.tensor.matmul(ps[:, bank, :], w[:, c, j * P:(j + 1) * P], hT[h][:, c, :],
                                                                start=(c == 0 and h == 0), stop=(c == DC - 1 and h == 1))
                                last.then_inc(s[done], 1)
                            if first and j + AHEAD < FC:
                                for q in range(3 * (j + AHEAD), 3 * (j + AHEAD) + 3):
                                    turn_weights(q)
                        down(n, 0)
                        if first:
                            pe.wait_ge(s["prepped"], NW)
                        turn(n + 1, xh)
                        for t in range(1, TB):
                            down(n, t)

                    for b in range(B):
                        gate_rows(pe, b, 1, MOD_GB, b).then_inc(s["gates"], 1)
                    for q in range(3):
                        turn_weights(q)
                    pe.wait_ge(s["prepped"], 3)
                    turn(0, xt[:, 1])
                    pe.wait_ge(s["hi"], DC + DC)
                    for q in range(3, 3 * AHEAD):
                        turn_weights(q)
                    batch(0, True)
                    with pe.Fori(1, B) as n:
                        batch(n, False)


_INS = ['L0_attn_x', 'L0_attn_Wq', 'L0_attn_bq', 'L0_attn_Wk', 'L0_attn_bk', 'L0_attn_Wv', 'L0_attn_bv', 'L0_ffn_weight',
        'L0_ffn_bias', 'L0_ffn_centroids', 'L0_ffn_assignments', 'L0_c', 'L0_wmod', 'L1_attn_w_q', 'L1_attn_w_k',
        'L1_attn_w_v', 'L1_attn_w_o', 'L1_ffn_gate_wq', 'L1_ffn_gate_scale', 'L1_ffn_up_wq', 'L1_ffn_up_scale',
        'L1_ffn_down_wq', 'L1_ffn_down_scale', 'L1_c', 'L1_wmod']


def kernel(**inputs):
    import numpy as _np
    import concourse.bacc as _bacc
    from concourse import mybir as _mybir
    from concourse.bass_utils import run_bass_kernel_spmd as _run

    nc = _bacc.Bacc("TRN2", target_bir_lowering=False, num_devices=1)
    arrays, args = {}, []
    for name in _INS:
        a = _np.ascontiguousarray(inputs[name])
        arrays[f"in_{name}_dram"] = a
        args.append(nc.dram_tensor(f"in_{name}_dram", a.shape, _mybir.dt.from_np(a.dtype), kind="ExternalInput").ap())
    x = arrays["in_L0_attn_x_dram"]
    args.append(nc.dram_tensor("out_0_dram", x.shape, _mybir.dt.from_np(x.dtype), kind="ExternalOutput").ap())
    adaln_two_blocks(nc, *args)
    r = _run(nc, [arrays], core_ids=[0])
    return r.results[0]["out_0_dram"]
```

```python
from contextlib import ExitStack

import concourse.bass as bass
from concourse import mybir

ALU = mybir.AluOpType
ACT = mybir.ActivationFunctionType
AX = mybir.AxisListType
F32 = mybir.dt.float32
F32R = mybir.dt.float32r
BF16 = mybir.dt.bfloat16
I32 = mybir.dt.int32

P = 128
EPS = 1e-5
NEG = -1e30
GATE_MIN = 0.25
THRESHOLD = 0.01
TEMPERATURE = 0.1
MOD_SA, MOD_CA, MOD_GA, MOD_SB, MOD_CB, MOD_GB = range(6)


def adaln_two_blocks(nc, x, Wq, bq, Wk, bk, Wv, bv, ffn_w, ffn_b, cent, assign, c0, wmod0,
                     w_q, w_k, w_v, w_o, gate_wq, gate_s, up_wq, up_s, down_wq, down_s, c1, wmod1, out):
    B, S, D = x.shape
    DC = D // P
    TB = S // P
    NT = B * TB
    NM = 6 * D // P
    E0, H0 = Wq.shape[1], Wq.shape[2]
    NCL = cent.shape[0]
    HD = P
    NQ = w_q.shape[1] // HD
    NKV = w_k.shape[1] // HD
    GQ = NQ // NKV
    F = gate_wq.shape[0]
    FC = F // P
    QSCALE = float(HD) ** -0.5
    PAIR = 2
    assert D == 512 and S == 512 and E0 * H0 == D and GQ * HD == D and F % P == 0

    x_t = x.rearrange("b (t p) d -> b p t d", p=P)
    out_t = out.rearrange("b (t p) d -> b p t d", p=P)
    mid = nc.dram_tensor("x_mid", [B, S, D], F32, kind="Internal").ap()
    mid_t = mid.rearrange("b (t p) d -> b p t d", p=P)
    att = nc.dram_tensor("attended", [B, S, D], F32, kind="Internal").ap()
    att_t = att.rearrange("b (t p) d -> b p t d", p=P)

    ctx = ExitStack()
    with ctx:
        names = [0]

        def sb(stack, name, shape, dt):
            names[0] += 1
            return stack.enter_context(nc.sbuf_tensor(f"{name}_{names[0]}", shape, dt))

        def sem(name):
            names[0] += 1
            return ctx.enter_context(nc.semaphore(f"{name}_{names[0]}"))

        ps = ctx.enter_context(nc.psum_tensor("ps", [P, 8, 512], F32))
        ident = sb(ctx, "ident", [P, P], F32)
        ident_b = sb(ctx, "ident_b", [P, P], BF16)
        mod = [sb(ctx, f"mod{layer}", [P, NM, B], F32) for layer in range(2)]

        mv_2 = sb(ctx, "mv_2", [P, NT, 2], F32)
        rstd_2 = sb(ctx, "rstd_2", [P, NT], F32)

        def gate_rows(pe, bank, layer, which, b):
            for c in range(DC):
                col = mod[layer][:, DC * which + c, b:b + 1].to_broadcast([P, P])
                last = nc.tensor.transpose(ps[:, bank, c * P:(c + 1) * P], col, ident[:])
            return last

        def mods_finish(link, layer, turned_mods, first, end, tmp):
            m = mod[layer]
            span = slice(DC * first, DC * end)
            link(nc.vector.tensor_copy(m[:, span, :], turned_mods.rearrange("p (n b) -> p n b", b=B)[:, span, :]))
            for which in range(first, end):
                v = m[:, DC * which:DC * which + DC, :]
                if which in (MOD_CA, MOD_CB):
                    link(nc.vector.tensor_scalar(v, v, 1.0, None, ALU.add))
                if which in (MOD_GA, MOD_GB):
                    link(nc.vector.tensor_scalar(tmp[:, 0], v, 0.0, 2.0, ALU.is_ge, ALU.mult))
                    link(nc.vector.tensor_scalar(tmp[:, 0], tmp[:, 0], 1.0, None, ALU.subtract))
                    link(nc.vector.scalar_tensor_tensor(tmp[:, 1], v, -1.0, v, ALU.mult, ALU.max))
                    link(nc.vector.scalar_tensor_tensor(v, tmp[:, 1], GATE_MIN, tmp[:, 0], ALU.max, ALU.mult))

        def tile_stats(link, xt, stats, mv):
            for t in range(TB):
                last = nc.vector.bn_stats(stats[:, t, :], xt[:, t, :])
            link(last)
            for t in range(TB):
                last = nc.vector.bn_aggr(mv[:, t, :], stats[:, t, :])
            link(last)
            return nc.vector.tensor_scalar(mv[:, :, 1], mv[:, :, 1], EPS, None, ALU.add)

        def normalise(link, xt, mv, std, xh):
            link(nc.vector.reciprocal(std[:], std[:]))
            for t in range(TB):
                last = nc.vector.tensor_scalar(xh[:, t, :], xt[:, t, :], mv[:, t, 0:1], std[:, t:t + 1],
                                               ALU.subtract, ALU.mult)
            return last

        def turn_chunk(bank, xh, c):
            for t in range(TB):
                last = nc.tensor.transpose(ps[:, bank, t * P:(t + 1) * P], xh[:, t, c * P:(c + 1) * P], ident[:])
            return last

        def modulate(dst, bank, layer, scale, shift, c, b):
            return nc.scalar.activation(dst, ps[:, bank, :], ACT.Identity,
                                        bias=mod[layer][:, DC * shift + c, b:b + 1],
                                        scale=mod[layer][:, DC * scale + c, b:b + 1])

        WB = 4
        wb = sb(ctx, "wb", [P, WB, D], BF16)
        with ExitStack() as early:
            wm1_a = sb(early, "wm1_a", [P, DC, 4 * D], F32)
        with ExitStack() as late:
            xt = sb(late, "xt", [P, 2, TB, D], F32)
            xh_m = sb(late, "xh_m", [P, TB, D], F32)
            at_first = sb(late, "at_first", [P, TB, D], F32)
        raw = xh_m[:].bitcast(I32)
        second = ctx.enter_context(ExitStack())
        hA = [sb(second, f"hA{i}", [P, DC, PAIR * S], F32R) for i in range(2)]
        wk_in = sb(second, "wk_in", [P, DC, HD], F32)
        wv_in = sb(second, "wv_in", [P, DC, HD], F32)

        kv_in, q_in = sem("kv_in"), sem("q_in")
        ld_raw = [sem(f"ld_raw{k}") for k in range(WB)]
        ld_xm, ld_at_first, cast_done = sem("ld_xm"), sem("ld_at_first"), sem("cast_done")
        g_v = gate_wq.rearrange("(j p) i -> j p i", p=P)
        u_v = up_wq.rearrange("(j p) i -> j p i", p=P)
        d_v = down_wq.rearrange("(o p) (j i) -> j p o i", p=P, i=P)

        def load_weights(dma, q):
            j, slot = q // 3, q % WB
            if q % 3 < 2:
                dma(raw[:, slot, :], (g_v, u_v)[q % 3][j]).then_inc(ld_raw[slot], 16)
            else:
                dma(raw[:, slot, :].rearrange("p (o i) -> p o i", i=P), d_v[j]).then_inc(ld_raw[slot], 16)

        def cast_weights(act, q):
            act.wait_ge(ld_raw[q % WB], 16 * (q // WB + 1))
            nc.scalar.activation(wb[:, q % WB, :], raw[:, q % WB, :], ACT.Copy).then_inc(cast_done, 1)

        wk_v = w_k.rearrange("(c p) n -> p c n", p=P)
        wv_v = w_v.rearrange("(c p) n -> p c n", p=P)

        def load_kv(sp, g):
            sp.dma_start(wk_in[:], wk_v[:, :, bass.ts(g, HD)]).then_inc(kv_in, 16)
            sp.dma_start(wv_in[:], wv_v[:, :, bass.ts(g, HD)]).then_inc(kv_in, 16)

        l0 = ExitStack()
        with l0:
            X = sb(l0, "X", [P, NT, D], F32)
            w_in = sb(l0, "w_in", [P, DC, D], F32)
            cen_in = sb(l0, "cen_in", [NCL, D], F32)
            bias_r = sb(l0, "bias_r", [P, D], F32)
            asg = sb(l0, "asg", [NCL, D], I32)
            ld_ffn = sem("ld_ffn")
            MODS = [(layer, v) for layer in range(2) for v in range(6)]
            MODS_EARLY = 8
            ld_wm = [sem(f"ld_wm{k}") for k in range(len(MODS) // 2)]
            rows_full, rows_copied, mods_ps = (sem(n) for n in ("rows_full", "rows_copied", "mods_ps"))
            cT = sb(l0, "cT", [P, 2, DC, B], F32)
            mrow = sb(l0, "mrow", [B, 2, D], F32)
            tmp_g = sb(l0, "tmp_g", [P, 2, DC, B], F32)

            def make_mod(pe, m, banks, wm):
                pe.wait_ge(ld_wm[m // 2], 16)
                if m >= 2:
                    pe.wait_ge(rows_copied, m - 1)
                for k in range(DC):
                    last = nc.tensor.matmul(ps[0:B, banks + m % 2, :], cT[:, MODS[m][0], k, :], wm[:, k, :],
                                            start=(k == 0), stop=(k == DC - 1))
                last.then_inc(rows_full, 1)

            def copy_mod(act, m, banks):
                act.wait_ge(rows_full, m + 1)
                if m >= 2:
                    act.wait_ge(mods_ps, m - 1)
                nc.scalar.activation(mrow[:, m % 2, :], ps[0:B, banks + m % 2, :], ACT.Copy).then_inc(rows_copied, 1)

            def turn_mod(pe, m, turned):
                pe.wait_ge(rows_copied, m + 1)
                for c in range(DC):
                    k = (MODS[m][1] * DC + c) * B
                    last = nc.tensor.transpose(turned[:, k:k + B], mrow[:, m % 2, c * P:(c + 1) * P], ident[0:B, 0:B])
                last.then_inc(mods_ps, 1)


            a = ExitStack()
            with a:
                wm0 = sb(a, "wm0", [P, DC, 6 * D], F32)
                wm1_b = sb(a, "wm1_b", [P, DC, 2 * D], F32)
                c_in = sb(a, "c_in", [B, 2, D], F32)
                wq_in = sb(a, "wq_in", [P, DC, D], F32)
                wcat = sb(a, "wcat", [P, DC, 3 * E0], F32)
                bq_in = sb(a, "bq_in", [P, D], F32)
                bcat = sb(a, "bcat", [P, 3 * E0], F32)
                stats = sb(a, "stats", [P, TB, 6], F32)
                mv = sb(a, "mv", [P, TB, 2], F32)
                std = sb(a, "std", [P, TB], F32)
                xh = sb(a, "xh", [P, TB, D], F32)
                hT = sb(a, "hT", [P, DC, S], F32)
                qkv = sb(a, "qkv", [P, TB, 3 * E0], F32)
                sc = sb(a, "sc", [P, TB, E0 * E0], F32)
                ex = sb(a, "ex", [P, TB, E0 * E0], F32)
                red = sb(a, "red", [P, 4, TB * E0], F32)
                upd = sb(a, "upd", [P, TB, D], F32)
                ld_c, ld_w, ld_b = (sem(n) for n in ("ld_c", "ld_w", "ld_b"))

                ld_x = [sem(f"ld_x{b}") for b in range(B)]
                consts, silu_done, ct_turned, ct_copied = (sem(n) for n in ("consts", "silu", "ct_turned", "ct_copied"))
                mods_done, chain = sem("mods_done"), sem("chain")
                var_done, std_done, xh_done, turned, hT_done = (sem(n) for n in ("var", "std", "xh", "turned", "hT"))
                projected, logits, ex_done, upd_done, wcat_done = (sem(n) for n in ("projected", "logits", "ex", "upd", "wcat"))
                gates_ps, gates_copied, o_done, x1_done = (sem(n) for n in ("gates_ps", "gates_copied", "o", "x1"))
                last_upd = sem("last_upd")
                gates_sb = sb(a, "gates_sb", [P, D], F32)
                o_t = sb(a, "o_t", [P, 2, TB * E0], F32)
                LAST_VECTOR = TB // 2

                def gated(t, b):
                    by_head = lambda v: v.rearrange("p (d h) -> p d h", h=H0)
                    o = o_t[:, b % 2, t * E0:(t + 1) * E0].rearrange("p (d o) -> p d o", o=1).to_broadcast([P, E0, H0])
                    return by_head(upd[:, t, :]), by_head(gates_sb[:]), o

                BANK_R, BANK_T, BANK_P, BANK_G = 0, 2, 6, 7
                turned_mods = [ps[:, BANK_P, TB * 3 * E0 + k * NM * B:TB * 3 * E0 + (k + 1) * NM * B] for k in range(2)]
                at_c = TB * 3 * E0 + 2 * NM * B
                turned_c = ps[:, BANK_P, at_c:at_c + 2 * DC * B]
                MODS_BEHIND = {0: range(3, 5), 1: range(5, 7), 2: range(7, 8), 3: ()}

                with nc.Block() as block:
                    @block.sync
                    def _(sp):
                        for layer, c in enumerate((c0, c1)):
                            sp.dma_start(c_in[:, layer, :], c).then_inc(ld_c, 16)
                        sp.dma_start(X[:, 0:TB, :], x_t[0]).then_inc(ld_x[0], 16)
                        def load_wm(dst, src, k, done):
                            cols = slice(2 * D * k, 2 * D * (k + 1))
                            sp.dma_start(dst, src.rearrange("(c p) n -> p c n", p=P)[:, :, cols]).then_inc(done, 16)

                        load_wm(wm0[:, :, 0:2 * D], wmod0, 0, ld_wm[0])
                        sp.dma_start(wq_in[:], Wq.rearrange("(c p) e h -> p c (e h)", p=P)).then_inc(ld_w, 16)
                        sp.dma_start(wcat[:, :, E0:2 * E0], Wk.rearrange("(c p) e o -> p c (e o)", p=P)).then_inc(ld_w, 16)
                        sp.dma_start(wcat[:, :, 2 * E0:3 * E0], Wv.rearrange("(c p) e o -> p c (e o)", p=P)).then_inc(ld_w, 16)
                        sp.dma_start(bq_in[:], bq.rearrange("(o e) h -> o (e h)", o=1).to_broadcast([P, D])).then_inc(ld_b, 16)
                        sp.dma_start(bcat[:, E0:2 * E0], bk.rearrange("e o -> o e").to_broadcast([P, E0])).then_inc(ld_b, 16)
                        sp.dma_start(bcat[:, 2 * E0:3 * E0], bv.rearrange("e o -> o e").to_broadcast([P, E0])).then_inc(ld_b, 16)
                        for b in range(1, B):
                            sp.dma_start(X[:, b * TB:(b + 1) * TB, :], x_t[b]).then_inc(ld_x[b], 16)
                            if b < 3:
                                load_wm(wm0[:, :, 2 * D * b:2 * D * (b + 1)], wmod0, b, ld_wm[b])
                        for k in range(3):
                            load_wm(wm1_b[:] if k == 0 else wm1_a[:, :, 2 * D * (k - 1):2 * D * k], wmod1, k, ld_wm[3 + k])
                        sp.dma_start(cen_in[:], cent).then_inc(ld_ffn, 16)
                        sp.dma_start(w_in[:], ffn_w.rearrange("(c p) i -> p c i", p=P)).then_inc(ld_ffn, 16)
                        sp.dma_start(bias_r[:], ffn_b.rearrange("(o d) -> o d", o=1).to_broadcast([P, D])).then_inc(ld_ffn, 16)
                        sp.dma_start(asg[:], assign.rearrange("(o d) -> o d", o=1).to_broadcast([NCL, D])).then_inc(ld_ffn, 16)
                        load_kv(sp, 0)
                        sp.wait_ge(ld_ffn, 64)
                        sp.wait_ge(kv_in, 32)

                    @block.gpsimd
                    def _(pool):
                        nc.gpsimd.memset(ident[:], 0.0).then_inc(consts, 1)
                        pool.wait_ge(consts, 1)
                        nc.gpsimd.affine_select(out=ident[:], in_=ident[:], compare_op=ALU.not_equal, fill=1.0,
                                                base=0, pattern=[[-1, P]], channel_multiplier=1).then_inc(consts, 1)
                        pool.wait_ge(consts, 2)
                        nc.gpsimd.tensor_copy(ident_b[:], ident[:]).then_inc(consts, 1)
                        for b in range(B):
                            pool.wait_ge(o_done, b + 1)
                            pool.wait_ge(gates_copied, b + 1)
                            tiles = range(LAST_VECTOR if b == B - 1 else 0, TB)
                            for t in tiles:
                                last = nc.gpsimd.tensor_tensor(*gated(t, b), ALU.mult)
                            last.then_inc(upd_done, 1)
                            pool.wait_ge(upd_done, b + 1)
                            for t in tiles:
                                x_ = X[:, b * TB + t, :]
                                last = nc.gpsimd.tensor_tensor(x_, x_, upd[:, t, :], ALU.add)
                            last.then_inc(x1_done, 1)

                    @block.scalar
                    def _(act):
                        act.wait_ge(ld_c, 32)
                        nc.scalar.activation(c_in[:], c_in[:], ACT.Silu).then_inc(silu_done, 1)
                        act.wait_ge(ct_turned, 1)
                        nc.scalar.activation(cT[:], turned_c.rearrange("p (l c b) -> p l c b", l=2, b=B), ACT.Copy).then_inc(ct_copied, 1)

                        def root(b):
                            act.wait_ge(var_done, b + 1)
                            nc.scalar.activation(std[:], mv[:, :, 1], ACT.Sqrt).then_inc(std_done, 1)

                        def transposed(b):
                            if b == 0:
                                act.wait_ge(mods_done, 1)
                            else:
                                act.wait_ge(projected, b)
                            for c in range(DC):
                                act.wait_ge(turned, DC * b + c + 1)
                                modulate(hT[:, c, :], BANK_T + c, 0, MOD_CA, MOD_SA, c, b).then_inc(hT_done, 1)

                        def copy_rows(m):
                            copy_mod(act, m, BANK_R)

                        root(0)
                        copy_rows(0)
                        copy_rows(1)
                        root(1)
                        transposed(0)
                        copy_rows(2)
                        for b in range(B):
                            if b + 1 < B:
                                transposed(b + 1)
                            act.wait_ge(gates_ps, b + 1)
                            if b >= 1:
                                act.wait_ge(x1_done, b)
                            nc.scalar.activation(gates_sb[:], ps[:, BANK_G, :], ACT.Copy).then_inc(gates_copied, 1)
                            act.wait_ge(logits, b + 1)
                            nc.scalar.activation(ex[:], sc[:], ACT.Exp, scale=float(E0) ** -0.5).then_inc(ex_done, 1)
                            if b + 2 < B:
                                root(b + 2)
                            for m in MODS_BEHIND[b]:
                                copy_rows(m)

                    @block.vector
                    def _(dve):
                        n_chain = [0]

                        def link(ins):
                            n_chain[0] += 1
                            ins.then_inc(chain, 1)
                            dve.wait_ge(chain, n_chain[0])

                        def statistics(b):
                            dve.wait_ge(ld_x[b], 16)
                            if b >= 1:
                                dve.wait_ge(xh_done, b)
                            tile_stats(link, X[:, b * TB:(b + 1) * TB, :], stats, mv).then_inc(var_done, 1)

                        def normal(b):
                            dve.wait_ge(std_done, b + 1)
                            if b >= 1:
                                dve.wait_ge(turned, DC * b)
                            normalise(link, X[:, b * TB:(b + 1) * TB, :], mv, std, xh).then_inc(xh_done, 1)

                        statistics(0)
                        normal(0)
                        dve.wait_ge(ld_w, 48)
                        for c in range(DC):
                            last = nc.vector.tensor_reduce(wcat[:, c, 0:E0], wq_in[:, c, :].rearrange(
                                "p (e h) -> p e h", h=H0), AX.X, ALU.add)
                        last.then_inc(wcat_done, 1)
                        dve.wait_ge(ld_b, 48)
                        link(nc.vector.tensor_reduce(bcat[:, 0:E0], bq_in[:].rearrange("p (e h) -> p e h", h=H0),
                                                     AX.X, ALU.add))
                        statistics(1)
                        normal(1)
                        dve.wait_ge(mods_ps, 2)
                        mods_finish(link, 0, turned_mods[0], MOD_SA, MOD_GA, tmp_g)
                        dve.sem_inc(mods_done, 1)

                        for b in range(B):
                            if b == 0:
                                dve.wait_ge(mods_ps, 3)
                                mods_finish(link, 0, turned_mods[0], MOD_GA, MOD_SB, tmp_g)
                                dve.sem_inc(mods_done, 1)
                            dve.wait_ge(projected, b + 1)
                            pv = ps[:, BANK_P, 0:TB * 3 * E0].rearrange("p (t k) -> p t k", t=TB)
                            link(nc.vector.tensor_tensor(qkv[:], pv, bcat[:].rearrange("p (o k) -> p o k", o=1)
                                                         .to_broadcast([P, TB, 3 * E0]), ALU.add))
                            s4 = sc[:].rearrange("p t (d e) -> p t d e", e=E0)
                            row = lambda k: qkv[:, :, k * E0:(k + 1) * E0].rearrange("p t (o e) -> p t o e", o=1) \
                                .to_broadcast([P, TB, E0, E0])
                            col = qkv[:, :, 0:E0].rearrange("p t (d o) -> p t d o", o=1).to_broadcast([P, TB, E0, E0])
                            link(nc.vector.tensor_tensor(s4, col, row(1), ALU.mult))
                            s3 = sc[:].rearrange("p t (d e) -> p (t d) e", e=E0)
                            e3 = ex[:].rearrange("p t (d e) -> p (t d) e", e=E0)
                            wide = lambda v: v.rearrange("p (k o) -> p k o", o=1).to_broadcast([P, TB * E0, E0])
                            link(nc.vector.tensor_reduce(red[:, 0], s3, AX.X, ALU.max))
                            nc.vector.tensor_tensor(s3, s3, wide(red[:, 0]), ALU.subtract).then_inc(logits, 1)
                            if b + 2 < B:
                                statistics(b + 2)
                            dve.wait_ge(ex_done, b + 1)
                            link(nc.vector.tensor_reduce(red[:, 1], e3, AX.X, ALU.add))
                            link(nc.vector.tensor_tensor(s4, ex[:].rearrange("p t (d e) -> p t d e", e=E0), row(2), ALU.mult))
                            link(nc.vector.tensor_reduce(red[:, 2], s3, AX.X, ALU.add))
                            link(nc.vector.reciprocal(red[:, 1], red[:, 1]))
                            if b >= 2:
                                dve.wait_ge(upd_done, b - 1)
                            nc.vector.tensor_tensor(o_t[:, b % 2, :], red[:, 2], red[:, 1], ALU.mult).then_inc(o_done, 1)
                            if b + 2 < B:
                                normal(b + 2)
                        dve.wait_ge(o_done, B)
                        dve.wait_ge(gates_copied, B)
                        dve.wait_ge(x1_done, B - 1)
                        for t in range(LAST_VECTOR):
                            last = nc.vector.tensor_tensor(*gated(t, B - 1), ALU.mult)
                        last.then_inc(last_upd, 1)
                        dve.wait_ge(last_upd, 1)
                        for t in range(LAST_VECTOR):
                            x_ = X[:, (B - 1) * TB + t, :]
                            nc.vector.tensor_tensor(x_, x_, upd[:, t, :], ALU.add)
                        dve.wait_ge(mods_ps, MODS_EARLY)
                        mods_finish(link, 0, turned_mods[0], MOD_SB, 6, tmp_g)
                        mods_finish(link, 1, turned_mods[1], MOD_SA, MOD_GA, tmp_g)

                    @block.tensor
                    def _(pe):
                        pe.wait_ge(consts, 2)
                        pe.wait_ge(silu_done, 1)
                        for layer in range(2):
                            for c in range(DC):
                                k = (layer * DC + c) * B
                                last = nc.tensor.transpose(turned_c[:, k:k + B], c_in[:, layer, c * P:(c + 1) * P],
                                                           ident[0:B, 0:B])
                        last.then_inc(ct_turned, 1)

                        def turn(b):
                            pe.wait_ge(xh_done, b + 1)
                            for c in range(DC):
                                if b >= 1:
                                    pe.wait_ge(hT_done, DC * (b - 1) + c + 1)
                                turn_chunk(BANK_T + c, xh, c).then_inc(turned, 1)

                        def make_rows(m):
                            layer, which = MODS[m]
                            wm = wm0[:, :, which * D:(which + 1) * D] if layer == 0 else wm1_b[:, :, which * D:(which + 1) * D]
                            make_mod(pe, m, BANK_R, wm)

                        def turn_rows(m):
                            turn_mod(pe, m, turned_mods[MODS[m][0]])

                        turn(0)
                        pe.wait_ge(ct_copied, 1)
                        make_rows(0)
                        make_rows(1)
                        turn_rows(0)
                        turn_rows(1)
                        make_rows(2)
                        pe.wait_ge(wcat_done, 1)
                        for b in range(B):
                            pe.wait_ge(hT_done, DC * (b + 1))
                            if b >= 1:
                                pe.wait_ge(logits, b)
                            for t in range(TB):
                                for c in range(DC):
                                    last = nc.tensor.matmul(ps[:, BANK_P, t * 3 * E0:(t + 1) * 3 * E0],
                                                            hT[:, c, t * P:(t + 1) * P], wcat[:, c, :],
                                                            start=(c == 0), stop=(c == DC - 1))
                            last.then_inc(projected, 1)
                            if b + 1 < B:
                                turn(b + 1)
                            if b >= 1:
                                pe.wait_ge(gates_copied, b)
                            else:
                                turn_rows(2)
                                pe.wait_ge(mods_done, 2)
                            gate_rows(pe, BANK_G, 0, MOD_GA, b).then_inc(gates_ps, 1)
                            for m in MODS_BEHIND[b]:
                                make_rows(m)
                                turn_rows(m)


            f = ExitStack()
            with f:
                wT = [sb(f, f"wT{i}", [P, DC, D], F32R) for i in range(2)]
                cenT = sb(f, "cenT", [P, DC, NCL], F32)
                stats = sb(f, "stats", [P, NT, 6], F32)
                mv = sb(f, "mv", [P, TB, 2], F32)
                shift = sb(f, "shift", [P, NT], F32)
                std = sb(f, "std", [P, TB], F32)
                xh = sb(f, "xh", [P, TB, D], F32)
                hT = sb(f, "hT", [P, DC, S], F32)
                hP = [sb(f, f"hP{i}", [P, 2, DC, S], F32R) for i in range(2)]
                dense = sb(f, "dense", [P, NT, D], F32)
                wf = dense[:, NT - DC:, :]
                lg = sb(f, "lg", [P, TB, NCL], F32)
                pr = sb(f, "pr", [P, TB, NCL], F32)
                top = sb(f, "top", [P, TB, NCL], F32)
                red = sb(f, "red", [P, 3, TB], F32)
                qsel = sb(f, "qsel", [P, NT], F32)
                topc = sb(f, "topc", [P, NCL], F32)
                topv = sb(f, "topv", [NCL, 2], F32)
                ones = sb(f, "ones", [NCL, P], F32)
                selb = sb(f, "selb", [NCL, P], F32)
                clid = sb(f, "clid", [NCL, 1], I32)
                clidf = sb(f, "clidf", [NCL, 1], F32)
                onehot = asg[:].bitcast(F32)
                ROW_LO = 32
                with ExitStack() as early:
                    bias_hi = sb(early, "bias_hi", [ROW_LO + 1, D], F32R)
                rsel = sb(f, "rsel", [P, D], F32)
                bias_p = sb(f, "bias_p", [ROW_LO + 1, D], F32R)
                ones_p = sb(f, "ones_p", [ROW_LO + 1, P], F32R)
                gsel = sb(f, "gsel", [P, B, D], F32)
                names_ = ("chain", "var", "std", "xh", "turned", "hT", "hi", "lo", "cen_ps", "cenT", "w_ps", "wf", "w_hi",
                          "w_lo", "lgps", "lg", "ex", "iota", "zeroed", "bias_hi", "bias", "top_done", "top_ps", "selb", "rsel_ps",
                          "rsel", "gate_ps", "gsel", "dense", "drained", "u_done", "x2", "stored",
                          "var_2", "std_2", "rstd_2", "xh_2", "turned_2", "hf_2", "hi_2", "lo_2")
                s = {n: sem("f_" + n) for n in names_}
                BANK_L, BANK_X = 0, 1
                BANK_T, BANK_D = 2, 6
                turned_late = ps[:, BANK_X, 2 * P:2 * P + NM * B]

                with nc.Block() as block:
                    @block.sync
                    def _(sp):
                        for t in range(NT):
                            sp.wait_ge(s["x2"], t + 1)
                            sp.dma_start(mid_t[t // TB][:, t % TB, :], X[:, t, :]).then_inc(s["stored"], 16)
                        sp.wait_ge(s["stored"], 16 * NT)

                    @block.gpsimd
                    def _(pool):
                        nc.gpsimd.iota(clid[:], pattern=[[0, 1]], base=0, channel_multiplier=1).then_inc(s["iota"], 1)
                        nc.gpsimd.memset(bias_p[:].bitcast(F32), 0.0).then_inc(s["zeroed"], 1)
                        nc.gpsimd.memset(ones_p[:].bitcast(F32), 1.0).then_inc(s["zeroed"], 1)
                        nc.gpsimd.memset(ones[:], 1.0).then_inc(s["zeroed"], 1)
                        nc.gpsimd.memset(top[:], 0.0).then_inc(s["zeroed"], 1)
                        for c in range(DC):
                            pool.wait_ge(s["wf"], c + 1)
                            pool.wait_ge(s["w_hi"], c + 1)
                            nc.gpsimd.tensor_tensor(wT[1][:, c, :], wf[:, c, :], wT[0][:, c, :].bitcast(F32),
                                                    ALU.subtract).then_inc(s["w_lo"], 1)
                        for t in range(NT):
                            pool.wait_ge(s["u_done"], t + 1)
                            nc.gpsimd.tensor_tensor(X[:, t, :], X[:, t, :], dense[:, t, :], ALU.add).then_inc(s["x2"], 1)

                    @block.scalar
                    def _(act):
                        def root(b):
                            act.wait_ge(s["var"], b + 1)
                            nc.scalar.activation(std[:], mv[:, :, 1], ACT.Sqrt).then_inc(s["std"], 1)

                        def transposed(b):
                            if b >= 1:
                                act.wait_ge(s["lgps"], b)
                                act.wait_ge(s["lo"], DC * b)
                            if b >= 2:
                                act.wait_ge(s["dense"], TB * (b - 1))
                            for c in range(DC):
                                act.wait_ge(s["turned"], DC * b + c + 1)
                                modulate(hT[:, c, :], BANK_T + c, 0, MOD_CB, MOD_SB, c, b).then_inc(s["hT"], 1)
                                modulate(hP[0][:, b % 2, c, :], BANK_T + c, 0, MOD_CB, MOD_SB, c, b).then_inc(s["hi"], 1)

                        def drain(t):
                            act.wait_ge(s["dense"], t + 1)
                            if t >= NT - DC:
                                act.wait_ge(s["w_lo"], DC)
                            nc.scalar.activation(dense[:, t, :], ps[:, BANK_D + t % 2, :], ACT.Copy).then_inc(s["drained"], 1)

                        act.wait_ge(s["cen_ps"], 1)
                        nc.scalar.activation(cenT[:], ps[:, BANK_X, 0:DC * NCL].rearrange("p (c k) -> p c k", c=DC),
                                             ACT.Copy).then_inc(s["cenT"], 1)
                        for c in range(DC):
                            act.wait_ge(s["w_ps"], c + 1)
                            nc.scalar.activation(wf[:, c, :], ps[:, BANK_T + c, :], ACT.Copy).then_inc(s["wf"], 1)
                            nc.scalar.activation(wT[0][:, c, :], ps[:, BANK_T + c, :], ACT.Copy).then_inc(s["w_hi"], 1)
                            if c == 1:
                                root(0)
                        nc.scalar.activation(bias_hi[:], bias_r[0:ROW_LO + 1, :], ACT.Copy).then_inc(s["bias_hi"], 1)
                        act.wait_ge(s["zeroed"], 1)
                        nc.scalar.activation(bias_p[0:1, :], bias_r[0:1, :], ACT.Copy).then_inc(s["bias"], 1)
                        transposed(0)
                        for b in range(B):
                            if b + 1 < B:
                                root(b + 1)
                            act.wait_ge(s["lg"], b + 1)
                            nc.scalar.activation(lg[:], lg[:], ACT.Exp, scale=1.0 / TEMPERATURE).then_inc(s["ex"], 1)
                            for t in range(TB):
                                drain(TB * b + t)
                                if t == 1 and b + 1 < B:
                                    transposed(b + 1)
                        act.wait_ge(s["rsel_ps"], 1)
                        nc.scalar.activation(rsel[:], ps[:, BANK_L, :], ACT.Copy).then_inc(s["rsel"], 1)
                        copy_mod(act, MODS_EARLY, BANK_D)
                        copy_mod(act, MODS_EARLY + 1, BANK_D)
                        for i in range(PAIR):
                            tiles = slice(TB * i, TB * (i + 1))
                            act.wait_ge(s["var_2"], i + 1)
                            nc.scalar.activation(rstd_2[:, tiles], mv_2[:, tiles, 1], ACT.Sqrt).then_inc(s["std_2"], 1)
                            act.wait_ge(s["rstd_2"], i + 1)
                            for t in range(TB * i, TB * (i + 1)):
                                last = nc.scalar.activation(xh[:, t % TB, :], X[:, t, :], ACT.Identity, bias=shift[:, t:t + 1],
                                                            scale=rstd_2[:, t:t + 1])
                            last.then_inc(s["xh_2"], 1)
                            if i == 0:
                                for m in range(MODS_EARLY + 2, len(MODS)):
                                    copy_mod(act, m, BANK_D)
                            for c in range(DC):
                                act.wait_ge(s["turned_2"], DC * i + c + 1)
                                if i == 1:
                                    act.wait_ge(s["lo_2"], c + 1)
                                modulate(hT[:, c, :], BANK_T + c, 1, MOD_CA, MOD_SA, c, i).then_inc(s["hf_2"], 1)
                                modulate(hA[0][:, c, i * S:(i + 1) * S], BANK_T + c, 1, MOD_CA, MOD_SA, c, i).then_inc(s["hi_2"], 1)
                        tiles = slice(TB * PAIR, NT)
                        act.wait_ge(s["var_2"], PAIR + 1)
                        nc.scalar.activation(rstd_2[:, tiles], mv_2[:, tiles, 1], ACT.Sqrt).then_inc(s["std_2"], 1)

                    @block.vector
                    def _(dve):
                        n_chain = [0]

                        def link(ins):
                            n_chain[0] += 1
                            ins.then_inc(s["chain"], 1)
                            dve.wait_ge(s["chain"], n_chain[0])

                        def statistics(b):
                            tile_stats(link, X[:, b * TB:(b + 1) * TB, :], stats, mv).then_inc(s["var"], 1)

                        def normal(b):
                            dve.wait_ge(s["std"], b + 1)
                            if b >= 1:
                                dve.wait_ge(s["turned"], DC * b)
                            normalise(link, X[:, b * TB:(b + 1) * TB, :], mv, std, xh).then_inc(s["xh"], 1)

                        statistics(0)
                        normal(0)
                        dve.wait_ge(s["iota"], 1)
                        link(nc.vector.tensor_copy(clidf[:], clid[:]))
                        link(nc.vector.tensor_scalar(onehot, asg[:], clidf[:, 0:1], None, ALU.is_equal))
                        dve.wait_ge(s["zeroed"], 4)
                        dve.wait_ge(s["bias_hi"], 1)
                        nc.vector.tensor_tensor(bias_p[ROW_LO:ROW_LO + 1, :], bias_r[ROW_LO:ROW_LO + 1, :],
                                                bias_hi[ROW_LO:ROW_LO + 1, :].bitcast(F32), ALU.subtract).then_inc(s["bias"], 1)
                        wide = lambda v: v.rearrange("p (k o) -> p k o", o=1).to_broadcast([P, TB, NCL])
                        for b in range(B):
                            for c in range(DC):
                                dve.wait_ge(s["hi"], DC * b + c + 1)
                                nc.vector.tensor_tensor(hP[1][:, b % 2, c, :], hT[:, c, :], hP[0][:, b % 2, c, :].bitcast(F32),
                                                        ALU.subtract).then_inc(s["lo"], 1)
                            if b + 1 < B:
                                dve.wait_ge(s["xh"], b + 1)
                                statistics(b + 1)
                            dve.wait_ge(s["lgps"], b + 1)
                            lp = ps[:, BANK_L, 0:TB * NCL].rearrange("p (t k) -> p t k", t=TB)
                            link(nc.vector.tensor_reduce(red[:, 0], lp, AX.X, ALU.max))
                            nc.vector.tensor_tensor(lg[:], lp, wide(red[:, 0]), ALU.subtract).then_inc(s["lg"], 1)
                            if b + 1 < B:
                                normal(b + 1)
                            dve.wait_ge(s["ex"], b + 1)
                            link(nc.vector.tensor_reduce(red[:, 1], lg[:], AX.X, ALU.add))
                            link(nc.vector.reciprocal(red[:, 1], red[:, 1]))
                            link(nc.vector.tensor_tensor(pr[:], lg[:], wide(red[:, 1]), ALU.mult))
                            link(nc.vector.tensor_reduce(red[:, 2], pr[:], AX.X, ALU.max))
                            link(nc.vector.tensor_scalar(qsel[:, b * TB:(b + 1) * TB], red[:, 2], THRESHOLD, None, ALU.is_gt))
                            link(nc.vector.tensor_tensor(top[:], top[:], pr[:], ALU.max))
                        nc.vector.tensor_reduce(topc[:], top[:].rearrange("p t k -> p k t"), AX.X, ALU.max).then_inc(s["top_done"], 1)
                        dve.wait_ge(s["top_ps"], 1)
                        link(nc.vector.tensor_reduce(topv[:, 0:1], ps[0:NCL, BANK_X, 0:P], AX.X, ALU.max))
                        link(nc.vector.tensor_scalar(topv[:, 1:2], topv[:, 0:1], THRESHOLD, None, ALU.is_gt))
                        nc.vector.tensor_scalar(selb[:], ones[:], topv[:, 1:2], None, ALU.mult).then_inc(s["selb"], 1)
                        dve.wait_ge(s["rsel"], 1)
                        dve.wait_ge(s["gate_ps"], B)
                        for b in range(B):
                            last = nc.vector.tensor_tensor(gsel[:, b, :], ps[:, BANK_T + b, :], rsel[:], ALU.mult)
                            last.then_inc(s["gsel"], 1)

                        def gated(b):
                            if b == 0:
                                dve.wait_ge(s["gsel"], B)
                            for t in range(TB * b, TB * (b + 1)):
                                dve.wait_ge(s["drained"], t + 1)
                                nc.vector.scalar_tensor_tensor(dense[:, t, :], dense[:, t, :], qsel[:, t:t + 1],
                                                               gsel[:, b, :], ALU.mult, ALU.mult).then_inc(s["u_done"], 1)

                        def statistics_2(b):
                            for t in range(TB * b, TB * (b + 1)):
                                dve.wait_ge(s["x2"], t + 1)
                                last = nc.vector.bn_stats(stats[:, t, :], X[:, t, :])
                            return last

                        def variances_2(first, end):
                            for t in range(first, end):
                                last = nc.vector.bn_aggr(mv_2[:, t, :], stats[:, t, :])
                            link(last)
                            nc.vector.tensor_scalar(mv_2[:, first:end, 1], mv_2[:, first:end, 1], EPS, None, ALU.add) \
                                .then_inc(s["var_2"], 1)

                        def inverse_2(i):
                            tiles = slice(TB * i, TB * (i + 1))
                            dve.wait_ge(s["std_2"], i + 1)
                            link(nc.vector.reciprocal(rstd_2[:, tiles], rstd_2[:, tiles]))
                            nc.vector.scalar_tensor_tensor(shift[:, tiles], mv_2[:, tiles, 0], -1.0, rstd_2[:, tiles],
                                                           ALU.mult, ALU.mult).then_inc(s["rstd_2"], 1)

                        def lows_2(i):
                            for c in range(DC):
                                dve.wait_ge(s["hi_2"], DC * i + c + 1)
                                nc.vector.tensor_tensor(hA[1][:, c, i * S:(i + 1) * S], hT[:, c, :],
                                                        hA[0][:, c, i * S:(i + 1) * S].bitcast(F32), ALU.subtract) \
                                    .then_inc(s["lo_2"], 1)

                        gated(0)
                        gated(1)
                        link(statistics_2(0))
                        variances_2(0, TB)
                        gated(2)
                        inverse_2(0)
                        link(statistics_2(1))
                        variances_2(TB, 2 * TB)
                        gated(3)
                        lows_2(0)
                        inverse_2(1)
                        for b in range(PAIR, B):
                            last = statistics_2(b)
                        link(last)
                        lows_2(1)
                        variances_2(TB * PAIR, NT)
                        dve.wait_ge(s["std_2"], PAIR + 1)
                        link(nc.vector.reciprocal(rstd_2[:, TB * PAIR:], rstd_2[:, TB * PAIR:]))
                        dve.wait_ge(mods_ps, len(MODS))
                        mods_finish(link, 1, turned_late, MOD_GA, 6, tmp_g)

                    @block.tensor
                    def _(pe):
                        for c in range(DC):
                            last = nc.tensor.transpose(ps[:, BANK_X, c * NCL:(c + 1) * NCL], cen_in[:, c * P:(c + 1) * P],
                                                       ident[0:NCL, 0:NCL])
                        last.then_inc(s["cen_ps"], 1)
                        for c in range(DC):
                            for o in range(DC):
                                last = nc.tensor.transpose(ps[:, BANK_T + c, o * P:(o + 1) * P],
                                                           w_in[:, o, c * P:(c + 1) * P], ident[:])
                            last.then_inc(s["w_ps"], 1)

                        def turn(b):
                            pe.wait_ge(s["xh"], b + 1)
                            for c in range(DC):
                                if b == 0:
                                    pe.wait_ge(s["w_hi"], c + 1)
                                else:
                                    pe.wait_ge(s["hi"], DC * (b - 1) + c + 1)
                                turn_chunk(BANK_T + c, xh, c).then_inc(s["turned"], 1)

                        def linear(t):
                            b, r = t // TB, t % TB
                            if t >= 2:
                                pe.wait_ge(s["drained"], t - 1)
                            if t == 0:
                                pe.wait_ge(s["w_lo"], DC)
                                pe.wait_ge(s["bias"], 2)
                            if r == 0:
                                pe.wait_ge(s["lo"], DC * (b + 1))
                            bank = ps[:, BANK_D + t % 2, :]
                            nc.tensor.matmul(bank, ones_p[:], bias_p[:], start=True, stop=False)
                            for c in range(DC):
                                for n, (i, k) in enumerate(((0, 0), (1, 0), (0, 1))):
                                    last = nc.tensor.matmul(bank, hP[i][:, b % 2, c, r * P:(r + 1) * P], wT[k][:, c, :],
                                                            start=False, stop=(c == DC - 1 and n == 2))
                            last.then_inc(s["dense"], 1)

                        turn(0)
                        for b in range(B):
                            if b == 0:
                                pe.wait_ge(s["cenT"], 1)
                            else:
                                pe.wait_ge(s["lg"], b)
                            pe.wait_ge(s["hT"], DC * (b + 1))
                            for t in range(TB):
                                for c in range(DC):
                                    last = nc.tensor.matmul(ps[:, BANK_L, t * NCL:(t + 1) * NCL],
                                                            hT[:, c, t * P:(t + 1) * P], cenT[:, c, :],
                                                            start=(c == 0), stop=(c == DC - 1))
                            last.then_inc(s["lgps"], 1)
                            linear(TB * b)
                            linear(TB * b + 1)
                            if b + 1 < B:
                                turn(b + 1)
                            else:
                                pe.wait_ge(s["hi"], DC * B)
                                for i in range(B):
                                    last = gate_rows(pe, BANK_T + i, 0, MOD_GB, i).then_inc(s["gate_ps"], 1)
                                pe.wait_ge(s["top_done"], 1)
                                nc.tensor.transpose(ps[0:NCL, BANK_X, 0:P], topc[:], ident[:]).then_inc(s["top_ps"], 1)
                            linear(TB * b + 2)
                            if b == B - 1:
                                pe.wait_ge(s["selb"], 1)
                                nc.tensor.matmul(ps[:, BANK_L, :], selb[:], onehot, start=True, stop=True).then_inc(s["rsel_ps"], 1)
                            linear(TB * b + 3)
                        pe.wait_ge(s["drained"], NT)
                        for m in range(MODS_EARLY, len(MODS)):
                            at_ = (m - MODS_EARLY) * D
                            make_mod(pe, m, BANK_D, wm1_a[:, :, at_:at_ + D])
                            if m > MODS_EARLY:
                                turn_mod(pe, m - 1, turned_late)
                        turn_mod(pe, len(MODS) - 1, turned_late)
                        pe.wait_ge(s["gsel"], B)
                        for i in range(PAIR):
                            pe.wait_ge(s["xh_2"], i + 1)
                            for c in range(DC):
                                if i >= 1:
                                    pe.wait_ge(s["hi_2"], c + 1)
                                turn_chunk(BANK_T + c, xh, c).then_inc(s["turned_2"], 1)

        a = ExitStack()
        with a:
            NP = PAIR * TB
            UNITS = PAIR * GQ
            KEYS = [(i + 1) * P for i in range(TB)]
            SC = [(3, 0, 0), (2, 1, 0), (1, 2, 0), (0, 2, 256)]
            PO = {3: 0, 2: 512, 1: 896, 0: 1152}
            PW = 1280
            T0, T2, T1 = 0, 512, 768
            TW = 1152
            PVS = [(T0, 512, 0, 0), (T1, 384, P, 1), (T2, 256, 2 * P, 2)]
            BANK_S, BANK_T, BANK_V, BANK_J = 0, 3, 5, 6
            JOBS = ["V0", "K0", "Q0", "K1", "Q1", "V1"] + [f"Q{u}" for u in range(2, UNITS)] + \
                   [f"W{t}" for t in range(NP)]
            NJ = len(JOBS)
            TJOBS = ["V0"] + [f"0.{k}" for k in range(3)] + ["V1"] + [f"{u}.{k}" for u in range(1, UNITS) for k in range(3)]
            NTJ = len(TJOBS)
            TJOB = {n: i for i, n in enumerate(TJOBS)}
            assert NJ % 2 == 0 and NTJ % 2 == 0
            JOB = {n: i for i, n in enumerate(JOBS)}

            wq_in = sb(a, "wq_in", [P, DC, D], F32)
            wo_in = sb(a, "wo_in", [P, GQ, D], F32)
            wq = [sb(a, f"wq{i}", [P, DC, D], F32R) for i in range(2)]
            wk = [sb(a, f"wk{i}", [P, DC, HD], F32R) for i in range(2)]
            wv = [sb(a, f"wv{i}", [P, DC, HD], F32R) for i in range(2)]
            wo = [sb(a, f"wo{i}", [P, GQ, D], F32R) for i in range(2)]
            hT = hA
            acc = sb(a, "acc", [P, NP, D], F32)

            wq_v = w_q.rearrange("(c p) n -> p c n", p=P)
            wo_v = w_o.rearrange("(g h p) n -> g p h n", p=P, h=GQ)
            wo_ld = sem("wo_ld")
            qkv_split, wo_split = sem("qkv_split"), sem("wo_split")
            NSPL = 2 + GQ

            def load_q(sp, g):
                sp.dma_start(wq_in[:], wq_v[:, :, bass.ts(g, D)]).then_inc(q_in, 16)

            waits_seen = sem("waits_seen")

            def round_part(dst, src):
                nc.gpsimd.sem_inc(waits_seen, 1)
                return nc.gpsimd.tensor_copy(dst, src)

            def split_qkv(pool, hi_done, hi_base, before):
                n = 0
                for dst, src, w in ((wk, wk_in, HD), (wv, wv_in, HD), (wq, wq_in, D)):
                    for q in range(w // HD):
                        cols = slice(q * HD, (q + 1) * HD)
                        before(n)
                        round_part(dst[0][:, :, cols], src[:, :, cols]).then_inc(hi_done, 1)
                        n += 1
                        pool.wait_ge(hi_done, hi_base + n)
                        nc.gpsimd.tensor_tensor(dst[1][:, :, cols], src[:, :, cols], dst[0][:, :, cols].bitcast(F32),
                                                ALU.subtract).then_inc(qkv_split, 1)

            at = ExitStack()
            with at:
                with ExitStack() as early:
                    rows_1 = sb(early, "rows_1", [P, TB, D], F32)
                    hf = sb(early, "hf", [P, PAIR, DC, S], F32)
                kT = [sb(at, f"kT{i}", [P, PAIR, S], F32R) for i in range(2)]
                oT = [sb(at, f"oT{i}", [P, PAIR, GQ, S], F32R) for i in range(2)]
                vT = sb(at, "vT", [P, S], F32)
                V = [sb(at, f"V{i}", [P, PAIR, TB - 1, HD], F32R) for i in range(2)]
                qT = [sb(at, f"qT{i}", [P, 2, S - P], F32R) for i in range(2)]
                pe_ = sb(at, "probs", [P, 2, PW], F32)
                pt = [sb(at, f"pt{i}", [P, TW], F32R) for i in range(2)]
                q_first = sb(at, "q_first", [P, 2, P], F32)
                k_first = sb(at, "k_first", [P, PAIR, P], F32)
                v_last = sb(at, "v_last", [P, PAIR, HD], F32)
                pt_last = sb(at, "pt_last", [P, P], F32)
                nmax = sb(at, "nmax", [P, 2, TB], F32)
                rsum = sb(at, "rsum", [P, 2, TB], F32)
                rinv = sb(at, "rinv", [P, 2, TB], F32)

                job_full = sem("job_full")
                job_hi, kq_ready, v_copied = (sem(n) for n in ("job_hi", "kq_ready", "v_copied"))
                s_full, max_done, exp_done, rinv_done, p_ready = (sem(n) for n in (
                    "s_full", "max_done", "exp_done", "rinv_done", "p_ready"))
                t_full, t_hi, t_ready = (sem(n) for n in ("t_full", "t_hi", "t_ready"))
                o_full, o_hi, o_ready = (sem(n) for n in ("o_full", "o_hi", "o_ready"))
                w_hi, acc_done, cleared = (sem(n) for n in ("w_hi", "acc_done", "cleared"))
                gate_r = sb(at, "gate_r", [P, B, D], F32)
                mask = sb(at, "mask", [P, TB * P], F32)
                masked = sem("masked")
                gates_full, gates_copied, gated = (sem(n) for n in ("gates_full", "gates_copied", "gated"))
                n_xh, n_turned, n_hf, n_hi, n_lo = (sem("n_" + n) for n in ("xh", "turned", "hf", "hi", "lo"))
                ld_x = [sem(f"ld_x{i}") for i in range(PAIR)]
                stored = sem("stored")

                probs_flat = pe_[:].rearrange("p u k -> p (u k)")[:, 0:TB * D].rearrange("p (t d) -> p t d", d=D)
                BANK_H = [(2, 3, 4, 5), (6, 7, 0, 1)]
                BANK_G = (0, 1, 2, 5)
                
                def rows(i, t):
                    return probs_flat[:, t, :] if i == 0 else rows_1[:, t, :]

                KQ_JOBS = [j for j in JOBS if j[0] in "KQ"]
                NKQ = len(KQ_JOBS)
                STEP_Q = {u: u + 2 for u in range(UNITS - 2)}
                STEP_W = {UNITS - 2: (0, 1), UNITS - 1: (2, 3)}

                def full(g, name):
                    return NJ * g + (JOB[name] + 2)

                def turned(g, name):
                    return NTJ * g + (TJOB[name] + 1)

                def parted(g, name):
                    return NTJ * g + (TJOB[name] + 3)

                def left(g, j):
                    name = JOBS[j]
                    if j < 0:
                        return acc_done, NP * g + (NP + j + 1)
                    if name[0] == "W":
                        return acc_done, NP * g + (NP + int(name[1:]) + 1)
                    if name[0] == "V":
                        return v_copied, PAIR * g + (int(name[1:]) + 1)
                    return kq_ready, NKQ * g + (KQ_JOBS.index(name) + 1)

                with nc.Block() as block:
                    @block.sync
                    def _(sp):
                        for pair in range(B // PAIR):
                            if pair == 0:
                                load_q(sp, 0)
                            with sp.Fori(NKV * pair, NKV * (pair + 1)) as g:
                                sp.wait_ge(wo_split, GQ * g + GQ)
                                sp.dma_start(wo_in[:], wo_v[bass.ds(g % NKV, 1)].rearrange("g p h n -> p (g h) n")).then_inc(wo_ld, 16)
                                sp.wait_ge(qkv_split, NSPL * g + NSPL)
                                load_kv(sp, (g + 1) % NKV)
                                load_q(sp, (g + 1) % NKV)

                            for t in range(NP):
                                sp.wait_ge(gated, NP * pair + t + 1)
                                sp.dma_start(att_t[PAIR * pair + t // TB][:, t % TB, :], acc[:, t, :]).then_inc(stored, 16)
                    @block.gpsimd
                    def _(pool):
                        HIS = GQ + NSPL
                        def before_split(n):
                            if n == 2:
                                nc.gpsimd.memset(mask[:], 0.0).then_inc(masked, 1)
                                pool.wait_ge(masked, 1)
                                nc.gpsimd.affine_select(out=mask[:, (TB - 1) * P:], in_=mask[:, (TB - 1) * P:],
                                                        compare_op=ALU.is_ge, fill=NEG, base=0, pattern=[[-1, P]],
                                                        channel_multiplier=1).then_inc(masked, 1)
                                pool.wait_ge(q_in, 16)

                        split_qkv(pool, w_hi, 0, before_split)
                        for t in range(NP):
                            nc.gpsimd.memset(acc[:, t, :], 0.0).then_inc(cleared, 1)
                        pool.wait_ge(cleared, NP)
                        pool.sem_inc(wo_split, GQ)
                        for pair in range(B // PAIR):
                            with pool.Fori(NKV * pair, NKV * (pair + 1)) as g:
                                pool.wait_ge(wo_ld, 16 * g + 16)
                                pool.wait_ge(job_full, NJ * g + 1)
                                for h in range(GQ):
                                    round_part(wo[0][:, h, :], wo_in[:, h, :]).then_inc(w_hi, 1)
                                    pool.wait_ge(w_hi, HIS * g + (NSPL + h + 1))
                                    nc.gpsimd.tensor_tensor(wo[1][:, h, :], wo_in[:, h, :], wo[0][:, h, :].bitcast(F32),
                                                            ALU.subtract).then_inc(wo_split, 1)
                                pool.wait_ge(kv_in, 32 * g + 32 * 2)
                                pool.wait_ge(q_in, 16 * g + 16 * 2)
                                last_use = ["K1", "V1"] + [f"Q{u}" for u in range(UNITS - GQ, UNITS)]
                                split_qkv(pool, w_hi, HIS * g + HIS, lambda n: pool.wait_ge(job_full, full(g, last_use[n])))

                            for t in range(NP):
                                pool.wait_ge(acc_done, NP * NKV * (pair + 1) + t + 1)
                                pool.wait_ge(gates_copied, B)
                                nc.gpsimd.tensor_tensor(acc[:, t, :], acc[:, t, :], gate_r[:, PAIR * pair + t // TB, :],
                                                        ALU.mult).then_inc(gated, 1)
                            if pair + 1 < B // PAIR:
                                pool.wait_ge(stored, 16 * NP * (pair + 1))
                                for t in range(NP):
                                    nc.gpsimd.memset(acc[:, t, :], 0.0).then_inc(cleared, 1)

                    @block.tensor
                    def _(pe):
                        pe.sem_inc(job_full, 1)
                        for b in range(B):
                            gate_rows(pe, BANK_G[b], 1, MOD_GA, b).then_inc(gates_full, 1)
                        for pair in range(B // PAIR):
                            heads = NKV * pair
                            if pair >= 1:
                                pe.wait_ge(exp_done, UNITS * TB * heads + TB)
                                pe.wait_ge(t_ready, NTJ * heads + 2)
                                pe.wait_ge(o_ready, UNITS * heads + 1)
                                for i in range(PAIR):
                                    pe.wait_ge(n_xh, PAIR * (pair - 1) + i + 1)
                                    if i == 1:
                                        pe.wait_ge(acc_done, NP * heads + NP)
                                    for c in range(DC):
                                        for t in range(TB):
                                            last = nc.tensor.transpose(ps[:, BANK_H[i][c], t * P:(t + 1) * P],
                                                                       rows(i, t)[:, c * P:(c + 1) * P], ident[:])
                                        last.then_inc(n_turned, 1)
                                pe.wait_ge(n_lo, DC * (PAIR * (pair - 1) + 1))
                                pe.wait_ge(n_hf, DC * (PAIR * (pair - 1) + 1) + 2)
                            with pe.Fori(NKV * pair, NKV * (pair + 1)) as g:
                                def job_bank(name):
                                    j = JOB[name]
                                    pe.wait_ge(*left(g, j - 2))
                                    return BANK_J + j % 2

                                def project(name, w, cols, b):
                                    bank = job_bank(name)
                                    for c in range(DC):
                                        for n, (i, k) in enumerate(((0, 0), (0, 1), (1, 0))):
                                            last = nc.tensor.matmul(ps[:, bank, :], w[i][:, c, cols],
                                                                    hT[k][:, c, b * S:(b + 1) * S],
                                                                    start=(c == 0 and n == 0), stop=(c == DC - 1 and n == 2))
                                    last.then_inc(job_full, 1)
                                    return last

                                def q_project(u):
                                    h = u % GQ
                                    project(f"Q{u}", wq, slice(h * HD, (h + 1) * HD), u // GQ)

                                def turn_bank(name):
                                    j = TJOB[name]
                                    pe.wait_ge(t_ready, NTJ * g + (j + 1))
                                    return BANK_T + j % 2

                                def turn_v(b):
                                    bank = turn_bank(f"V{b}")
                                    pe.wait_ge(v_copied, PAIR * g + (b + 1))
                                    for t in range(TB):
                                        last = nc.tensor.transpose(ps[:, bank, t * P:(t + 1) * P], vT[:, t * P:(t + 1) * P], ident[:])
                                    last.then_inc(t_full, 1)

                                def scores(u):
                                    b = u // GQ
                                    pe.wait_ge(kq_ready, NKQ * g + (KQ_JOBS.index(f"Q{u}") + 1))
                                    for n, (i, bank, col) in enumerate(SC):
                                        if n < 3:
                                            pe.wait_ge(exp_done, UNITS * TB * g + (TB * u + (1, 2, 4)[n]))
                                        dst = ps[:, BANK_S + bank, col:col + KEYS[i]]
                                        if i == 0:
                                            last = nc.tensor.matmul(dst, q_first[:, u % 2, :], k_first[:, b, :],
                                                                    start=True, stop=True)
                                        else:
                                            for k, (x_, y_) in enumerate(((0, 0), (0, 1), (1, 0))):
                                                last = nc.tensor.matmul(dst, qT[x_][:, u % 2, (i - 1) * P:i * P],
                                                                        kT[y_][:, b, 0:KEYS[i]], start=(k == 0), stop=(k == 2))
                                        last.then_inc(s_full, 1)

                                def turn(u, k):
                                    if k == 0:
                                        pe.wait_ge(p_ready, UNITS * TB * g + TB * (u + 1))
                                    bank = turn_bank(f"{u}.{k}")
                                    blocks = ([(i, 0) for i in range(4)], [(3, 3), (1, 1), (2, 1), (3, 1)], [(2, 2), (3, 2)])[k]
                                    for n, (i, kt) in enumerate(blocks):
                                        last = nc.tensor.transpose(ps[:, bank, n * P:(n + 1) * P],
                                                                   pe_[:, u % 2, PO[i] + kt * P:PO[i] + (kt + 1) * P], ident[:])
                                    last.then_inc(t_full, 1)

                                def outputs(u):
                                    b = u // GQ
                                    if u % GQ == 0:
                                        pe.wait_ge(t_ready, parted(g, f"V{b}"))
                                    pe.wait_ge(o_ready, UNITS * g + (u + 1))
                                    for n, (col, N, q0, kt) in enumerate(PVS):
                                        pe.wait_ge(t_ready, parted(g, f"{u}.{n}"))
                                        for k, (x_, y_) in enumerate(((0, 0), (1, 0), (0, 1))):
                                            last = nc.tensor.matmul(ps[:, BANK_V, q0:q0 + N], V[x_][:, b, kt, :],
                                                                    pt[y_][:, col:col + N], start=(n == 0 and k == 0), stop=(n == 2 and k == 2))
                                        if n == 1:
                                            nc.tensor.matmul(ps[:, BANK_V, 3 * P:], v_last[:, b, :], pt_last[:],
                                                             start=False, stop=False)
                                    last.then_inc(o_full, 1)

                                def out_project(t):
                                    bank = job_bank(f"W{t}")
                                    b, r = t // TB, t % TB
                                    if t == 0:
                                        pe.wait_ge(wo_split, GQ * g + GQ * 2)
                                    for h in range(GQ):
                                        if r == 0:
                                            pe.wait_ge(o_ready, UNITS * g + (GQ * b + h + 2))
                                        for n, (x_, y_) in enumerate(((0, 0), (1, 0), (0, 1))):
                                            last = nc.tensor.matmul(ps[:, bank, :], oT[x_][:, b, h, r * P:(r + 1) * P], wo[y_][:, h, :],
                                                                    start=(h == 0 and n == 0), stop=(h == GQ - 1 and n == 2))
                                    last.then_inc(job_full, 1)

                                def split_done(n):
                                    pe.wait_ge(qkv_split, NSPL * g + n)

                                split_done(2)
                                project("V0", wv, slice(0, HD), 0)
                                project("K0", wk, slice(0, HD), 0)
                                split_done(3)
                                q_project(0)
                                turn_v(0)
                                if pair >= 1:
                                    pe.wait_ge(n_lo, DC * PAIR * pair)
                                project("K1", wk, slice(0, HD), 1)
                                if pair == 0:
                                    pe.wait_ge(gates_copied, B)
                                scores(0)
                                split_done(4)
                                q_project(1)
                                project("V1", wv, slice(0, HD), 1)
                                for u in range(UNITS):
                                    if u + 1 < UNITS:
                                        scores(u + 1)
                                    turn(u, 0)
                                    turn(u, 1)
                                    if u in STEP_Q:
                                        if STEP_Q[u] < GQ:
                                            split_done(3 + STEP_Q[u])
                                        q_project(STEP_Q[u])
                                    for t in STEP_W.get(u, ())[0:1]:
                                        out_project(t)
                                    turn(u, 2)
                                    for t in STEP_W.get(u, ())[1:2]:
                                        out_project(t)
                                    outputs(u)
                                    if u == 0:
                                        turn_v(1)
                                for t in range(TB, NP):
                                    out_project(t)

                    @block.scalar
                    def _(act):
                        def load_rows(pair):
                            nc.scalar.dma_start(probs_flat, mid_t[PAIR * pair]).then_inc(ld_x[0], 16)
                            nc.scalar.dma_start(rows_1[:], mid_t[PAIR * pair + 1]).then_inc(ld_x[1], 16)

                        act.sem_inc(exp_done, TB)
                        for b in range(B):
                            act.wait_ge(gates_full, b + 1)
                            nc.scalar.activation(gate_r[:, b, :], ps[:, BANK_G[b], :], ACT.Copy).then_inc(gates_copied, 1)
                        for pair in range(B // PAIR):
                            if pair >= 1:
                                act.wait_ge(t_full, NTJ * NKV * pair)
                                load_rows(pair)
                            for i in range(PAIR if pair >= 1 else 0):
                                for c in range(DC):
                                    act.wait_ge(n_turned, DC * (PAIR * (pair - 1) + i) + c + 1)
                                    modulate(hf[:, i, c, :], BANK_H[i][c], 1, MOD_CA, MOD_SA, c, PAIR * pair + i).then_inc(n_hf, 1)
                            with act.Fori(NKV * pair, NKV * (pair + 1)) as g:
                                def hi(name, dst, first, scale=1.0):
                                    j = JOB[name]
                                    act.wait_ge(job_full, full(g, JOBS[j]))
                                    bank = ps[:, BANK_J + j % 2, :]
                                    nc.scalar.activation(first, bank[:, 0:P], ACT.Copy, scale=scale)
                                    nc.scalar.activation(dst, bank[:, S - dst.shape[-1]:], ACT.Copy, scale=scale).then_inc(job_hi, 1)

                                def v_copy(b):
                                    j = JOB[f"V{b}"]
                                    act.wait_ge(job_full, full(g, JOBS[j]))
                                    nc.scalar.activation(vT[:], ps[:, BANK_J + j % 2, :], ACT.Copy).then_inc(v_copied, 1)

                                def exps(u):
                                    for n, (i, bank, col) in enumerate(SC):
                                        if n < 3:
                                            act.wait_ge(max_done, UNITS * TB * g + (TB * u + (1, 2, 4)[n]))
                                        nc.scalar.activation(pe_[:, u % 2, PO[i]:PO[i] + KEYS[i]], ps[:, BANK_S + bank, col:col + KEYS[i]],
                                                             ACT.Exp, bias=nmax[:, u % 2, i:i + 1], scale=-1.0,
                                                             accum_out=rsum[:, u % 2, i:i + 1]).then_inc(exp_done, 1)

                                def turned_hi(name, dst, col, single=None, single_col=0):
                                    act.wait_ge(t_full, turned(g, name))
                                    bank = ps[:, BANK_T + TJOB[name] % 2, :]
                                    if single is not None:
                                        nc.scalar.activation(single, bank[:, single_col:single_col + P], ACT.Copy)
                                    nc.scalar.activation(dst, bank[:, col:col + dst.shape[-1]], ACT.Copy).then_inc(t_hi, 1)

                                def t_part(u, k):
                                    first, N, _, _ = PVS[k]
                                    dst = pt[0][:, first:first + N]
                                    if k == 1:
                                        turned_hi(f"{u}.{k}", dst, P, pt_last[:])
                                    else:
                                        turned_hi(f"{u}.{k}", dst, 0)

                                def v_part(b):
                                    turned_hi(f"V{b}", V[0][:, b].rearrange("p t d -> p (t d)"), 0, v_last[:, b, :], (TB - 1) * P)

                                hi_q = lambda u: hi(f"Q{u}", qT[0][:, u % 2, :], q_first[:, u % 2, :], QSCALE)
                                v_copy(0)
                                hi("K0", kT[0][:, 0, :], k_first[:, 0, :])
                                hi_q(0)
                                v_part(0)
                                hi("K1", kT[0][:, 1, :], k_first[:, 1, :])
                                exps(0)
                                hi_q(1)
                                v_copy(1)
                                for u in range(UNITS):
                                    if u + 1 < UNITS:
                                        exps(u + 1)
                                    t_part(u, 0)
                                    t_part(u, 1)
                                    if u in STEP_Q:
                                        hi_q(STEP_Q[u])
                                    t_part(u, 2)
                                    act.wait_ge(o_full, UNITS * g + (u + 1))
                                    nc.scalar.activation(oT[0][:, u // GQ, u % GQ, :], ps[:, BANK_V, :], ACT.Copy).then_inc(o_hi, 1)
                                    if u == 0:
                                        v_part(1)

                        act.wait_ge(job_full, NJ * NKV * (B // PAIR) + 1 - NP)
                        for q in range(3):
                            load_weights(nc.scalar.dma_start, q)
                        nc.scalar.dma_start(xt[:, 0], mid_t[0]).then_inc(ld_xm, 16)
                        act.wait_ge(stored, 16 * NP)
                        nc.scalar.dma_start(at_first[:], att_t[0]).then_inc(ld_at_first, 16)
                        load_weights(nc.scalar.dma_start, 3)
                        nc.scalar.activation(rstd_2[:, 0:1], rstd_2[:, 0:1], ACT.Sqrt)
                        for q in range(WB):
                            cast_weights(act, q)

                    @block.vector
                    def _(dve):
                        dve.sem_inc(t_ready, 2)
                        dve.sem_inc(o_ready, 1)
                        dve.sem_inc(acc_done, NP)
                        dve.wait_ge(masked, 2)
                        for pair in range(B // PAIR):
                            for i in range(PAIR if pair >= 1 else 0):
                                dve.wait_ge(ld_x[i], 16 * pair)
                                for t in range(TB):
                                    n = (PAIR * pair + i) * TB + t
                                    last = nc.vector.tensor_scalar(rows(i, t), rows(i, t), mv_2[:, n, 0:1], rstd_2[:, n:n + 1],
                                                                   ALU.subtract, ALU.mult)
                                last.then_inc(n_xh, 1)
                            for i in range(PAIR if pair >= 1 else 0):
                                for c in range(DC + 1):
                                    n = DC * (PAIR * (pair - 1) + i) + c
                                    if c < DC:
                                        dve.wait_ge(n_hf, n + 1)
                                        nc.vector.tensor_copy(hT[0][:, c, i * S:(i + 1) * S], hf[:, i, c, :]).then_inc(n_hi, 1)
                                    if c >= 1:
                                        dve.wait_ge(n_hi, n)
                                        nc.vector.tensor_tensor(hT[1][:, c - 1, i * S:(i + 1) * S], hf[:, i, c - 1, :],
                                                                hT[0][:, c - 1, i * S:(i + 1) * S].bitcast(F32),
                                                                ALU.subtract).then_inc(n_lo, 1)
                            with dve.Fori(NKV * pair, NKV * (pair + 1)) as g:
                                def lo(name, dst, hi_part, done, scale=1.0):
                                    j = JOB[name]
                                    dve.wait_ge(job_hi, NKQ * g + (KQ_JOBS.index(name) + 1))
                                    nc.vector.scalar_tensor_tensor(dst, ps[:, BANK_J + j % 2, S - dst.shape[-1]:], scale, hi_part.bitcast(F32),
                                                                   ALU.mult, ALU.subtract).then_inc(done, 1)

                                def lo_kq(name, dst, hi_part, scale=1.0):
                                    lo(name, dst, hi_part, kq_ready, scale)

                                def lo_q(u):
                                    lo_kq(f"Q{u}", qT[1][:, u % 2, :], qT[0][:, u % 2, :], QSCALE)

                                def maxima(u):
                                    for n, (i, bank, col) in enumerate(SC):
                                        if n < 3:
                                            dve.wait_ge(s_full, UNITS * TB * g + (TB * u + (1, 2, 4)[n]))
                                            dve.sem_inc(waits_seen, 1)
                                        v = ps[:, BANK_S + bank, col:col + KEYS[i]]
                                        nc.vector.tensor_tensor_reduce(out=v, in0=v, in1=mask[:, TB * P - KEYS[i]:], scale=-1.0,
                                                                       scalar=3e38, op0=ALU.add, op1=ALU.min,
                                                                       accum_out=nmax[:, u % 2, i:i + 1]).then_inc(max_done, 1)

                                def scale_rows(u):
                                    dve.wait_ge(exp_done, UNITS * TB * g + (TB * (u + 1) + TB))
                                    nc.vector.reciprocal(rinv[:, u % 2, :], rsum[:, u % 2, :]).then_inc(rinv_done, 1)
                                    dve.wait_ge(rinv_done, UNITS * g + (u + 1))
                                    for i in range(TB):
                                        v = pe_[:, u % 2, PO[i]:PO[i] + KEYS[i]]
                                        nc.vector.tensor_scalar(v, v, rinv[:, u % 2, i:i + 1], None, ALU.mult).then_inc(p_ready, 1)

                                def turned_lo(name, dst, hi_part, col):
                                    dve.wait_ge(t_hi, turned(g, name))
                                    nc.vector.tensor_tensor(dst, ps[:, BANK_T + TJOB[name] % 2, col:col + dst.shape[-1]],
                                                            hi_part.bitcast(F32), ALU.subtract).then_inc(t_ready, 1)

                                def t_part(u, k):
                                    first, N, _, _ = PVS[k]
                                    turned_lo(f"{u}.{k}", pt[1][:, first:first + N], pt[0][:, first:first + N], P if k == 1 else 0)

                                def v_part(b):
                                    flat = lambda t: t[:, b].rearrange("p t d -> p (t d)")
                                    turned_lo(f"V{b}", flat(V[1]), flat(V[0]), 0)

                                def add_out(t):
                                    j = JOB[f"W{t}"]
                                    dve.wait_ge(job_full, full(g, JOBS[j]))
                                    nc.vector.tensor_tensor(acc[:, t, :], acc[:, t, :], ps[:, BANK_J + j % 2, :], ALU.add) \
                                        .then_inc(acc_done, 1)

                                lo_kq("K0", kT[1][:, 0, :], kT[0][:, 0, :])
                                lo_q(0)
                                v_part(0)
                                lo_kq("K1", kT[1][:, 1, :], kT[0][:, 1, :])
                                maxima(0)
                                scale_rows(0)
                                lo_q(1)
                                for u in range(UNITS):
                                    if u + 1 < UNITS:
                                        maxima(u + 1)
                                    t_part(u, 0)
                                    t_part(u, 1)
                                    if u in STEP_Q:
                                        lo_q(STEP_Q[u])
                                    for t in STEP_W.get(u, ())[0:1]:
                                        add_out(t)
                                    t_part(u, 2)
                                    if u + 1 < UNITS:
                                        scale_rows(u + 1)
                                    for t in STEP_W.get(u, ())[1:2]:
                                        add_out(t)
                                    dve.wait_ge(o_hi, UNITS * g + (u + 1))
                                    nc.vector.tensor_tensor(oT[1][:, u // GQ, u % GQ, :], ps[:, BANK_V, :],
                                                            oT[0][:, u // GQ, u % GQ, :].bitcast(F32), ALU.subtract) \
                                        .then_inc(o_ready, 1)
                                    if u == 0:
                                        v_part(1)
                                for t in range(TB, NP):
                                    add_out(t)



        second.close()

        f = ExitStack()
        with f:
            sb(f, "kept_xt", [P, 2, TB, D], F32)
            sb(f, "kept_xh", [P, TB, D], F32)
            with ExitStack() as early:
                sb(early, "kept_at", [P, TB, D], F32)
                dsc = sb(early, "dsc", [P, D], F32)
            hd = [sb(f, f"hd{i}", [P, FC, S], F32R) for i in (1, 0)][::-1]
            gw = sb(f, "gw", [P, DC, F], F32R)
            uw = sb(f, "uw", [P, DC, F], F32R)
            dw = sb(f, "dw", [P, FC, D], F32R)
            gsc = sb(f, "gsc", [P, FC], F32)
            usc = sb(f, "usc", [P, FC], F32)
            dgb = sb(f, "dgb", [P, B, D], F32)
            at = sb(f, "at", [P, 2, D], F32)
            stats = sb(f, "stats", [P, TB, 6], F32)
            mv = sb(f, "mv", [P, TB, 2], F32)
            std = sb(f, "std", [P, TB], F32)
            xh = xh_m
            hT = [sb(f, f"hT{i}", [P, DC, S], F32R) for i in range(2)]
            sg = sb(f, "sg", [P, 2, S], F32)
            hid = sb(f, "hid", [P, 2, S], F32)
            hf, yt = sg, hid
            s = {n: sem("m_" + n) for n in ("x3", "stat", "stat_seen", "agg", "var", "std", "rstd", "xh", "turned", "hf", "hi",
                                            "lo", "gate", "up", "sg", "hid", "hhi", "hlo", "down", "yt", "y",
                                            "w_turned", "prepped", "gates", "dgb", "ld_dsc", "st")}
            ld_s = sem("ld_s")
            s["ld_x"], s["cast"] = ld_xm, cast_done
            ld_at = [sem(f"ld_at{k}") for k in range(2)]
            BANK_T, BANK_W = 4, 5
            J_STAT, J_ROOT = 6, 12
            NW = 3 * FC
            AHEAD = 2
            with nc.Block() as block:
                @block.sync
                def _(sp):
                    def next_weights(q):
                        sp.wait_ge(s["cast"], q - WB + 1)
                        load_weights(sp.dma_start, q)

                    for q in range(WB, 2 * WB):
                        next_weights(q)
                    sp.dma_start(dsc[:], down_s.rearrange("(o d) -> o d", o=1).to_broadcast([P, D])).then_inc(s["ld_dsc"], 16)
                    with nc.allow_non_contiguous_dma("scales with the hidden width on partitions"):
                        sp.dma_start(gsc[:], gate_s.rearrange("(j p) -> p j", p=P)).then_inc(ld_s, 16)
                        sp.dma_start(usc[:], up_s.rearrange("(j p) -> p j", p=P)).then_inc(ld_s, 16)
                    for q in range(2 * WB, NW // 3):
                        next_weights(q)
                    sp.wait_ge(s["turned"], DC)
                    sp.dma_start(xt[:, 1], mid_t[1]).then_inc(s["ld_x"], 16)
                    for t in range(TB):
                        if t == 2:
                            for q in range(NW // 3, NW // 3 + 2 * WB):
                                next_weights(q)
                        sp.wait_ge(s["x3"], TB + t - 1)
                        sp.dma_start(at[:, t % 2, :], att_t[1][:, t, :]).then_inc(ld_at[t % 2], 16)
                    for q in range(NW // 3 + 2 * WB, NW):
                        next_weights(q)
                    for t in range(TB):
                        sp.wait_ge(s["y"], t + 1)
                        sp.dma_start(out_t[0][:, t, :], xt[:, 0, t, :]).then_inc(s["st"], 16)
                    with sp.Fori(1, B) as n:
                        nxt = (n + 1) % B
                        sp.wait_ge(s["st"], 16 * TB * n)
                        sp.dma_start(xt[:, bass.ds((n + 1) % 2, 1)].rearrange("p k t d -> p (k t) d"),
                                     mid_t[bass.ds(nxt, 1)].rearrange("b p t d -> p (b t) d")).then_inc(s["ld_x"], 16)
                        for t in range(TB):
                            sp.wait_ge(s["x3"], TB * n + (TB + t - 1))
                            sp.dma_start(at[:, t % 2, :], att_t[bass.ds(nxt, 1), :, t, :].rearrange("b p d -> p (b d)")) \
                                .then_inc(ld_at[t % 2], 16)
                        for t in range(TB):
                            sp.wait_ge(s["y"], TB * n + (t + 1))
                            sp.dma_start(out_t[bass.ds(n, 1), :, t, :].rearrange("b p d -> p (b d)"),
                                         xt[:, bass.ds(n % 2, 1), t, :].rearrange("p k d -> p (k d)")).then_inc(s["st"], 16)
                    sp.wait_ge(s["st"], 16 * TB * B)

                @block.gpsimd
                def _(pool):
                    def add_attention(n, slot):
                        for t in range(TB):
                            pool.wait_ge(s["ld_x"], 16 * n + 32)
                            pool.wait_ge(ld_at[t % 2], 32 * n + 16 * (t // 2 + 1))
                            pool.sem_inc(waits_seen, 1)
                            x_ = xt[:, slot, t, :].rearrange("p k d -> p (k d)")
                            nc.gpsimd.tensor_tensor(x_, x_, at[:, t % 2, :], ALU.add).then_inc(s["x3"], 1)

                    add_attention(0, slice(1, 2))
                    with pool.Fori(1, B) as n:
                        add_attention(n, bass.ds((n + 1) % 2, 1))

                @block.scalar
                def _(act):
                    def cast(q):
                        act.wait_ge(s["w_turned"], q - WB + 1)
                        cast_weights(act, q)

                    def root(r):
                        act.wait_ge(s["var"], r + 1)
                        nc.scalar.activation(std[:], mv[:, :, 1], ACT.Sqrt).then_inc(s["std"], 1)

                    def modulated(r, b):
                        for c in range(DC):
                            act.wait_ge(s["turned"], DC * r + (c + 1))
                            act.wait_ge(s["lo"], DC * r + (c + 1))
                            bias = mod[1][:, DC * MOD_SB + c, bass.ds(b, 1)]
                            scale = mod[1][:, DC * MOD_CB + c, bass.ds(b, 1)]
                            for dst, done in ((hf[:, c % 2, :], "hf"), (hT[0][:, c, :], "hi")):
                                nc.scalar.activation(dst, ps[:, BANK_T + c, :], ACT.Identity, bias=bias, scale=scale) \
                                    .then_inc(s[done], 1)

                    def batch(n, first):
                        for j in range(FC):
                            act.wait_ge(s["gate"], FC * n + (j + 1))
                            act.wait_ge(s["hid"], FC * n + (j + 1))
                            nc.scalar.activation(sg[:, j % 2, :], ps[:, 2 * (j % 2), :], ACT.Silu,
                                                 scale=gsc[:, j:j + 1]).then_inc(s["sg"], 1)
                            if first and j + AHEAD < FC:
                                for q in range(3 * (j + AHEAD), 3 * (j + AHEAD) + 3):
                                    cast(q)
                            act.wait_ge(s["hid"], FC * n + (j + 3))
                            nc.scalar.activation(hd[0][:, j, :], hid[:, j % 2, :], ACT.Copy).then_inc(s["hhi"], 1)
                            if j == J_ROOT:
                                root(n + 1)
                        modulated(n + 1, (n + 1) % B)

                    act.sem_inc(s["hi"], DC)
                    root(0)
                    for q in range(WB, 3 * AHEAD):
                        cast(q)
                    modulated(0, 0)
                    act.wait_ge(ld_s, 32)
                    batch(0, True)
                    with act.Fori(1, B) as n:
                        batch(n, False)

                @block.vector
                def _(dve):
                    def statistics(r, tile, t):
                        dve.wait_ge(s["x3"], TB * r + (t + 1))
                        nc.vector.bn_stats(stats[:, t, :], tile).then_inc(s["stat"], 1)

                    def variances(r):
                        dve.wait_ge(s["stat"], TB * r + TB)
                        dve.sem_inc(s["stat_seen"], 1)
                        for t in range(TB):
                            last = nc.vector.bn_aggr(mv[:, t, :], stats[:, t, :])
                        last.then_inc(s["agg"], 1)
                        dve.wait_ge(s["agg"], r + 1)
                        nc.vector.tensor_scalar(mv[:, :, 1], mv[:, :, 1], EPS, None, ALU.add).then_inc(s["var"], 1)

                    def normal(r, tiles, dst):
                        dve.wait_ge(s["std"], r + 1)
                        nc.vector.reciprocal(std[:], std[:]).then_inc(s["rstd"], 1)
                        dve.wait_ge(s["rstd"], r + 1)
                        for t in range(TB):
                            nc.vector.tensor_scalar(dst[:, t, :], tiles(t), mv[:, t, 0:1], std[:, t:t + 1],
                                                    ALU.subtract, ALU.mult).then_inc(s["xh"], 1)

                    def lows(r):
                        for c in range(DC):
                            dve.wait_ge(s["hi"], DC * r + (DC + c + 1))
                            nc.vector.tensor_tensor(hT[1][:, c, :], hf[:, c % 2, :], hT[0][:, c, :].bitcast(F32),
                                                    ALU.subtract).then_inc(s["lo"], 1)

                    def prepare(q):
                        j = q // 3
                        dve.wait_ge(s["w_turned"], q + 1)
                        bank = ps[:, BANK_W + q % 3, 0:D // 2].bitcast(BF16)
                        if q % 3 < 2:
                            nc.vector.tensor_copy((gw, uw)[q % 3][:, :, j * P:(j + 1) * P],
                                                  bank.rearrange("p (c o) -> p c o", c=DC)).then_inc(s["prepped"], 1)
                        else:
                            nc.vector.tensor_copy(dw[:, j, :], bank).then_inc(s["prepped"], 1)

                    def batch(n, first, here, other):
                        for j in range(FC):
                            q = FC * n + j
                            dve.wait_ge(s["up"], q + 1)
                            dve.wait_ge(s["sg"], q + 1)
                            dve.wait_ge(s["hlo"], q + 1)
                            nc.vector.scalar_tensor_tensor(hid[:, j % 2, :], ps[:, 2 * (j % 2) + 1, :], usc[:, j:j + 1],
                                                           sg[:, j % 2, :], ALU.mult, ALU.mult).then_inc(s["hid"], 1)
                            if first and j + AHEAD < FC:
                                for w in range(3 * (j + AHEAD), 3 * (j + AHEAD) + 3):
                                    prepare(w)
                            dve.wait_ge(s["hhi"], q + 1)
                            nc.vector.tensor_tensor(hd[1][:, j, :], hid[:, j % 2, :], hd[0][:, j, :].bitcast(F32),
                                                    ALU.subtract).then_inc(s["hlo"], 1)
                            if J_STAT <= j < J_STAT + TB:
                                statistics(n + 1, other(j - J_STAT), j - J_STAT)
                            if j == J_STAT + TB:
                                variances(n + 1)
                        normal(n + 1, other, xh)
                        for t in range(TB):
                            q = TB * n + t
                            dve.wait_ge(s["down"], q + 1)
                            gate = dgb[:, bass.ds(n, 1), :].rearrange("p b d -> p (b d)")
                            nc.vector.tensor_tensor(yt[:, t % 2, :], gate, ps[:, t, :], ALU.mult).then_inc(s["yt"], 1)
                            dve.wait_ge(s["yt"], q + 1)
                            nc.vector.tensor_tensor(here(t), here(t), yt[:, t % 2, :], ALU.add).then_inc(s["y"], 1)
                            if t == 0:
                                lows(n + 1)

                    dve.sem_inc(s["hid"], 2)
                    dve.sem_inc(s["lo"], 2)
                    dve.sem_inc(s["hlo"], 1)
                    dve.wait_ge(s["ld_x"], 16)
                    dve.wait_ge(ld_at_first, 16)
                    for t in range(TB + 1):
                        if t < TB:
                            nc.vector.tensor_tensor(xt[:, 0, t, :], xt[:, 0, t, :], at_first[:, t, :], ALU.add).then_inc(s["x3"], 1)
                        if t >= 1:
                            statistics(0, xt[:, 0, t - 1, :], t - 1)
                    variances(0)
                    dve.wait_ge(stored, 16 * NT)
                    prepare(0)
                    normal(0, lambda t: xt[:, 0, t, :], xt[:, 1])
                    for q in range(1, 3):
                        prepare(q)
                    lows(0)
                    for q in range(3, 3 * AHEAD):
                        prepare(q)
                    dve.wait_ge(s["ld_dsc"], 16)
                    for b in range(B):
                        dve.wait_ge(s["gates"], b + 1)
                        nc.vector.tensor_tensor(dgb[:, b, :], dsc[:], ps[:, b, :], ALU.mult).then_inc(s["dgb"], 1)
                    dve.wait_ge(ld_s, 32)
                    batch(0, True, lambda t: xt[:, 0, t, :], lambda t: xt[:, 1, t, :])
                    with dve.Fori(1, B) as n:
                        def tile(k):
                            return lambda t: xt[:, bass.ds((n + k) % 2, 1), t, :].rearrange("p k d -> p (k d)")
                        batch(n, False, tile(0), tile(1))

                @block.tensor
                def _(pe):
                    def turn(r, src):
                        pe.wait_ge(s["xh"], TB * r + TB)
                        for c in range(DC):
                            pe.wait_ge(s["hi"], DC * r + (c + 1))
                            turn_chunk(BANK_T + c, src, c).then_inc(s["turned"], 1)

                    def turn_weights(q):
                        pe.wait_ge(s["cast"], q + 1)
                        if q >= 3:
                            pe.wait_ge(s["prepped"], q - 2)
                        bank = ps[:, BANK_W + q % 3, 0:D // 2].bitcast(BF16)
                        for c in range(DC):
                            last = nc.tensor.transpose(bank[:, c * P:(c + 1) * P], wb[:, q % WB, c * P:(c + 1) * P], ident_b[:])
                        last.then_inc(s["w_turned"], 1)

                    def down(n, t):
                        pe.wait_ge(s["hlo"], FC * n + FC)
                        for j in range(FC):
                            if j == FC - 1:
                                pe.wait_ge(s["hlo"], FC * n + (FC + 1))
                            for h in range(2):
                                last = nc.tensor.matmul(ps[:, t, :], hd[h][:, j, t * P:(t + 1) * P], dw[:, j, :],
                                                        start=(j == 0 and h == 0), stop=(j == FC - 1 and h == 1))
                        last.then_inc(s["down"], 1)

                    def batch(n, first):
                        for j in range(FC):
                            if j == 0:
                                pe.wait_ge(s["lo"], DC * n + (DC + 2))
                            if first:
                                pe.wait_ge(s["prepped"], 3 * j + 3)
                                if j < 2:
                                    pe.wait_ge(s["dgb"], 2 * j + 2)
                            elif j < 2:
                                pe.wait_ge(s["y"], TB * n + (2 * j + 2 - TB))
                            pe.wait_ge(s["hid"], FC * n + (j + 1))
                            for w, bank, done in ((gw, 2 * (j % 2), "gate"), (uw, 2 * (j % 2) + 1, "up")):
                                for c in range(DC):
                                    for h in range(2):
                                        last = nc.tensor.matmul(ps[:, bank, :], w[:, c, j * P:(j + 1) * P], hT[h][:, c, :],
                                                                start=(c == 0 and h == 0), stop=(c == DC - 1 and h == 1))
                                last.then_inc(s[done], 1)
                            if first and j + AHEAD < FC:
                                for q in range(3 * (j + AHEAD), 3 * (j + AHEAD) + 3):
                                    turn_weights(q)
                        down(n, 0)
                        if first:
                            pe.wait_ge(s["prepped"], NW)
                        turn(n + 1, xh)
                        for t in range(1, TB):
                            down(n, t)

                    for b in range(B):
                        gate_rows(pe, b, 1, MOD_GB, b).then_inc(s["gates"], 1)
                    for q in range(3):
                        turn_weights(q)
                    pe.wait_ge(s["prepped"], 3)
                    turn(0, xt[:, 1])
                    pe.wait_ge(s["hi"], DC + DC)
                    for q in range(3, 3 * AHEAD):
                        turn_weights(q)
                    batch(0, True)
                    with pe.Fori(1, B) as n:
                        batch(n, False)


_INS = ['L0_attn_x', 'L0_attn_Wq', 'L0_attn_bq', 'L0_attn_Wk', 'L0_attn_bk', 'L0_attn_Wv', 'L0_attn_bv', 'L0_ffn_weight',
        'L0_ffn_bias', 'L0_ffn_centroids', 'L0_ffn_assignments', 'L0_c', 'L0_wmod', 'L1_attn_w_q', 'L1_attn_w_k',
        'L1_attn_w_v', 'L1_attn_w_o', 'L1_ffn_gate_wq', 'L1_ffn_gate_scale', 'L1_ffn_up_wq', 'L1_ffn_up_scale',
        'L1_ffn_down_wq', 'L1_ffn_down_scale', 'L1_c', 'L1_wmod']


def kernel(**inputs):
    import numpy as _np
    import concourse.bacc as _bacc
    from concourse import mybir as _mybir
    from concourse.bass_utils import run_bass_kernel_spmd as _run

    nc = _bacc.Bacc("TRN2", target_bir_lowering=False, num_devices=1)
    arrays, args = {}, []
    for name in _INS:
        a = _np.ascontiguousarray(inputs[name])
        arrays[f"in_{name}_dram"] = a
        args.append(nc.dram_tensor(f"in_{name}_dram", a.shape, _mybir.dt.from_np(a.dtype), kind="ExternalInput").ap())
    x = arrays["in_L0_attn_x_dram"]
    args.append(nc.dram_tensor("out_0_dram", x.shape, _mybir.dt.from_np(x.dtype), kind="ExternalOutput").ap())
    adaln_two_blocks(nc, *args)
    r = _run(nc, [arrays], core_ids=[0])
    return r.results[0]["out_0_dram"]
```
